# Optimizing a Trainium2 kernel written in Bass

```python
import numpy as np
import jax
import jax.numpy as jnp

def _softmax(x, axis=-1):
    return jax.nn.softmax(x, axis=axis)

def _gelu(x):
    return jax.nn.gelu(x, approximate=True)

def _silu(x):
    return jax.nn.silu(x)

def _sigmoid(x):
    return jax.nn.sigmoid(x)

def _layernorm(x, axis=-1, eps=1e-05):
    m = jnp.mean(x, axis=axis, keepdims=True)
    v = jnp.var(x, axis=axis, keepdims=True)
    return (x - m) / jnp.sqrt(v + eps)

def _scatter_add(tgt, idx, src, axis=0):
    return tgt.at[idx].add(src)

def _segment_sum(src, seg, n):
    return jax.ops.segment_sum(src, seg, n)
kernel_name = 'mk_adj_ffn_d2_adj_r2_f294c9'

def setup_inputs(seed: int=0):
    np.random.seed(seed)
    _w = jnp.asarray

    def _rec_inputs():
        import jax
        import jax.numpy as jnp
        _gk = jax.random.key(seed)
        x = -0.0006008 + 1.001 * jax.random.normal(jax.random.fold_in(_gk, 1), (4096, 128), jnp.float32)
        _a = jax.random.bernoulli(jax.random.fold_in(_gk, 2), 0.00390625, (4096, 4096))
        _a = jnp.logical_or(_a, jnp.swapaxes(_a, -1, -2))
        _a = jnp.logical_or(_a, jnp.eye(4096, dtype=bool))
        adj = _a.astype(jnp.int32)
        return (x, adj)
    x, adj = _rec_inputs()

    def _L0_gnn_setup():
        import jax, jax.numpy as jnp
        import numpy as np
        N, D_IN, D_OUT = (5000, 128, 128)
        key = jax.random.key(seed)
        k1, k2, k3, k4 = jax.random.split(key, 4)

        def xavier(k, shape, gain=1.414):
            fan_in, fan_out = (shape[0], shape[1])
            bound = gain * np.sqrt(6.0 / (fan_in + fan_out))
            return jax.random.uniform(k, shape, jnp.float32, -bound, bound)
        return {'input': jax.random.normal(k1, (N, D_IN), jnp.float32), 'adj': jax.random.randint(k2, (N, N), 0, 2, jnp.int32), 'M': N, 'W': xavier(k3, (D_IN, D_OUT)), 'b': jnp.zeros((D_OUT,), jnp.float32), 'a': xavier(k4, (D_OUT, 1))}
    _L0_gnn_all = _L0_gnn_setup()
    _L0_gnn_in = {k: v for k, v in _L0_gnn_all.items() if k in ('W', 'b', 'a')}
    del _L0_gnn_all

    def _L0_ffn_setup():
        import jax, jax.numpy as jnp
        import numpy as np
        D_MODEL = 128
        N_EXPERTS = 16
        HIDDEN = 256
        SCALE = 0.02
        key = jax.random.key(seed)
        ks = jax.random.split(key, 5)
        x = jax.random.normal(ks[0], (4, 4096, D_MODEL), dtype=jnp.float32)
        gate_w = jax.random.normal(ks[1], (D_MODEL, N_EXPERTS), dtype=jnp.float32) * SCALE
        gate_b = jnp.zeros((N_EXPERTS,), dtype=jnp.float32)
        w1 = jax.random.normal(ks[2], (N_EXPERTS, D_MODEL, HIDDEN), dtype=jnp.float32) * SCALE
        w2 = jax.random.normal(ks[3], (N_EXPERTS, D_MODEL, HIDDEN), dtype=jnp.float32) * SCALE
        w3 = jax.random.normal(ks[4], (N_EXPERTS, HIDDEN, D_MODEL), dtype=jnp.float32) * SCALE
        return {'x': x, 'gate_w': gate_w, 'gate_b': gate_b, 'w1': w1, 'w2': w2, 'w3': w3}
    _L0_ffn_all = _L0_ffn_setup()
    _L0_ffn_in = {k: v for k, v in _L0_ffn_all.items() if k in ('gate_w', 'gate_b', 'w1', 'w2', 'w3')}
    del _L0_ffn_all

    def _L1_gnn_setup():
        import jax, jax.numpy as jnp
        import numpy as np
        N = 8192
        D = 128
        key = jax.random.key(seed)
        k1, k2, k3, k4 = jax.random.split(key, 4)
        x = jax.random.normal(k1, (N, D), dtype=jnp.float32)
        adj = jax.random.randint(k2, (N, N), 0, 2, dtype=jnp.int32)
        W = jax.random.normal(k3, (D, D), dtype=jnp.float32) * 0.05
        b = jax.random.normal(k4, (D,), dtype=jnp.float32) * 0.05
        return {'x': x, 'adj': adj, 'W': W, 'b': b}
    _L1_gnn_all = _L1_gnn_setup()
    _L1_gnn_in = {k: v for k, v in _L1_gnn_all.items() if k in ('W', 'b')}
    del _L1_gnn_all

    def _L1_ffn_setup():
        import jax, jax.numpy as jnp
        import numpy as np
        B, K, D = (256, 16, 128)
        E = 32
        H = int(D * 0.25)
        key = jax.random.key(seed)
        ks = jax.random.split(key, 7)
        d_rs = D ** (-0.5)
        h_rs = H ** (-0.5)
        x = jax.random.normal(ks[0], (B, K, D), dtype=jnp.float32)
        router_w = jax.random.uniform(ks[1], (E, D), jnp.float32, -d_rs, d_rs)
        router_b = jax.random.uniform(ks[2], (E,), jnp.float32, -d_rs, d_rs)
        W1 = jax.random.uniform(ks[3], (E, D, H), jnp.float32, -h_rs, h_rs)
        b1 = jax.random.uniform(ks[4], (E, H), jnp.float32, -h_rs, h_rs)
        W2 = jax.random.uniform(ks[5], (E, H, D), jnp.float32, -d_rs, d_rs)
        b2 = jax.random.uniform(ks[6], (E, D), jnp.float32, -d_rs, d_rs)
        return {'x': x, 'router_w': router_w, 'router_b': router_b, 'W1': W1, 'b1': b1, 'W2': W2, 'b2': b2}
    _L1_ffn_all = _L1_ffn_setup()
    _L1_ffn_in = {k: v for k, v in _L1_ffn_all.items() if k in ('router_w', 'router_b', 'W1', 'b1', 'W2', 'b2')}
    del _L1_ffn_all
    return {'x': x, 'adj': adj, 'L0_gnn_W': _L0_gnn_in['W'], 'L0_gnn_b': _L0_gnn_in['b'], 'L0_gnn_a': _L0_gnn_in['a'], 'L0_ffn_gate_w': _L0_ffn_in['gate_w'], 'L0_ffn_gate_b': _L0_ffn_in['gate_b'], 'L0_ffn_w1': _L0_ffn_in['w1'], 'L0_ffn_w2': _L0_ffn_in['w2'], 'L0_ffn_w3': _L0_ffn_in['w3'], 'L1_gnn_W': _L1_gnn_in['W'], 'L1_gnn_b': _L1_gnn_in['b'], 'L1_ffn_router_w': _L1_ffn_in['router_w'], 'L1_ffn_router_b': _L1_ffn_in['router_b'], 'L1_ffn_W1': _L1_ffn_in['W1'], 'L1_ffn_b1': _L1_ffn_in['b1'], 'L1_ffn_W2': _L1_ffn_in['W2'], 'L1_ffn_b2': _L1_ffn_in['b2']}

def reference(x, adj, L0_gnn_W, L0_gnn_b, L0_gnn_a, L0_ffn_gate_w, L0_ffn_gate_b, L0_ffn_w1, L0_ffn_w2, L0_ffn_w3, L1_gnn_W, L1_gnn_b, L1_ffn_router_w, L1_ffn_router_b, L1_ffn_W1, L1_ffn_b1, L1_ffn_W2, L1_ffn_b2):
    import jax
    import jax.numpy as jnp

    def _L0_gnn_ref(input, adj, M, W, b, a):
        import jax, jax.numpy as jnp
        import numpy as np
        N, D_IN, D_OUT = (5000, 128, 128)
        h = jnp.tanh(input @ W + b)
        inp = input @ W
        e = (h @ a)[:, 0]
        valid = jnp.sum(h, axis=1) != 0
        mask = (adj[:M] > 0) & valid[None, :]
        neg = jnp.asarray(-1e+30, h.dtype)
        scores = jnp.where(mask, e[None, :], neg)
        m = jnp.max(scores, axis=1, keepdims=True)
        w = jnp.where(mask, jnp.exp(scores - m), 0.0)
        denom = jnp.sum(w, axis=1, keepdims=True)
        att = w / jnp.maximum(denom, 1e-30)
        return att @ inp

    def _L0_ffn_ref(x, gate_w, gate_b, w1, w2, w3):
        import jax, jax.numpy as jnp
        import numpy as np
        D_MODEL = 128
        N_EXPERTS = 16
        HIDDEN = 256
        SCALE = 0.02
        n_experts = w1.shape[0]
        logits = jnp.einsum('bsd,de->bse', x, gate_w) + gate_b
        probs = jax.nn.softmax(logits, axis=-1)
        top_probs, top_idx = jax.lax.top_k(probs, 2)
        top_probs = top_probs / jnp.sum(top_probs, axis=-1, keepdims=True)
        dispatch = jnp.sum(jax.nn.one_hot(top_idx, n_experts, dtype=x.dtype) * top_probs[..., None], axis=-2)
        h1 = jnp.einsum('bsd,edh->bseh', x, w1)
        h2 = jnp.einsum('bsd,edh->bseh', x, w2)
        hidden = jax.nn.silu(h1) * h2
        expert_out = jnp.einsum('bseh,eho->bseo', hidden, w3)
        return jnp.einsum('bseo,bse->bso', expert_out, dispatch)

    def _L1_gnn_ref(x, adj, W, b):
        import jax, jax.numpy as jnp
        import numpy as np
        N = 8192
        D = 128
        a = (adj == 1).astype(x.dtype)
        deg = jnp.sum(a, axis=1, keepdims=True)
        agg = jnp.einsum('ij,jf->if', a, x) / deg
        return agg @ W.T + b

    def _L1_ffn_ref(x, router_w, router_b, W1, b1, W2, b2):
        import jax, jax.numpy as jnp
        import numpy as np
        B, K, D = (256, 16, 128)
        E = 32
        H = int(D * 0.25)
        xf = x.reshape(-1, D)
        logits = xf @ router_w.T + router_b
        idx = jnp.argmax(logits, axis=-1)
        w1t = jnp.take(W1, idx, axis=0)
        h = jnp.einsum('nd,ndh->nh', xf, w1t) + jnp.take(b1, idx, axis=0)
        h = jax.nn.relu(h)
        w2t = jnp.take(W2, idx, axis=0)
        out = jnp.einsum('nh,nhd->nd', h, w2t) + jnp.take(b2, idx, axis=0)
        out = jax.nn.relu(out)
        return out.reshape(x.shape)
    x = x + _L0_gnn_ref(_layernorm(x, axis=-1), adj, 4096, L0_gnn_W, L0_gnn_b, L0_gnn_a)
    x = x + _L0_ffn_ref(_layernorm(x, axis=-1)[None], L0_ffn_gate_w, L0_ffn_gate_b, L0_ffn_w1, L0_ffn_w2, L0_ffn_w3)[0]
    x = x + _L1_gnn_ref(_layernorm(x, axis=-1), adj, L1_gnn_W, L1_gnn_b)
    x = x + _L1_ffn_ref(_layernorm(x, axis=-1)[None], L1_ffn_router_w, L1_ffn_router_b, L1_ffn_W1, L1_ffn_b1, L1_ffn_W2, L1_ffn_b2)[0]
    return x

_drawn_inputs = setup_inputs


def setup_inputs(seed=0):
    import zlib

    import numpy as np

    out = dict(_drawn_inputs(seed))
    spreads = {'L0_gnn_b': (0.0, 0.1), 'L0_ffn_gate_b': (0.0, 0.565)}
    factors = {'L0_ffn_gate_w': 5.172,
     'L0_ffn_w1': 4.638,
     'L0_ffn_w2': 4.415,
     'L0_ffn_w3': 4.863,
     'L1_ffn_b1': 4.588}
    for name, (base, spread) in spreads.items():
        noise = np.random.default_rng([zlib.crc32(name.encode()), seed]).standard_normal(out[name].shape)
        drawn = base * np.exp(spread * noise) if base else spread * noise
        out[name] = jnp.asarray(drawn.astype(out[name].dtype))
    for name, factor in factors.items():
        out[name] = (out[name] * factor).astype(out[name].dtype)
    return out
```

```python
from contextlib import ExitStack

import concourse.bass as bass
from concourse import mybir

ALU = mybir.AluOpType
ACT = mybir.ActivationFunctionType
AX = mybir.AxisListType
F32 = mybir.dt.float32
BF16 = mybir.dt.bfloat16
F16 = mybir.dt.float16
F8 = mybir.dt.float8e4
I32 = mybir.dt.int32
U32 = mybir.dt.uint32
U8 = mybir.dt.uint8
RMAX = bass.bass_isa.ReduceOp.max
ds = bass.ds

P = 128
F8_ONE = 56
EPS = 1e-5
SHIFT = 64.0
LOW_SCALE = 4096.0


class Steps:

    def __init__(self, eng, sem, base=0):
        self.eng, self.sem, self.base, self.n = eng, sem, base, 0

    def then(self, ins):
        ins.then_inc(self.sem, 1)
        self.n += 1

    def wait(self):
        self.eng.wait_ge(self.sem, self.base + self.n)


def over(ap, shape, axis):
    return ap.unsqueeze(axis).to_broadcast(shape)


def build(nc, x, adj_t, g0_w, g0_b, g0_a, gate_w, gate_b, w1, w2, w3, g1_wt, g1_b,
          router_wt, router_b, f_w1, f_b1, f_w2, f_b2, out):
    N, D = x.shape
    NB = N // P
    E0, _, H0 = w1.shape
    E1, _, H1 = f_w1.shape
    HC0 = H0 // P
    TOP = 2
    TILES = N * TOP // P + E0
    ROWS = TILES * P
    EH1 = E1 * H1
    KC1 = EH1 // P
    V3 = 3 * (D + 1)
    V2 = 2 * D + 1
    PART = D + 1

    sorted_x = nc.dram_tensor("sorted_x", (ROWS, D), F32).ap()
    sorted_y = nc.dram_tensor("sorted_y", (ROWS, D), F32).ap()

    with ExitStack() as whole:
        def sb(name, shape, dt, ctx=whole):
            return ctx.enter_context(nc.sbuf_tensor(name, shape, dt))

        def ps(name, shape, dt, ctx=whole):
            return ctx.enter_context(nc.psum_tensor(name, shape, dt))

        def sem(name):
            return whole.enter_context(nc.semaphore(name))

        equal_one = sb("equal_one", [P, NB, N], U8)
        xs = sb("xs", [P, NB, D], F32)
        ident = sb("ident", [P, P], F32)
        ident16 = sb("ident16", [P, P], BF16)
        before = sb("before", [P, P], BF16)
        ones16 = sb("ones16", [P, P], BF16)
        stats = sb("stats", [P, NB, 6], F32)
        mean = sb("mean", [P, NB], F32)
        rstd = sb("rstd", [P, NB], F32)
        tmp = [sb(f"tmp{i}", [P, NB], F32) for i in range(4)]
        pos = sb("pos", [P, TOP, NB], U32)
        gates = sb("gates", [P, TOP, NB], F32)
        tile_w12 = sb("tile_w12", [1, TILES], I32)
        tile_w3 = sb("tile_w3", [1, TILES], I32)

        def inverse_root(dve, v, r, var, root, t):
            v.then(dve.reciprocal(t, root))
            v.wait()
            v.then(dve.tensor_tensor(t, t, var, ALU.mult))
            v.wait()
            v.then(dve.tensor_tensor(t, t, root, ALU.add))
            v.wait()
            v.then(dve.reciprocal(r, t))
            v.wait()
            v.then(dve.tensor_scalar(r, r, 2.0, None, ALU.mult))

        def row_norms(dve, v, var_ready, root_ready, arrived=None):
            Q = NB // 4
            for q in range(4):
                if arrived:
                    dve.wait_ge(arrived[q], 16)
                with dve.Fori(0, Q) as c:
                    dve.bn_stats(stats[:, ds(c + q * Q, 1), :], xs[:, ds(c + q * Q, 1), :]).then_inc(v.sem, 1)
            v.n += NB
            v.wait()
            v.then(dve.tensor_tensor(mean[:, :], stats[:, :, 1], stats[:, :, 4], ALU.add))
            v.then(dve.tensor_tensor(tmp[2][:, :], stats[:, :, 1], stats[:, :, 4], ALU.subtract))
            v.then(dve.tensor_tensor(tmp[3][:, :], stats[:, :, 2], stats[:, :, 5], ALU.add))
            v.wait()
            v.then(dve.tensor_scalar(mean[:, :], mean[:, :], 0.5, None, ALU.mult))
            v.then(dve.tensor_tensor(tmp[2][:, :], tmp[2][:, :], tmp[2][:, :], ALU.mult))
            v.wait()
            v.then(dve.scalar_tensor_tensor(out=tmp[3][:, :], in0=tmp[2][:, :], scalar=D / 4.0, in1=tmp[3][:, :],
                                            op0=ALU.mult, op1=ALU.add))
            v.wait()
            dve.tensor_scalar(tmp[0][:, :], tmp[3][:, :], 1.0 / D, EPS, ALU.mult, ALU.add).then_inc(var_ready, 1)
            dve.wait_ge(root_ready, 1)
            inverse_root(dve, v, rstd[:, :], tmp[0][:, :], tmp[1][:, :], tmp[2][:, :])
            v.wait()

        attend_ctx = ExitStack()
        parts = sb("parts", [P, NB, V3], BF16, attend_ctx)
        with ExitStack() as ctx:
            G = 4
            w_sb = sb("w_sb", [P, D], F32, ctx)
            b_bc = sb("b_bc", [P, D], F32, ctx)
            a_bc = sb("a_bc", [P, D], F32, ctx)
            zeros = sb("zeros", [P, D], F32, ctx)
            xn = sb("xn", [P, 2, G, D], F32, ctx)
            xnt = sb("xnt", [P, 2, G * P], F32, ctx)
            h = sb("h", [P, 2, G, D], F32, ctx)
            ha = sb("ha", [P, G, D], F32, ctx)
            values = sb("values", [P, NB, PART], F32, ctx)
            score = sb("score", [P, NB], F32, ctx)
            hsum = sb("hsum", [P, NB], F32, ctx)
            top = sb("top", [P, 2], F32, ctx)
            ps_t = ps("ps_t", [P, 2, G * P], F32, ctx)
            ps_v = ps("ps_v", [P, 2, G * D], F32, ctx)

            x_in = [sem(f"x_in{i}") for i in range(4)]
            w_in, zeroed, cleared = sem("w_in"), sem("zeroed"), sem("cleared")
            ids_ready, ids_zero = sem("ids_ready"), sem("ids_zero")
            v_a, var_ready, root_ready = sem("v_a"), sem("var_ready"), sem("root_ready")
            xn_ready, xt_ready, xt_copied = sem("xn_ready"), sem("xt_ready"), sem("xt_copied")
            val_ready, val_copied, hb_ready, h_ready = sem("val_ready"), sem("val_copied"), sem("hb_ready"), sem("h_ready")
            h_free = sem("h_free")
            local_top, all_top, weight_ready, high_ready, mid_ready = sem("local_top"), sem("all_top"), sem("weight_ready"), sem("high_ready"), sem("mid_ready")
            bias_ready = sem("bias_ready")

            with nc.Block() as block:
                @block.sync
                def _(sp):
                    q = NB // 4
                    for i in range(4):
                        sp.dma_start(xs[:, i * q:(i + 1) * q, :],
                                     x[i * q * P:(i + 1) * q * P, :].rearrange("(c p) d -> p c d", p=P)).then_inc(x_in[i], 16)

                @block.gpsimd
                def _(pool):
                    pool.memset(ident[:, :], 0.0).then_inc(ids_zero, 1)
                    pool.memset(before[:, :], 1.0).then_inc(ids_zero, 1)
                    pool.memset(ones16[:, :], 1.0).then_inc(ids_zero, 1)
                    pool.wait_ge(ids_zero, 3)
                    pool.affine_select(out=ident[:, :], in_=ident[:, :], compare_op=ALU.not_equal, fill=1.0,
                                       base=0, pattern=[[-1, P]], channel_multiplier=1).then_inc(ids_ready, 1)
                    pool.affine_select(out=before[:, :], in_=before[:, :], compare_op=ALU.is_gt, fill=0.0,
                                       base=0, pattern=[[1, P]], channel_multiplier=-1).then_inc(ids_ready, 1)
                    pool.wait_ge(ids_ready, 2)
                    pool.tensor_copy(ident16[:, :], ident[:, :]).then_inc(ids_ready, 1)
                    pool.wait_ge(local_top, 1)
                    pool.partition_all_reduce(top[:, 1:2], top[:, 0:1], P, RMAX).then_inc(all_top, 1)

                @block.scalar
                def _(act):
                    act.dma_start(w_sb[:, :], g0_w).then_inc(w_in, 16)
                    act.dma_start(b_bc[:, :], g0_b.partition_broadcast(P)).then_inc(w_in, 16)
                    act.dma_start(a_bc[:, :], g0_a.rearrange("d a -> (a d)").partition_broadcast(P)).then_inc(w_in, 16)
                    act.wait_ge(zeroed, 1)
                    act.dma_start(sorted_x.rearrange("(t p) d -> p t d", p=P),
                                  over(zeros[:, :], [P, TILES, D], 1)).then_inc(cleared, 16)
                    act.wait_ge(var_ready, 1)
                    act.activation(tmp[1][:, :], tmp[0][:, :], ACT.Sqrt).then_inc(root_ready, 1)
                    with act.Fori(0, NB // G // 2) as i:
                        for k in range(2):
                            g = i * 2 + k
                            act.wait_ge(xt_ready, g + 1)
                            act.activation(xnt[:, k, :], ps_t[:, k, :], ACT.Copy).then_inc(xt_copied, 1)
                            act.wait_ge(val_ready, g + 1)
                            act.activation(values[:, ds(g * G, G), 0:D],
                                           ps_v[:, k, :].rearrange("p (c d) -> p c d", c=G), ACT.Copy).then_inc(val_copied, 1)
                            act.wait_ge(hb_ready, g + 1)
                            act.activation(h[:, k, :, :], h[:, k, :, :], ACT.Tanh).then_inc(h_ready, 1)
                    act.wait_ge(bias_ready, 1)
                    act.activation(values[:, :, D], score[:, :], ACT.Exp, bias=top[:, 0:1]).then_inc(weight_ready, 1)
                    act.wait_ge(high_ready, 1)
                    act.activation(parts[:, :, 0:PART], values[:, :, :], ACT.Copy).then_inc(high_ready, 1)
                    act.wait_ge(mid_ready, 1)
                    act.activation(parts[:, :, PART:2 * PART], values[:, :, :], ACT.Copy).then_inc(mid_ready, 1)
                    act.wait_ge(cleared, 16)

                @block.tensor
                def _(pe):
                    pe.wait_ge(w_in, 48)
                    pe.wait_ge(ids_ready, 3)
                    with pe.Fori(0, NB // G // 2) as i:
                        for k in range(2):
                            g = i * 2 + k
                            pe.wait_ge(xn_ready, g + 1)
                            for c in range(G):
                                t = pe.transpose(ps_t[:, k, c * P:(c + 1) * P], xn[:, k, c, :], ident[:, :])
                            t.then_inc(xt_ready, 1)
                            pe.wait_ge(xt_copied, g + 1)
                            for c in range(G):
                                m = pe.matmul(ps_v[:, k, c * D:(c + 1) * D], xnt[:, k, c * P:(c + 1) * P], w_sb[:, :],
                                              start=True, stop=True)
                            m.then_inc(val_ready, 1)

                @block.vector
                def _(dve):
                    v = Steps(dve, v_a)
                    dve.memset(zeros[:, :], 0.0).then_inc(zeroed, 1)
                    row_norms(dve, v, var_ready, root_ready, x_in)
                    base = v.n

                    dve.wait_ge(w_in, 48)
                    STEPS = 1
                    with dve.Fori(0, NB // G // 2) as i:
                        for k in range(2):
                            g = i * 2 + k
                            for c in range(G):
                                n = dve.tensor_scalar(xn[:, k, c, :], xs[:, ds(g * G + c, 1), :].rearrange("p a d -> p (a d)"),
                                                      mean[:, ds(g * G + c, 1)], rstd[:, ds(g * G + c, 1)],
                                                      ALU.subtract, ALU.mult)
                            n.then_inc(xn_ready, 1)
                            dve.wait_ge(val_copied, g + 1)
                            dve.tensor_tensor(h[:, k, :, :], values[:, ds(g * G, G), 0:D],
                                              over(b_bc[:, :], [P, G, D], 1), ALU.add).then_inc(hb_ready, 1)
                            dve.wait_ge(h_ready, g + 1)
                            dve.tensor_tensor(ha[:, :, :], h[:, k, :, :], over(a_bc[:, :], [P, G, D], 1), ALU.mult)\
                               .then_inc(v_a, 1)
                            dve.tensor_reduce(hsum[:, ds(g * G, G)], h[:, k, :, :], AX.X, ALU.add)
                            dve.wait_ge(v_a, g * STEPS + (base + 1))
                            dve.tensor_reduce(score[:, ds(g * G, G)], ha[:, :, :], AX.X, ALU.add).then_inc(h_free, 1)
                    v.n = base + NB // G
                    dve.wait_ge(h_free, NB // G)
                    dve.tensor_reduce(top[:, 0:1], score[:, :], AX.X, ALU.max).then_inc(local_top, 1)
                    dve.wait_ge(all_top, 1)
                    dve.tensor_scalar(top[:, 0:1], top[:, 1:2], -1.0, SHIFT, ALU.mult, ALU.add).then_inc(bias_ready, 1)
                    dve.wait_ge(weight_ready, 1)
                    v.then(dve.tensor_scalar(hsum[:, :], hsum[:, :], 0.0, None, ALU.not_equal))
                    v.wait()
                    v.then(dve.tensor_tensor(values[:, :, D], values[:, :, D], hsum[:, :], ALU.mult))
                    v.wait()
                    dve.wait_ge(val_copied, NB // G)
                    dve.tensor_tensor(values[:, :, 0:D], values[:, :, 0:D],
                                      values[:, :, D:PART].to_broadcast([P, NB, D]), ALU.mult).then_inc(high_ready, 1)
                    dve.wait_ge(high_ready, 2)
                    dve.tensor_tensor(values[:, :, :], values[:, :, :], parts[:, :, 0:PART], ALU.subtract).then_inc(mid_ready, 1)
                    dve.wait_ge(mid_ready, 2)
                    dve.tensor_tensor(parts[:, :, 2 * PART:V3], values[:, :, :], parts[:, :, PART:2 * PART], ALU.subtract)

        with ExitStack() as ctx:
            HALF = NB * P // 2
            NST = 3
            stage = [sb(f"stage{i}", [P, HALF], I32, ctx) for i in range(NST)]
            mask = [sb(f"mask{i}", [P, NB * P], U8, ctx) for i in range(2)]
            agg = sb("agg", [P, 2, PART], F32, ctx)
            inv = sb("inv", [P, 2], F32, ctx)
            ps_a = ps("ps_a", [P, 2, 512], F32, ctx)

            adj_in = [sem(f"adj_in{i}") for i in range(NST)]
            adj_used, mask_ready, agg_ready, agg_free, v_b = sem("adj_used"), sem("mask_ready"), sem("agg_ready"), sem("agg_free"), sem("v_b")
            UN = 6
            NH = 2 * NB
            with nc.Block() as block:
                def load(sp, half, s, wait):
                    if wait is not None:
                        sp.wait_ge(adj_used, wait)
                    sp.dma_start(stage[s][:, :], adj_t[ds(half, 1), :, :].rearrange("a p n -> p (a n)")).then_inc(adj_in[s], 16)

                @block.sync
                def _(sp):
                    for j in range(NST):
                        load(sp, j, j % NST, None)
                    with sp.Fori(0, NH // NST - 1) as i:
                        for s in range(NST):
                            load(sp, i * NST + (s + NST), s, i * NST + (s + 1))
                    for j in range(NH // NST * NST, NH):
                        load(sp, j, j % NST, j - NST + 1)

                @block.tensor
                def _(pe):
                    with pe.Fori(0, NB // 2) as i:
                        for k in range(2):
                            b = i * 2 + k
                            pe.wait_ge(mask_ready, b * 2 + 2)
                            pe.wait_ge(agg_free, b + 1)
                            pe.ldweights(ident16[:, :], tile_position=(0, 0))
                            for c in range(NB):
                                m = pe.matmul(ps_a[:, k, 0:V3], mask[k][:, c * P:(c + 1) * P].bitcast(F8), parts[:, c, :],
                                              start=(c == 0), stop=(c == NB - 1))
                            m.then_inc(agg_ready, 1)

                @block.vector
                def _(dve):
                    dve.sem_inc(agg_free, 2)

                    def masks(half, s, k, part, in_loop_round):
                        dve.wait_ge(adj_in[s], in_loop_round)
                        m = mask[k][:, part * HALF:(part + 1) * HALF]
                        dve.tensor_scalar(m, stage[s][:, :], 0, F8_ONE, ALU.is_gt, ALU.mult).then_inc(mask_ready, 1)
                        dve.tensor_scalar(equal_one[:, :, :].rearrange("p b n -> p (b n)")[:, ds(half * HALF, HALF)],
                                          stage[s][:, :], 1, F8_ONE, ALU.is_equal, ALU.mult).then_inc(adj_used, 1)

                    def finish(b, k, n):
                        dve.wait_ge(agg_ready, b + 1)
                        dve.tensor_reduce(agg[:, k, :], ps_a[:, k, 0:V3].rearrange("p (t f) -> p f t", t=3), AX.X, ALU.add)\
                           .then_inc(agg_free, 1)
                        dve.wait_ge(agg_free, b + 3)
                        dve.tensor_scalar(inv[:, k:k + 1], agg[:, k, D:PART], 1e-30, None, ALU.max).then_inc(v_b, 1)
                        dve.wait_ge(v_b, b * 2 + 1)
                        dve.reciprocal(inv[:, k:k + 1], inv[:, k:k + 1]).then_inc(v_b, 1)
                        dve.wait_ge(v_b, b * 2 + 2)
                        row = xs[:, ds(b, 1), :].rearrange("p a d -> p (a d)")
                        dve.scalar_tensor_tensor(out=row, in0=agg[:, k, 0:D], scalar=inv[:, k:k + 1], in1=row,
                                                 op0=ALU.mult, op1=ALU.add)

                    def halves(b, base_round, h0):
                        raise NotImplementedError

                    def body(b0, rounds, nblocks, first):
                        for j in range(nblocks):
                            for part in range(2):
                                hh = 2 * j + part
                                if part == 0 and not (first and j < 2):
                                    dve.wait_ge(agg_ready, b0 + (j - 1))
                                masks(b0 * 2 + hh, hh % NST, j % 2, part, rounds + 16 * (hh // NST + 1))
                            if not (first and j == 0):
                                finish(b0 + (j - 1), (j - 1) % 2, j)

                    body(0, 0, 6, True)
                    with dve.Fori(1, NB // 6) as i:
                        body(i * 6, i * 64, 6, False)
                    body(NB // 6 * 6, NB // 6 * 64, NB % 6, False)
                    finish(NB - 1, (NB - 1) % 2, 0)

                @block.gpsimd
                def _(pool):
                    pool.wait_ge(agg_ready, NB)

                @block.scalar
                def _(act):
                    act.wait_ge(agg_ready, NB)
        attend_ctx.close()

        with ExitStack() as ctx:
            G = 4
            TOPK_LOW = -3e38
            xn = sb("xn_rows", [P, NB, D], F32, ctx)
            xnt = sb("xnt_r", [P, 2, G * P], F32, ctx)
            gw = sb("gw", [P, E0], F32, ctx)
            gb = sb("gb", [P, E0], F32, ctx)
            falling = sb("falling", [P, E0], F32, ctx)
            tile_edge = sb("tile_edge", [P, NB], F32, ctx)
            tile_no = sb("tile_no", [1, TILES], F32, ctx)
            logit = sb("logit", [P, NB, E0], F32, ctx)
            pick = sb("pick", [P, NB, E0], F32, ctx)
            hot = [sb(f"hot{k}", [P, NB, E0], F32, ctx) for k in range(TOP)]
            both = sb("both", [P, E0, NB], BF16, ctx)
            keep = sb("keep", [P, E0, NB], F32, ctx)
            upto = sb("upto", [P, E0, NB], F32, ctx)
            place = sb("place", [P, E0, NB], F32, ctx)
            best = [sb(f"best{k}", [P, NB], F32, ctx) for k in range(TOP)]
            which = sb("which", [P, NB], F32, ctx)
            over_edge = sb("over_edge", [P, E0, NB], F32, ctx)
            ntiles = sb("ntiles", [P, E0], F32, ctx)
            ones_e = sb("ones_e", [P, E0], F32, ctx)
            cum = sb("cum", [P, E0], F32, ctx)
            first_row = sb("first_row", [P, E0], F32, ctx)
            past = sb("past", [1, TILES, E0], F32, ctx)
            texp = sb("texp", [1, TILES], F32, ctx)
            ps_t = ps("ps_t2", [P, 2, G * P], F32, ctx)
            ps_l = ps("ps_l", [P, NB * E0], F32, ctx)
            ps_rank = ps("ps_rank", [P, E0 * NB], F32, ctx)
            ps_count = ps("ps_count", [P, E0 * NB], F32, ctx)

            v_c, var_ready, root_ready = sem("v_c"), sem("var_ready2"), sem("root_ready2")
            gate_in, xn_ready, xt_ready, xt_copied = sem("gate_in"), sem("xn_ready2"), sem("xt_ready2"), sem("xt_copied2")
            iotas, logit_ready, gap_ready, ratio_ready = sem("iotas"), sem("logit_ready"), sem("gap_ready"), sem("ratio_ready")
            both_ready, count_ready, pos_ready, scattered = sem("both_ready"), sem("count_ready"), sem("pos_ready"), sem("scattered")
            with nc.Block() as block:
                @block.sync
                def _(sp):
                    sp.dma_start(gw[:, :], gate_w).then_inc(gate_in, 16)
                    sp.dma_start(gb[:, :], gate_b.partition_broadcast(P)).then_inc(gate_in, 16)

                @block.gpsimd
                def _(pool):
                    exact = dict(allow_small_or_imprecise_dtypes=True)
                    pool.iota(falling[:, :], pattern=[[-1, E0]], base=E0, channel_multiplier=0, **exact).then_inc(iotas, 1)
                    pool.iota(tile_edge[:, :], pattern=[[P, NB]], base=0, channel_multiplier=0, **exact).then_inc(iotas, 1)
                    pool.iota(tile_no[:, :], pattern=[[1, TILES]], base=0, channel_multiplier=0, **exact).then_inc(iotas, 1)
                    pool.memset(keep[:, :, :], 1.0).then_inc(iotas, 1)
                    pool.memset(ones_e[:, :], 1.0).then_inc(iotas, 1)
                    pool.wait_ge(iotas, 5)
                    pool.memset(keep[:, :, 0:1], 0.0).then_inc(iotas, 1)
                    pool.wait_ge(pos_ready, 2)
                    for c in range(NB):
                        for k in range(TOP):
                            pool.indirect_dma_start(out=sorted_x, out_offset=bass.IndirectOffsetOnAxis(ap=pos[:, k, c:c + 1], axis=0),
                                                    in_=xn[:, c, :], in_offset=None).then_inc(scattered, 16)
                    pool.wait_ge(scattered, 16 * TOP * NB)

                @block.scalar
                def _(act):
                    act.wait_ge(var_ready, 1)
                    act.activation(tmp[1][:, :], tmp[0][:, :], ACT.Sqrt).then_inc(root_ready, 1)
                    with act.Fori(0, NB // G // 2) as i:
                        for k in range(2):
                            act.wait_ge(xt_ready, i * 2 + (k + 1))
                            act.activation(xnt[:, k, :], ps_t[:, k, :], ACT.Copy).then_inc(xt_copied, 1)
                    act.wait_ge(gap_ready, 1)
                    act.activation(gates[:, 1, :], tmp[0][:, :], ACT.Exp).then_inc(ratio_ready, 1)

                @block.tensor
                def _(pe):
                    pe.wait_ge(gate_in, 32)
                    for g in range(NB // G):
                        k = g % 2
                        pe.wait_ge(xn_ready, g + 1)
                        for c in range(G):
                            t = pe.transpose(ps_t[:, k, c * P:(c + 1) * P], xn[:, g * G + c, :], ident[:, :])
                        t.then_inc(xt_ready, 1)
                        pe.wait_ge(xt_copied, g + 1)
                        for c in range(G):
                            b = g * G + c
                            m = pe.matmul(ps_l[:, b * E0:(b + 1) * E0], xnt[:, k, c * P:(c + 1) * P], gw[:, :],
                                          start=True, stop=True)
                        m.then_inc(logit_ready, 1)
                    pe.wait_ge(both_ready, 1)
                    rhs = both[:, :, :].rearrange("p e b -> p (e b)")
                    pe.matmul(ps_rank[:, :], before[:, :], rhs, start=True, stop=True)
                    pe.matmul(ps_count[:, :], ones16[:, :], rhs, start=True, stop=True).then_inc(count_ready, 1)

                @block.vector
                def _(dve):
                    v = Steps(dve, v_c)
                    row_norms(dve, v, var_ready, root_ready)
                    with dve.Fori(0, NB // G) as g:
                        for c in range(G):
                            b = g * G + c
                            n = dve.tensor_scalar(xn[:, ds(b, 1), :].rearrange("p a d -> p (a d)"),
                                                  xs[:, ds(b, 1), :].rearrange("p a d -> p (a d)"),
                                                  mean[:, ds(b, 1)], rstd[:, ds(b, 1)], ALU.subtract, ALU.mult)
                        n.then_inc(xn_ready, 1)
                    S3 = [P, NB, E0]
                    dve.wait_ge(iotas, 6)
                    dve.wait_ge(gate_in, 32)
                    dve.wait_ge(logit_ready, NB // G)
                    v.then(dve.tensor_tensor(logit[:, :, :], ps_l[:, :].rearrange("p (b e) -> p b e", e=E0),
                                             over(gb[:, :], S3, 1), ALU.add))
                    v.wait()
                    for k in range(TOP):
                        v.then(dve.tensor_reduce(best[k][:, :], logit[:, :, :], AX.X, ALU.max))
                        v.wait()
                        v.then(dve.tensor_tensor(pick[:, :, :], logit[:, :, :], over(best[k][:, :], S3, 2), ALU.is_ge))
                        v.wait()
                        v.then(dve.tensor_tensor(pick[:, :, :], pick[:, :, :], over(falling[:, :], S3, 1), ALU.mult))
                        v.wait()
                        v.then(dve.tensor_reduce(which[:, :], pick[:, :, :], AX.X, ALU.max))
                        v.wait()
                        v.then(dve.tensor_tensor(hot[k][:, :, :], over(falling[:, :], S3, 1), over(which[:, :], S3, 2), ALU.is_equal))
                        v.wait()
                        if k == 0:
                            v.then(dve.scalar_tensor_tensor(out=logit[:, :, :], in0=hot[0][:, :, :], scalar=TOPK_LOW,
                                                            in1=logit[:, :, :], op0=ALU.mult, op1=ALU.add))
                            v.wait()
                    dve.tensor_tensor(both[:, :, :].rearrange("p e b -> p b e"), hot[0][:, :, :], hot[1][:, :, :], ALU.add)\
                       .then_inc(both_ready, 1)
                    dve.tensor_tensor(tmp[0][:, :], best[1][:, :], best[0][:, :], ALU.subtract).then_inc(gap_ready, 1)
                    dve.wait_ge(ratio_ready, 1)
                    v.then(dve.tensor_scalar(tmp[1][:, :], gates[:, 1, :], 1.0, None, ALU.add))
                    v.wait()
                    v.then(dve.reciprocal(gates[:, 0, :], tmp[1][:, :]))
                    v.wait()
                    v.then(dve.tensor_tensor(gates[:, 1, :], gates[:, 1, :], gates[:, 0, :], ALU.mult))
                    dve.wait_ge(count_ready, 1)
                    v.then(dve.tensor_tensor_scan(upto[:, :, :].rearrange("p e b -> p (e b)"), keep[:, :, :].rearrange("p e b -> p (e b)"),
                                                  ps_count[:, :], 0.0, ALU.mult, ALU.add))
                    v.wait()
                    v.then(dve.tensor_tensor(over_edge[:, :, :], upto[:, :, NB - 1:NB].to_broadcast([P, E0, NB]),
                                             over(tile_edge[:, :], [P, E0, NB], 1), ALU.is_gt))
                    v.wait()
                    v.then(dve.tensor_reduce(ntiles[:, :], over_edge[:, :, :], AX.X, ALU.add))
                    v.then(dve.tensor_tensor(place[:, :, :].rearrange("p e b -> p (e b)"), upto[:, :, :].rearrange("p e b -> p (e b)"),
                                             ps_count[:, :], ALU.subtract))
                    v.wait()
                    v.then(dve.tensor_tensor_scan(cum[:, :], ones_e[:, :], ntiles[:, :], 0.0, ALU.mult, ALU.add))
                    v.wait()
                    v.then(dve.tensor_tensor(first_row[:, :], cum[:, :], ntiles[:, :], ALU.subtract))
                    v.wait()
                    v.then(dve.tensor_scalar(first_row[:, :], first_row[:, :], float(P), None, ALU.mult))
                    v.then(dve.tensor_tensor(place[:, :, :].rearrange("p e b -> p (e b)"), place[:, :, :].rearrange("p e b -> p (e b)"),
                                             ps_rank[:, :], ALU.add))
                    v.wait()
                    v.then(dve.tensor_tensor(place[:, :, :], place[:, :, :], over(first_row[:, :], [P, E0, NB], 2), ALU.add))
                    v.wait()
                    for k in range(TOP):
                        v.then(dve.tensor_tensor(pick[:, :, :], hot[k][:, :, :], place[:, :, :].rearrange("p e b -> p b e"), ALU.mult))
                        v.wait()
                        v.then(dve.tensor_reduce(best[k][:, :], pick[:, :, :], AX.X, ALU.add))
                        v.wait()
                        dve.tensor_copy(pos[:, k, :], best[k][:, :]).then_inc(pos_ready, 1)
                    S = [1, TILES, E0]
                    v.then(dve.tensor_tensor(past[:, :, :], over(tile_no[:, :], S, 2), over(cum[0:1, :], S, 1), ALU.is_ge))
                    v.wait()
                    v.then(dve.tensor_reduce(texp[:, :], past[:, :, :], AX.X, ALU.add))
                    v.wait()
                    v.then(dve.tensor_scalar(texp[:, :], texp[:, :], float(E0 - 1), None, ALU.min))
                    v.wait()
                    v.then(dve.tensor_scalar(tile_w12[:, :], texp[:, :], float(2 * H0), None, ALU.mult))
                    v.then(dve.tensor_scalar(tile_w3[:, :], texp[:, :], float(HC0 * D), None, ALU.mult))
                    v.wait()

        with ExitStack() as ctx:
            UN = 4
            w12 = sb("w12", [P, E0, 2 * H0], F32, ctx)
            w3s = sb("w3s", [P, E0, HC0, D], F32, ctx)
            xt = sb("xt", [P, UN, D], F32, ctx)
            xT = sb("xT", [P, 2, P], F32, ctx)
            gate_act = sb("gate_act", [P, 2, H0], F32, ctx)
            hid = sb("hid", [P, 2, H0], F32, ctx)
            hT = sb("hT", [P, 2, H0], F32, ctx)
            y = sb("y", [P, 2, D], F32, ctx)
            ps_x = ps("ps_x", [P, 2, 512], F32, ctx)
            ps_h = ps("ps_h", [P, 2, 512], F32, ctx)
            ps_ht = ps("ps_ht", [P, 2, 512], F32, ctx)
            ps_y = ps("ps_y", [P, 2, 512], F32, ctx)
            w_in = [sem(f"w_in_e{i}") for i in range(3)]
            row_in = [sem(f"row_in{i}") for i in range(UN)]
            stored = [sem(f"stored{i}") for i in range(2)]
            tx_ready, x_copied, h_ready, gated, hid_ready = sem("tx_ready"), sem("x_copied"), sem("h_ready_e"), sem("gated"), sem("hid_ready")
            ht_ready, ht_copied, y_ready, y_copied = sem("ht_ready"), sem("ht_copied"), sem("y_ready"), sem("y_copied")
            w12f = w12[:, :, :].rearrange("p e n -> p (e n)")
            w3f = w3s[:, :, :, :].rearrange("p e c n -> p (e c n)")
            LAST = TILES + 3
            assert TILES % UN == 0

            def in_steps(eng, step):
                for s in range(UN):
                    step(s, s, s)
                with eng.Fori(1, TILES // UN) as i:
                    for j in range(UN):
                        step(i * UN + j, j, None)
                for s in range(TILES, LAST):
                    step(s, s % UN, s)

            def runs(s, known, lag):
                return known is None or 0 <= known - lag < TILES

            with nc.Block() as block:
                @block.sync
                def _(sp):
                    sp.dma_start(w12[:, :, 0:H0], w1.rearrange("e d h -> d e h")).then_inc(w_in[0], 16)
                    sp.dma_start(w12[:, :, H0:2 * H0], w2.rearrange("e d h -> d e h")).then_inc(w_in[1], 16)
                    for c in range(HC0):
                        sp.dma_start(w3s[:, :, c, :], w3[:, c * P:(c + 1) * P, :].rearrange("e p o -> p e o")).then_inc(w_in[2], 16)

                    def load(s, j, known):
                        if not runs(s, known, 0):
                            return
                        if known is None:
                            sp.wait_ge(tx_ready, s - (UN - 1))
                        sp.dma_start(xt[:, j, :], sorted_x.rearrange("(t p) d -> t p d", p=P)[ds(s, 1), :, :]
                                     .rearrange("t p d -> p (t d)")).then_inc(row_in[j], 16)
                    in_steps(sp, load)

                @block.gpsimd
                def _(pool):
                    pool.wait_ge(y_copied, TILES)

                @block.scalar
                def _(act):
                    def step(s, j, known):
                        if runs(s, known, 0):
                            k = j % 2
                            act.wait_ge(tx_ready, s + 1)
                            act.activation(xT[:, k, :], ps_x[:, k, 0:P], ACT.Copy).then_inc(x_copied, 1)
                        if runs(s, known, 1):
                            k = (j - 1) % 2
                            act.wait_ge(h_ready, s)
                            act.activation(gate_act[:, k, :], ps_h[:, k, 0:H0], ACT.Silu).then_inc(gated, 1)
                        if runs(s, known, 3):
                            k = (j - 3) % 2
                            act.wait_ge(y_ready, s - 2)
                            if known is None or known - 3 >= 2:
                                act.wait_ge(stored[k], stored_upto(s, j, known))
                            act.activation(y[:, k, :], ps_y[:, k, 0:D], ACT.Copy).then_inc(y_copied, 1)
                            act.wait_ge(y_copied, s - 2)
                            act.dma_start(sorted_y.rearrange("(t p) d -> t p d", p=P)[ds(s - 3, 1), :, :]
                                          .rearrange("t p d -> p (t d)"), y[:, k, :]).then_inc(stored[k], 16)

                    def stored_upto(s, j, known):
                        if known is not None:
                            return (known - 3) // 2 * 16
                        return (s - j) * 8 + (j - 3) // 2 * 16
                    in_steps(act, step)
                    act.wait_ge(stored[0], TILES // 2 * 16)
                    act.wait_ge(stored[1], TILES // 2 * 16)

                @block.tensor
                def _(pe):
                    def row_round(s, j, known):
                        return (known // UN + 1) * 16 if known is not None else (s - j) * (16 // UN) + 16

                    def step(s, j, known):
                        if runs(s, known, 0):
                            pe.wait_ge(row_in[j], row_round(s, j, known))
                            pe.transpose(ps_x[:, j % 2, 0:P], xt[:, j, :], ident[:, :]).then_inc(tx_ready, 1)
                        if runs(s, known, 1):
                            k = (j - 1) % 2
                            if known == 1:
                                for w in w_in:
                                    pe.wait_ge(w, 16 if w is not w_in[2] else 16 * HC0)
                            off = pe.value_load(tile_w12[0:1, ds(s - 1, 1)], min_val=0, max_val=(E0 - 1) * 2 * H0)
                            pe.wait_ge(x_copied, s)
                            pe.matmul(ps_h[:, k, :], xT[:, k, :], w12f[:, ds(off, 2 * H0)], start=True, stop=True).then_inc(h_ready, 1)
                        if runs(s, known, 2):
                            k = (j - 2) % 2
                            pe.wait_ge(hid_ready, s - 1)
                            for c in range(HC0):
                                t = pe.transpose(ps_ht[:, k, c * P:(c + 1) * P], hid[:, k, c * P:(c + 1) * P], ident[:, :])
                            t.then_inc(ht_ready, 1)
                        if runs(s, known, 3):
                            k = (j - 3) % 2
                            off = pe.value_load(tile_w3[0:1, ds(s - 3, 1)], min_val=0, max_val=(E0 - 1) * HC0 * D)
                            pe.wait_ge(ht_copied, s - 2)
                            if known is None or known - 3 >= 2:
                                pe.wait_ge(y_copied, s - 4)
                            for c in range(HC0):
                                m = pe.matmul(ps_y[:, k, 0:D], hT[:, k, c * P:(c + 1) * P], w3f[:, ds(off + c * D, D)],
                                              start=(c == 0), stop=(c == HC0 - 1))
                            m.then_inc(y_ready, 1)
                    in_steps(pe, step)

                @block.vector
                def _(dve):
                    def step(s, j, known):
                        if runs(s, known, 1):
                            k = (j - 1) % 2
                            dve.wait_ge(gated, s)
                            dve.tensor_tensor(hid[:, k, :], gate_act[:, k, :], ps_h[:, k, H0:2 * H0], ALU.mult).then_inc(hid_ready, 1)
                        if runs(s, known, 2):
                            k = (j - 2) % 2
                            dve.wait_ge(ht_ready, s - 1)
                            if known is None or known - 2 >= 2:
                                dve.wait_ge(y_ready, s - 3)
                            dve.tensor_copy(hT[:, k, :], ps_ht[:, k, 0:H0]).then_inc(ht_copied, 1)
                    in_steps(dve, step)

        mean_ctx = ExitStack()
        parts2 = sb("parts2", [P, NB, V2], F16, mean_ctx)
        with ExitStack() as ctx:
            rows = sb("rows", [P, TOP, NB, D], F32, ctx)
            v_d, var_ready, root_ready = sem("v_d"), sem("var_ready3"), sem("root_ready3")
            gathered = [sem(f"gathered{i}") for i in range(NB)]
            xn_ready, high_ready = sem("xn_ready3"), sem("high_ready3")
            xn = rows[:, 0, :, :]
            with nc.Block() as block:
                @block.gpsimd
                def _(pool):
                    for c in range(NB):
                        for k in range(TOP):
                            pool.indirect_dma_start(out=rows[:, k, c, :], out_offset=None, in_=sorted_y,
                                                    in_offset=bass.IndirectOffsetOnAxis(ap=pos[:, k, c:c + 1], axis=0))\
                                .then_inc(gathered[c], 16)

                @block.scalar
                def _(act):
                    act.wait_ge(var_ready, 1)
                    act.activation(tmp[1][:, :], tmp[0][:, :], ACT.Sqrt).then_inc(root_ready, 1)
                    act.wait_ge(xn_ready, 1)
                    act.activation(parts2[:, :, 0:D], xn, ACT.Copy).then_inc(high_ready, 1)

                @block.vector
                def _(dve):
                    v = Steps(dve, v_d)
                    v.then(dve.memset(parts2[:, :, 2 * D:V2], 1.0))
                    for c in range(NB):
                        dve.wait_ge(gathered[c], 16 * TOP)
                        for k in range(TOP):
                            v.then(dve.scalar_tensor_tensor(out=xs[:, c, :], in0=rows[:, k, c, :], scalar=gates[:, k, c:c + 1],
                                                            in1=xs[:, c, :], op0=ALU.mult, op1=ALU.add))
                            v.wait()
                    row_norms(dve, v, var_ready, root_ready)
                    with dve.Fori(0, NB) as b:
                        n = dve.tensor_scalar(rows[:, 0, ds(b, 1), :].rearrange("p a d -> p (a d)"),
                                              xs[:, ds(b, 1), :].rearrange("p a d -> p (a d)"),
                                              mean[:, ds(b, 1)], rstd[:, ds(b, 1)], ALU.subtract, ALU.mult).then_inc(v_d, 1)
                    v.n += NB
                    dve.wait_ge(v_d, v.n)
                    dve.sem_inc(xn_ready, 1)
                    dve.wait_ge(high_ready, 1)
                    v.then(dve.tensor_tensor(xn, xn, parts2[:, :, 0:D], ALU.subtract))
                    v.wait()
                    v.then(dve.tensor_scalar(parts2[:, :, D:2 * D], xn, LOW_SCALE, None, ALU.mult))
                    v.wait()

        with ExitStack() as ctx:
            mask = sb("mask2", [P, 2, NB * P], U8, ctx)
            wt = sb("wt", [P, D], F32, ctx)
            wb = sb("wb", [P, D], F32, ctx)
            rt = sb("rt", [P, E1], F32, ctx)
            rb = sb("rb", [P, E1], F32, ctx)
            fw1 = sb("fw1", [P, E1, H1], F32, ctx)
            fb1 = sb("fb1", [P, KC1], F32, ctx)
            fw2 = sb("fw2", [P, KC1, D], F32, ctx)
            fb2 = sb("fb2", [E1, D], F32, ctx)
            expert_of = sb("expert_of", [P, KC1], F32, ctx)
            expert_no = sb("expert_no", [E1, 1], F32, ctx)
            sums = sb("sums", [P, 2, V2], F32, ctx)
            inv = sb("inv2", [P, 2], F32, ctx)
            agg = sb("agg2", [P, 2, D], F32, ctx)
            aggt = sb("aggt", [P, 2, P], F32, ctx)
            xc = sb("xc", [P, D], F32, ctx)
            sq = sb("sq", [P, 6], F32, ctx)
            xn = sb("xn3", [P, 2, D], F32, ctx)
            xnt = sb("xnt3", [P, 2, P], F32, ctx)
            lg = sb("lg", [P, E1], F32, ctx)
            best1 = sb("best_logit", [P, 1], F32, ctx)
            which1 = sb("which1", [P, 1], F32, ctx)
            falling1 = sb("falling1", [P, E1], F32, ctx)
            idx_wide = sb("idx_wide", [P, 2, P], BF16, ctx)
            hot_t = sb("hot_t", [E1, P], F32, ctx)
            hr = sb("hr", [P, KC1, P], F32, ctx)
            hm = sb("hm", [P, KC1, P], F32, ctx)
            fin = sb("fin", [P, 2, D], F32, ctx)
            ps_a = ps("ps_a2", [P, 2, 512], F32, ctx)
            ps_f = ps("ps_f", [P, 2, 512], F32, ctx)
            ps_t = ps("ps_t3", [P, 512], F32, ctx)
            ps_w = ps("ps_w", [P, 512], F32, ctx)
            ps_i = ps("ps_i", [P, 512], F32, ctx)
            ps_o = ps("ps_o", [P, 512], F32, ctx)
            names = "w_in_m const_ready mask_copied agg_ready sums_copied norm_ready at_ready at_copied wx_ready var_ready4 root_ready4 " \
                    "xn_ready4 xt_ready4 xt_copied4 lg_ready lg_read idx_ready ib_ready f_ready relu_ready hm_ready o_ready fin_ready v_e".split()
            (w_in, const_ready, mask_copied, agg_ready, sums_copied, norm_ready, at_ready, at_copied, wx_ready, var_ready, root_ready,
             xn_ready, xt_ready, xt_copied, lg_ready, lg_read, idx_ready, ib_ready, f_ready, relu_ready, hm_ready, o_ready, fin_ready,
             v_e) = [sem("m_" + n) for n in names]
            stored = [sem(f"stored_m{i}") for i in range(2)]
            LAST = NB + 3
            CH = KC1 // 2

            def in_steps(eng, step):
                for u in range(4):
                    step(u, u % 2, u)
                with eng.Fori(2, NB // 2) as i:
                    for k in range(2):
                        step(i * 2 + k, k, None)
                for u in range(NB, LAST):
                    step(u, u % 2, u)

            def runs(known, lag):
                return known is None or 0 <= known - lag < NB

            def late(known, lag):
                return known is None or known - lag >= 2

            with nc.Block() as block:
                @block.sync
                def _(sp):
                    loads = [(wt[:, :], g1_wt), (wb[:, :], g1_b.partition_broadcast(P)), (rt[:, :], router_wt),
                             (rb[:, :], router_b.partition_broadcast(P)), (fw1[:, :, :], f_w1.rearrange("e d h -> d e h")),
                             (fb1[:, :], f_b1),
                             (fw2[:, :, :], f_w2.rearrange("(k a) h d -> (a h) k d", k=KC1)), (fb2[:, :], f_b2)]
                    for to, of in loads:
                        sp.dma_start(to, of).then_inc(w_in, 16)

                    def step(u, k, known):
                        if runs(known, 3):
                            k = (k - 3) % 2
                            sp.wait_ge(fin_ready, u - 2)
                            sp.dma_start(out.rearrange("(b p) d -> b p d", p=P)[ds(u - 3, 1), :, :].rearrange("b p d -> p (b d)"),
                                         fin[:, k, :]).then_inc(stored[k], 16)
                    in_steps(sp, step)
                    sp.wait_ge(stored[0], NB // 2 * 16)
                    sp.wait_ge(stored[1], NB // 2 * 16)

                @block.gpsimd
                def _(pool):
                    exact = dict(allow_small_or_imprecise_dtypes=True)
                    per = P // H1
                    for a in range(per):
                        pool.iota(expert_of[a * H1:(a + 1) * H1, :], pattern=[[-per, KC1]], base=E1 - a, channel_multiplier=0, **exact)\
                            .then_inc(const_ready, 1)
                        pool.wait_ge(const_ready, a + 1)
                    pool.iota(falling1[:, :], pattern=[[-1, E1]], base=E1, channel_multiplier=0, **exact).then_inc(const_ready, 1)
                    pool.iota(expert_no[:, :], pattern=[[1, 1]], base=E1, channel_multiplier=-1, **exact).then_inc(const_ready, 1)

                    def step(u, k, known):
                        if runs(known, 0):
                            if late(known, 0):
                                pool.wait_ge(agg_ready, u - 1)
                            pool.tensor_copy(mask[:, k, :].bitcast(F32), equal_one[:, ds(u, 1), :].rearrange("p b n -> p (b n)").bitcast(F32))\
                                .then_inc(mask_copied, 1)
                    in_steps(pool, step)

                @block.scalar
                def _(act):
                    act.wait_ge(w_in, 16 * 8)

                    def step(u, k, known):
                        o = 1 - k
                        if runs(known, 1):
                            act.wait_ge(agg_ready, u)
                            if late(known, 1):
                                act.wait_ge(norm_ready, u - 2)
                            act.activation(sums[:, o, :], ps_a[:, o, 0:V2], ACT.Copy).then_inc(sums_copied, 1)
                            act.wait_ge(at_ready, u)
                            act.activation(aggt[:, o, :], ps_t[:, 0:P], ACT.Copy).then_inc(at_copied, 1)

                        def relus(half):
                            act.wait_ge(f_ready, u * 2 - 3 + half)
                            for c in range(half * CH, (half + 1) * CH):
                                r = act.activation(hr[:, c, :], ps_f[:, half, (c - half * CH) * P:(c - half * CH + 1) * P],
                                                   ACT.Relu, bias=fb1[:, c:c + 1])
                            r.then_inc(relu_ready, 1)
                        if runs(known, 2):
                            if known is None or known - 2 >= 1:
                                act.wait_ge(hm_ready, u - 2)
                            relus(0)
                        if runs(known, 1):
                            act.wait_ge(var_ready, u)
                            act.activation(sq[:, 1:2], sq[:, 0:1], ACT.Sqrt).then_inc(root_ready, 1)
                        if runs(known, 2):
                            relus(1)
                        if runs(known, 1):
                            act.wait_ge(xt_ready, u)
                            act.activation(xnt[:, o, :], ps_t[:, 0:P], ACT.Copy).then_inc(xt_copied, 1)
                    in_steps(act, step)

                @block.tensor
                def _(pe):
                    pe.wait_ge(w_in, 16 * 8)

                    def step(u, k, known):
                        o = 1 - k

                        def products(lo, hi):
                            if not runs(known, 0):
                                return
                            if lo == 0:
                                pe.wait_ge(mask_copied, u + 1)
                                if late(known, 0):
                                    pe.wait_ge(sums_copied, u - 1)
                                pe.ldweights(ident16[:, :], tile_position=(0, 0))
                            for c in range(lo, hi):
                                m = pe.matmul(ps_a[:, k, 0:V2], mask[:, k, c * P:(c + 1) * P].bitcast(F8), parts2[:, c, :],
                                              start=(c == 0), stop=(c == NB - 1))
                            if hi == NB:
                                m.then_inc(agg_ready, 1)

                        q = NB // 8
                        products(0, q)
                        if runs(known, 3):
                            pe.wait_ge(hm_ready, u - 2)
                            if known is None or known - 3 >= 1:
                                pe.wait_ge(fin_ready, u - 3)
                            for c in range(KC1):
                                pe.matmul(ps_o[:, 0:D], hm[:, c, :], fw2[:, c, :], start=(c == 0), stop=False)
                            pe.matmul(ps_o[:, 0:D], hot_t[:, :], fb2[:, :], start=False, stop=True).then_inc(o_ready, 1)
                        if runs(known, 0):
                            pe.ldweights(ident16[:, :], tile_position=(0, 0))
                        products(q, 3 * q)
                        if runs(known, 2):
                            pe.wait_ge(xt_copied, u - 1)
                            pe.matmul(ps_w[:, D:D + E1], xnt[:, k, :], rt[:, :], start=True, stop=True).then_inc(lg_ready, 1)
                            if known is None or known - 2 >= 1:
                                pe.wait_ge(relu_ready, u * 2 - 4)
                            for c in range(KC1):
                                m = pe.matmul(ps_f[:, c // CH, c % CH * P:(c % CH + 1) * P],
                                              fw1[:, c * (P // H1):(c + 1) * (P // H1), :].rearrange("p a h -> p (a h)"), xnt[:, k, :],
                                              start=True, stop=True)
                                if c % CH == CH - 1:
                                    m.then_inc(f_ready, 1)
                        if runs(known, 1):
                            pe.wait_ge(norm_ready, u)
                            pe.transpose(ps_t[:, 0:P], agg[:, o, :], ident[:, :]).then_inc(at_ready, 1)
                        if runs(known, 0):
                            pe.ldweights(ident16[:, :], tile_position=(0, 0))
                        products(3 * q, 5 * q)
                        if runs(known, 1):
                            pe.wait_ge(at_copied, u)
                            if runs(known, 2):
                                pe.wait_ge(lg_read, u - 1)
                            pe.matmul(ps_w[:, 0:D], aggt[:, o, :], wt[:, :], start=True, stop=True).then_inc(wx_ready, 1)
                        if runs(known, 0):
                            pe.ldweights(ident16[:, :], tile_position=(0, 0))
                        products(5 * q, 6 * q)
                        if runs(known, 2):
                            pe.wait_ge(idx_ready, u - 1)
                            if known is None or known - 2 >= 1:
                                pe.wait_ge(hm_ready, u - 2)
                            pe.matmul(ps_i[:, 0:P], idx_wide[:, k, :], ident16[:, :], start=True, stop=True).then_inc(ib_ready, 1)
                        if runs(known, 0):
                            pe.ldweights(ident16[:, :], tile_position=(0, 0))
                        products(6 * q, 8 * q)
                        if runs(known, 1):
                            pe.wait_ge(xn_ready, u)
                            pe.transpose(ps_t[:, 0:P], xn[:, o, :], ident[:, :]).then_inc(xt_ready, 1)
                    in_steps(pe, step)

                @block.vector
                def _(dve):
                    dve.wait_ge(w_in, 16 * 8)
                    dve.wait_ge(const_ready, P // H1 + 2)

                    def step(u, k, known):
                        o = 1 - k

                        if runs(known, 1):
                            dve.wait_ge(sums_copied, u)
                            dve.reciprocal(inv[:, o:o + 1], sums[:, o, 2 * D:V2]).then_inc(own["a"], 1)
                            dve.scalar_tensor_tensor(out=agg[:, o, :], in0=sums[:, o, D:2 * D], scalar=1.0 / LOW_SCALE,
                                                     in1=sums[:, o, 0:D], op0=ALU.mult, op1=ALU.add).then_inc(own["a"], 1)
                            dve.wait_ge(own["a"], u * 2)
                            dve.tensor_scalar(agg[:, o, :], agg[:, o, :], inv[:, o:o + 1], None, ALU.mult).then_inc(norm_ready, 1)
                        if runs(known, 3):
                            dve.wait_ge(o_ready, u - 2)
                            if late(known, 3):
                                dve.wait_ge(stored[o], stored_upto(u, k, known))
                            dve.scalar_tensor_tensor(out=fin[:, o, :], in0=ps_o[:, 0:D], scalar=0.0,
                                                     in1=xs[:, ds(u - 3, 1), :].rearrange("p a d -> p (a d)"),
                                                     op0=ALU.max, op1=ALU.add).then_inc(fin_ready, 1)
                        if runs(known, 2):
                            dve.wait_ge(lg_ready, u - 1)
                            dve.tensor_tensor(lg[:, :], ps_w[:, D:D + E1], rb[:, :], ALU.add).then_inc(lg_read, 1)
                            dve.wait_ge(lg_read, u - 1)
                            dve.tensor_reduce(best1[:, :], lg[:, :], AX.X, ALU.max).then_inc(own["b"], 1)
                            dve.wait_ge(own["b"], u * 3 - 5)
                            dve.scalar_tensor_tensor(out=lg[:, :], in0=lg[:, :], scalar=best1[:, :], in1=falling1[:, :],
                                                     op0=ALU.is_ge, op1=ALU.mult).then_inc(own["b"], 1)
                            dve.wait_ge(own["b"], u * 3 - 4)
                            dve.tensor_reduce(which1[:, :], lg[:, :], AX.X, ALU.max).then_inc(own["b"], 1)
                            dve.wait_ge(own["b"], u * 3 - 3)
                            dve.tensor_copy(idx_wide[:, k, :], which1[:, :].to_broadcast([P, P])).then_inc(idx_ready, 1)
                        if runs(known, 1):
                            row = xs[:, ds(u - 1, 1), :].rearrange("p a d -> p (a d)")
                            C = 8
                            at = lambda n: u * C - (C - n)
                            dve.wait_ge(wx_ready, u)
                            dve.tensor_tensor(xc[:, :], ps_w[:, 0:D], wb[:, :], ALU.add).then_inc(own["c"], 1)
                            dve.wait_ge(own["c"], at(1))
                            dve.scalar_tensor_tensor(out=row, in0=xc[:, :], scalar=1.0, in1=row, op0=ALU.mult, op1=ALU.add,
                                                     accum_out=sq[:, 4:5]).then_inc(own["c"], 1)
                            dve.wait_ge(own["c"], at(2))
                            dve.tensor_scalar(sq[:, 5:6], sq[:, 4:5], -1.0 / D, None, ALU.mult).then_inc(own["c"], 1)
                            dve.wait_ge(own["c"], at(3))
                            dve.tensor_scalar(xc[:, :], row, sq[:, 5:6], None, ALU.add).then_inc(own["c"], 1)
                            dve.wait_ge(own["c"], at(4))
                            dve.scalar_tensor_tensor(out=xn[:, o, :], in0=xc[:, :], scalar=1.0, in1=xc[:, :], op0=ALU.mult,
                                                     op1=ALU.mult, accum_out=sq[:, 4:5]).then_inc(own["c"], 1)
                            dve.wait_ge(own["c"], at(5))
                            dve.tensor_scalar(sq[:, 0:1], sq[:, 4:5], 1.0 / D, EPS, ALU.mult, ALU.add).then_inc(var_ready, 1)
                            dve.wait_ge(root_ready, u)
                            dve.reciprocal(sq[:, 2:3], sq[:, 1:2]).then_inc(own["c"], 1)
                            dve.wait_ge(own["c"], at(6))
                            dve.tensor_scalar(sq[:, 2:3], sq[:, 0:1], sq[:, 2:3], sq[:, 1:2], ALU.mult, ALU.add).then_inc(own["c"], 1)
                            dve.wait_ge(own["c"], at(7))
                            dve.reciprocal(sq[:, 3:4], sq[:, 2:3]).then_inc(own["c"], 1)
                            dve.wait_ge(own["c"], at(8))
                            dve.tensor_scalar(xn[:, o, :], xc[:, :], sq[:, 3:4], 2.0, ALU.mult, ALU.mult).then_inc(xn_ready, 1)
                        if runs(known, 2):
                            dve.wait_ge(ib_ready, u - 1)
                            if known is None or known - 2 >= 1:
                                dve.wait_ge(o_ready, u - 2)
                            dve.tensor_scalar(hot_t[:, :], ps_i[0:E1, 0:P], expert_no[:, :], None, ALU.is_equal)
                            for half in range(2):
                                dve.wait_ge(relu_ready, u * 2 - 3 + half)
                                for c in range(half * CH, (half + 1) * CH):
                                    m = dve.scalar_tensor_tensor(out=hm[:, c, :], in0=ps_i[:, 0:P], scalar=expert_of[:, c:c + 1],
                                                                 in1=hr[:, c, :], op0=ALU.is_equal, op1=ALU.mult)
                            m.then_inc(hm_ready, 1)

                    def stored_upto(u, k, known):
                        if known is not None:
                            return (known - 3) // 2 * 16
                        return (u - k) * 8 + (k - 3) // 2 * 16
                    own = {n: sem("own_" + n) for n in "abc"}
                    in_steps(dve, step)
        mean_ctx.close()


def kernel(**inputs):
    import numpy as np
    import concourse.bacc as bacc
    from concourse.bass_utils import run_bass_kernel_spmd

    a = {k: np.asarray(v) for k, v in inputs.items()}
    n = a["x"].shape[0]
    nb = n // 128
    adj = a["adj"].reshape(nb, 128, 2, nb // 2, 128).transpose(0, 2, 4, 3, 1).reshape(2 * nb, 128, nb // 2 * 128)
    e1, d, h1 = a["L1_ffn_W1"].shape
    arrays = {
        "x": a["x"],
        "adj_t": adj,
        "g0_w": a["L0_gnn_W"], "g0_b": a["L0_gnn_b"], "g0_a": a["L0_gnn_a"],
        "gate_w": a["L0_ffn_gate_w"], "gate_b": a["L0_ffn_gate_b"],
        "w1": a["L0_ffn_w1"], "w2": a["L0_ffn_w2"], "w3": a["L0_ffn_w3"],
        "g1_wt": a["L1_gnn_W"].T, "g1_b": a["L1_gnn_b"],
        "router_wt": a["L1_ffn_router_w"].T, "router_b": a["L1_ffn_router_b"],
        "f_w1": a["L1_ffn_W1"], "f_b1": a["L1_ffn_b1"].reshape(-1, 128).T, "f_w2": a["L1_ffn_W2"], "f_b2": a["L1_ffn_b2"],
    }
    nc = bacc.Bacc("TRN2", target_bir_lowering=False, num_devices=1)
    sent, args = {}, []
    for name, v in arrays.items():
        v = np.ascontiguousarray(v)
        sent[name] = v
        args.append(nc.dram_tensor(name, v.shape, mybir.dt.from_np(v.dtype), kind="ExternalInput").ap())
    args.append(nc.dram_tensor("out", (n, d), F32, kind="ExternalOutput").ap())
    build(nc, *args)
    r = run_bass_kernel_spmd(nc, [sent], core_ids=[0])
    return r.results[0]["out"]
```

```python
from contextlib import ExitStack

import concourse.bass as bass
from concourse import mybir

ALU = mybir.AluOpType
ACT = mybir.ActivationFunctionType
AX = mybir.AxisListType
F32 = mybir.dt.float32
BF16 = mybir.dt.bfloat16
F16 = mybir.dt.float16
F8 = mybir.dt.float8e4
I32 = mybir.dt.int32
U32 = mybir.dt.uint32
U8 = mybir.dt.uint8
RMAX = bass.bass_isa.ReduceOp.max
ds = bass.ds

P = 128
F8_ONE = 56
EPS = 1e-5
SHIFT = 64.0
S_X = 4096.0
S_W = 256.0
S_H = 64.0
S_E = 16.0
NEVER = 2.0 ** 100


class Steps:

    def __init__(self, eng, sem, base=0):
        self.eng, self.sem, self.base, self.n = eng, sem, base, 0

    def then(self, ins):
        ins.then_inc(self.sem, 1)
        self.n += 1

    def wait(self):
        self.eng.wait_ge(self.sem, self.base + self.n)


def over(ap, shape, axis):
    return ap.unsqueeze(axis).to_broadcast(shape)


def build(nc, x, adj_t, g0_w, g0_b, g0_a, gate_w, gate_b, w1, w2, w3, g1_wt, g1_b,
          router_wt, router_b, f_w1, f_b1, f_w2, f_b2, out):
    N, D = x.shape
    NB = N // P
    E0, _, H0 = w1.shape
    E1 = router_wt.shape[1]
    H1 = f_w1.shape[1] // E1
    HC0 = H0 // P
    TOP = 2
    TILES = N * TOP // P + E0
    ROWS = TILES * P
    EH1 = E1 * H1
    KC1 = EH1 // P
    V3 = 3 * (D + 1)
    V2 = 2 * D + 1
    PART = D + 1

    HALF_ROW = D // 2
    ROW = D + 2
    NOWHERE = TOP * N
    sorted_x = nc.dram_tensor("sorted_x", (ROWS, ROW), F32).ap()
    expert_rows = nc.dram_tensor("expert_rows", (TOP * N, D), F32).ap()

    with ExitStack() as whole:
        def sb(name, shape, dt, ctx=whole):
            return ctx.enter_context(nc.sbuf_tensor(name, shape, dt))

        def ps(name, shape, dt, ctx=whole):
            return ctx.enter_context(nc.psum_tensor(name, shape, dt))

        def sem(name):
            return whole.enter_context(nc.semaphore(name))

        equal_one = sb("equal_one", [P, NB, N], U8)
        xs = sb("xs", [P, NB, D], F32)
        ident = sb("ident", [P, P], F32)
        ident16 = sb("ident16", [P, P], F16)
        stats = sb("stats", [P, NB, 6], F32)
        mean = sb("mean", [P, NB], F32)
        rstd = sb("rstd", [P, NB], F32)
        tmp = [sb(f"tmp{i}", [P, NB], F32) for i in range(4)]
        pos = sb("pos", [P, TOP, NB], U32)
        gates = sb("gates", [P, TOP, NB], F32)
        row_ids = sb("row_ids", [P, TOP, NB], U32)
        tile_at = sb("tile_at", [1, TILES], I32)

        def inverse_root(dve, v, r, var, root, t, twice):
            v.then(dve.reciprocal(t, root))
            v.wait()
            v.then(dve.tensor_tensor(t, t, var, ALU.mult))
            v.wait()
            v.then(dve.tensor_tensor(t, t, root, ALU.add))
            v.wait()
            v.then(dve.reciprocal(r, t))
            v.wait()
            v.then(dve.tensor_scalar(r, r, twice, None, ALU.mult))

        def moments(dve, v, blocks):
            c = blocks
            v.wait()
            v.then(dve.tensor_tensor(mean[:, c], stats[:, c, 1], stats[:, c, 4], ALU.add))
            v.then(dve.tensor_tensor(tmp[2][:, c], stats[:, c, 1], stats[:, c, 4], ALU.subtract))
            v.then(dve.tensor_tensor(tmp[3][:, c], stats[:, c, 2], stats[:, c, 5], ALU.add))
            v.wait()
            v.then(dve.tensor_scalar(mean[:, c], mean[:, c], 0.5, None, ALU.mult))
            v.then(dve.tensor_tensor(tmp[2][:, c], tmp[2][:, c], tmp[2][:, c], ALU.mult))
            v.wait()
            v.then(dve.scalar_tensor_tensor(out=tmp[3][:, c], in0=tmp[2][:, c], scalar=D / 4.0, in1=tmp[3][:, c],
                                            op0=ALU.mult, op1=ALU.add))

        def row_norms(dve, v, var_ready, root_ready, arrived=None):
            for c in range(NB):
                if arrived and c % (NB // 4) == 0:
                    dve.wait_ge(arrived[c // (NB // 4)], 16)
                v.then(dve.bn_stats(stats[:, c, :], xs[:, c, :]))
            moments(dve, v, slice(0, NB))
            v.wait()
            dve.tensor_scalar(tmp[0][:, :], tmp[3][:, :], 1.0 / D, EPS, ALU.mult, ALU.add).then_inc(var_ready, 1)
            dve.wait_ge(root_ready, 1)
            inverse_root(dve, v, rstd[:, :], tmp[0][:, :], tmp[1][:, :], tmp[2][:, :], 2.0)
            v.wait()

        attend_ctx = ExitStack()
        parts = sb("parts", [P, NB, V3], BF16, attend_ctx)
        with ExitStack() as ctx:
            G = 4
            w_sb = sb("w_sb", [P, D], F32, ctx)
            b_bc = sb("b_bc", [P, D], F32, ctx)
            a_bc = sb("a_bc", [P, D], F32, ctx)
            zeros = sb("zeros", [P, ROW], F32, ctx)
            xn = sb("xn", [P, 2, G, D], F32, ctx)
            xnt = sb("xnt", [P, 2, G * P], F32, ctx)
            h = sb("h", [P, 2, G, D], F32, ctx)
            ha = sb("ha", [P, G, D], F32, ctx)
            values = sb("values", [P, NB, PART], F32, ctx)
            score = sb("score", [P, NB], F32, ctx)
            hsum = sb("hsum", [P, NB], F32, ctx)
            top = sb("top", [P, 2], F32, ctx)
            ps_t = ps("ps_t", [P, 2, G * P], F32, ctx)
            ps_v = ps("ps_v", [P, 2, G * D], F32, ctx)

            x_in = [sem(f"x_in{i}") for i in range(4)]
            w_in, zeroed, cleared = sem("w_in"), sem("zeroed"), sem("cleared")
            ids_ready, ids_zero = sem("ids_ready"), sem("ids_zero")
            v_a, var_ready, root_ready = sem("v_a"), sem("var_ready"), sem("root_ready")
            xn_ready, xt_ready, xt_copied = sem("xn_ready"), sem("xt_ready"), sem("xt_copied")
            val_ready, val_copied, hb_ready, h_ready = sem("val_ready"), sem("val_copied"), sem("hb_ready"), sem("h_ready")
            h_free = sem("h_free")
            local_top, all_top, weight_ready, high_ready, mid_ready = sem("local_top"), sem("all_top"), sem("weight_ready"), sem("high_ready"), sem("mid_ready")
            bias_ready = sem("bias_ready")

            with nc.Block() as block:
                @block.sync
                def _(sp):
                    q = NB // 4
                    for i in range(4):
                        sp.dma_start(xs[:, i * q:(i + 1) * q, :],
                                     x[i * q * P:(i + 1) * q * P, :].rearrange("(c p) d -> p c d", p=P)).then_inc(x_in[i], 16)

                @block.gpsimd
                def _(pool):
                    pool.memset(ident[:, :], 0.0).then_inc(ids_zero, 1)
                    pool.wait_ge(ids_zero, 1)
                    pool.affine_select(out=ident[:, :], in_=ident[:, :], compare_op=ALU.not_equal, fill=1.0,
                                       base=0, pattern=[[-1, P]], channel_multiplier=1).then_inc(ids_ready, 1)
                    pool.wait_ge(ids_ready, 1)
                    pool.tensor_copy(ident16[:, :], ident[:, :]).then_inc(ids_ready, 1)
                    pool.wait_ge(local_top, 1)
                    pool.partition_all_reduce(top[:, 1:2], top[:, 0:1], P, RMAX).then_inc(all_top, 1)

                @block.scalar
                def _(act):
                    act.dma_start(w_sb[:, :], g0_w).then_inc(w_in, 16)
                    act.dma_start(b_bc[:, :], g0_b.partition_broadcast(P)).then_inc(w_in, 16)
                    act.dma_start(a_bc[:, :], g0_a.rearrange("d a -> (a d)").partition_broadcast(P)).then_inc(w_in, 16)
                    act.wait_ge(zeroed, 2)
                    act.dma_start(sorted_x.rearrange("(t p) d -> p t d", p=P),
                                  over(zeros[:, :], [P, TILES, ROW], 1)).then_inc(cleared, 16)
                    act.wait_ge(var_ready, 1)
                    act.activation(tmp[1][:, :], tmp[0][:, :], ACT.Sqrt).then_inc(root_ready, 1)
                    with act.Fori(0, NB // G // 2) as i:
                        for k in range(2):
                            g = i * 2 + k
                            act.wait_ge(xt_ready, g + 1)
                            act.activation(xnt[:, k, :], ps_t[:, k, :], ACT.Copy).then_inc(xt_copied, 1)
                            act.wait_ge(val_ready, g + 1)
                            act.activation(values[:, ds(g * G, G), 0:D],
                                           ps_v[:, k, :].rearrange("p (c d) -> p c d", c=G), ACT.Copy).then_inc(val_copied, 1)
                            act.wait_ge(hb_ready, g + 1)
                            act.activation(h[:, k, :, :], h[:, k, :, :], ACT.Tanh).then_inc(h_ready, 1)
                    act.wait_ge(bias_ready, 1)
                    act.activation(values[:, :, D], score[:, :], ACT.Exp, bias=top[:, 0:1]).then_inc(weight_ready, 1)
                    act.wait_ge(high_ready, 1)
                    act.activation(parts[:, :, 0:PART], values[:, :, :], ACT.Copy).then_inc(high_ready, 1)
                    act.wait_ge(mid_ready, 1)
                    act.activation(parts[:, :, PART:2 * PART], values[:, :, :], ACT.Copy).then_inc(mid_ready, 1)
                    act.wait_ge(cleared, 16)

                @block.tensor
                def _(pe):
                    pe.wait_ge(w_in, 48)
                    pe.wait_ge(ids_ready, 2)
                    with pe.Fori(0, NB // G // 2) as i:
                        for k in range(2):
                            g = i * 2 + k
                            pe.wait_ge(xn_ready, g + 1)
                            for c in range(G):
                                t = pe.transpose(ps_t[:, k, c * P:(c + 1) * P], xn[:, k, c, :], ident[:, :])
                            t.then_inc(xt_ready, 1)
                            pe.wait_ge(xt_copied, g + 1)
                            for c in range(G):
                                m = pe.matmul(ps_v[:, k, c * D:(c + 1) * D], xnt[:, k, c * P:(c + 1) * P], w_sb[:, :],
                                              start=True, stop=True)
                            m.then_inc(val_ready, 1)

                @block.vector
                def _(dve):
                    v = Steps(dve, v_a)
                    dve.memset(zeros[:, :], 0.0).then_inc(zeroed, 1)
                    dve.wait_ge(zeroed, 1)
                    dve.memset(zeros[:, D:D + 1].bitcast(U32), NOWHERE).then_inc(zeroed, 1)
                    row_norms(dve, v, var_ready, root_ready, x_in)
                    base = v.n

                    dve.wait_ge(w_in, 48)
                    STEPS = 1
                    with dve.Fori(0, NB // G // 2) as i:
                        for k in range(2):
                            g = i * 2 + k
                            for c in range(G):
                                n = dve.tensor_scalar(xn[:, k, c, :], xs[:, ds(g * G + c, 1), :].rearrange("p a d -> p (a d)"),
                                                      mean[:, ds(g * G + c, 1)], rstd[:, ds(g * G + c, 1)],
                                                      ALU.subtract, ALU.mult)
                            n.then_inc(xn_ready, 1)
                            dve.wait_ge(val_copied, g + 1)
                            dve.tensor_tensor(h[:, k, :, :], values[:, ds(g * G, G), 0:D],
                                              over(b_bc[:, :], [P, G, D], 1), ALU.add).then_inc(hb_ready, 1)
                            dve.wait_ge(h_ready, g + 1)
                            dve.tensor_tensor(ha[:, :, :], h[:, k, :, :], over(a_bc[:, :], [P, G, D], 1), ALU.mult)\
                               .then_inc(v_a, 1)
                            dve.tensor_reduce(hsum[:, ds(g * G, G)], h[:, k, :, :], AX.X, ALU.add)
                            dve.wait_ge(v_a, g * STEPS + (base + 1))
                            dve.tensor_reduce(score[:, ds(g * G, G)], ha[:, :, :], AX.X, ALU.add).then_inc(h_free, 1)
                    v.n = base + NB // G
                    dve.wait_ge(h_free, NB // G)
                    dve.tensor_reduce(top[:, 0:1], score[:, :], AX.X, ALU.max).then_inc(local_top, 1)
                    dve.wait_ge(all_top, 1)
                    dve.tensor_scalar(top[:, 0:1], top[:, 1:2], -1.0, SHIFT, ALU.mult, ALU.add).then_inc(bias_ready, 1)
                    dve.wait_ge(weight_ready, 1)
                    v.then(dve.tensor_scalar(hsum[:, :], hsum[:, :], 0.0, None, ALU.not_equal))
                    v.wait()
                    v.then(dve.tensor_tensor(values[:, :, D], values[:, :, D], hsum[:, :], ALU.mult))
                    v.wait()
                    dve.wait_ge(val_copied, NB // G)
                    dve.tensor_tensor(values[:, :, 0:D], values[:, :, 0:D],
                                      values[:, :, D:PART].to_broadcast([P, NB, D]), ALU.mult).then_inc(high_ready, 1)
                    dve.wait_ge(high_ready, 2)
                    dve.tensor_tensor(values[:, :, :], values[:, :, :], parts[:, :, 0:PART], ALU.subtract).then_inc(mid_ready, 1)
                    dve.wait_ge(mid_ready, 2)
                    dve.tensor_tensor(parts[:, :, 2 * PART:V3], values[:, :, :], parts[:, :, PART:2 * PART], ALU.subtract)

        with ExitStack() as ctx:
            HALF = NB * P // 2
            NST = 3
            stage = [sb(f"stage{i}", [P, HALF], I32, ctx) for i in range(NST)]
            mask = [sb(f"mask{i}", [P, NB * P], U8, ctx) for i in range(2)]
            agg = sb("agg", [P, 2, PART], F32, ctx)
            inv = sb("inv", [P, 2], F32, ctx)
            ps_a = ps("ps_a", [P, 2, 512], F32, ctx)

            adj_in = [sem(f"adj_in{i}") for i in range(NST)]
            adj_used, mask_ready, agg_ready, agg_free, v_b = sem("adj_used"), sem("mask_ready"), sem("agg_ready"), sem("agg_free"), sem("v_b")
            UN = 6
            NH = 2 * NB
            with nc.Block() as block:
                def load(sp, half, s, wait):
                    if wait is not None:
                        sp.wait_ge(adj_used, wait)
                    sp.dma_start(stage[s][:, :], adj_t[ds(half, 1), :, :].rearrange("a p n -> p (a n)")).then_inc(adj_in[s], 16)

                @block.sync
                def _(sp):
                    for j in range(NST):
                        load(sp, j, j % NST, None)
                    with sp.Fori(0, NH // NST - 1) as i:
                        for s in range(NST):
                            load(sp, i * NST + (s + NST), s, i * NST + (s + 1))
                    for j in range(NH // NST * NST, NH):
                        load(sp, j, j % NST, j - NST + 1)

                @block.tensor
                def _(pe):
                    with pe.Fori(0, NB // 2) as i:
                        for k in range(2):
                            b = i * 2 + k
                            pe.wait_ge(mask_ready, b * 2 + 2)
                            pe.wait_ge(agg_free, b + 1)
                            pe.ldweights(ident16[:, :], tile_position=(0, 0))
                            for c in range(NB):
                                m = pe.matmul(ps_a[:, k, 0:V3], mask[k][:, c * P:(c + 1) * P].bitcast(F8), parts[:, c, :],
                                              start=(c == 0), stop=(c == NB - 1))
                            m.then_inc(agg_ready, 1)

                @block.vector
                def _(dve):
                    dve.sem_inc(agg_free, 2)

                    def masks(half, s, k, part, in_loop_round):
                        dve.wait_ge(adj_in[s], in_loop_round)
                        m = mask[k][:, part * HALF:(part + 1) * HALF]
                        dve.tensor_scalar(m, stage[s][:, :], 0, F8_ONE, ALU.is_gt, ALU.mult).then_inc(mask_ready, 1)
                        dve.tensor_scalar(equal_one[:, :, :].rearrange("p b n -> p (b n)")[:, ds(half * HALF, HALF)],
                                          stage[s][:, :], 1, F8_ONE, ALU.is_equal, ALU.mult).then_inc(adj_used, 1)

                    def finish(b, k, n):
                        dve.wait_ge(agg_ready, b + 1)
                        dve.tensor_reduce(agg[:, k, :], ps_a[:, k, 0:V3].rearrange("p (t f) -> p f t", t=3), AX.X, ALU.add)\
                           .then_inc(agg_free, 1)
                        dve.wait_ge(agg_free, b + 3)
                        dve.tensor_scalar(inv[:, k:k + 1], agg[:, k, D:PART], 1e-30, None, ALU.max).then_inc(v_b, 1)
                        dve.wait_ge(v_b, b * 2 + 1)
                        dve.reciprocal(inv[:, k:k + 1], inv[:, k:k + 1]).then_inc(v_b, 1)
                        dve.wait_ge(v_b, b * 2 + 2)
                        row = xs[:, ds(b, 1), :].rearrange("p a d -> p (a d)")
                        dve.scalar_tensor_tensor(out=row, in0=agg[:, k, 0:D], scalar=inv[:, k:k + 1], in1=row,
                                                 op0=ALU.mult, op1=ALU.add)

                    def halves(b, base_round, h0):
                        raise NotImplementedError

                    def body(b0, rounds, nblocks, first):
                        for j in range(nblocks):
                            for part in range(2):
                                hh = 2 * j + part
                                if part == 0 and not (first and j < 2):
                                    dve.wait_ge(agg_ready, b0 + (j - 1))
                                masks(b0 * 2 + hh, hh % NST, j % 2, part, rounds + 16 * (hh // NST + 1))
                            if not (first and j == 0):
                                finish(b0 + (j - 1), (j - 1) % 2, j)

                    body(0, 0, 6, True)
                    with dve.Fori(1, NB // 6) as i:
                        body(i * 6, i * 64, 6, False)
                    body(NB // 6 * 6, NB // 6 * 64, NB % 6, False)
                    finish(NB - 1, (NB - 1) % 2, 0)

                @block.gpsimd
                def _(pool):
                    pool.wait_ge(agg_ready, NB)

                @block.scalar
                def _(act):
                    act.wait_ge(agg_ready, NB)
        attend_ctx.close()

        with ExitStack() as ctx:
            G = 4
            TOPK_LOW = -3e38
            before = sb("before", [P, P], BF16, ctx)
            ones16 = sb("ones16", [P, P], BF16, ctx)
            xn = sb("xn_rows", [P, NB, D], F32, ctx)
            xnt = sb("xnt_r", [P, 2, G * P], F32, ctx)
            gw = sb("gw", [P, E0], F32, ctx)
            gb = sb("gb", [P, E0], F32, ctx)
            falling = sb("falling", [P, E0], F32, ctx)
            tile_edge = sb("tile_edge", [P, NB], F32, ctx)
            tile_no = sb("tile_no", [1, TILES], F32, ctx)
            logit = sb("logit", [P, NB, E0], F32, ctx)
            pick = sb("pick", [P, NB, E0], F32, ctx)
            hot = [sb(f"hot{k}", [P, NB, E0], F32, ctx) for k in range(TOP)]
            both = sb("both", [P, E0, NB], BF16, ctx)
            keep = sb("keep", [P, E0, NB], F32, ctx)
            upto = sb("upto", [P, E0, NB], F32, ctx)
            place = sb("place", [P, E0, NB], F32, ctx)
            best = [sb(f"best{k}", [P, NB], F32, ctx) for k in range(TOP)]
            which = sb("which", [P, NB], F32, ctx)
            over_edge = sb("over_edge", [P, E0, NB], F32, ctx)
            ntiles = sb("ntiles", [P, E0], F32, ctx)
            ones_e = sb("ones_e", [P, E0], F32, ctx)
            cum = sb("cum", [P, E0], F32, ctx)
            first_row = sb("first_row", [P, E0], F32, ctx)
            past = sb("past", [1, TILES, E0], F32, ctx)
            texp = sb("texp", [1, TILES], F32, ctx)
            ps_t = ps("ps_t2", [P, 2, G * P], F32, ctx)
            ps_l = ps("ps_l", [P, NB * E0], F32, ctx)
            ps_rank = ps("ps_rank", [P, E0 * NB], F32, ctx)
            ps_count = ps("ps_count", [P, E0 * NB], F32, ctx)

            v_c, var_ready, root_ready = sem("v_c"), sem("var_ready2"), sem("root_ready2")
            gate_in, xn_ready, xt_ready, xt_copied = sem("gate_in"), sem("xn_ready2"), sem("xt_ready2"), sem("xt_copied2")
            iotas, logit_ready, gap_ready, ratio_ready = sem("iotas"), sem("logit_ready"), sem("gap_ready"), sem("ratio_ready")
            both_ready, count_ready = sem("both_ready"), sem("count_ready")
            with nc.Block() as block:
                @block.sync
                def _(sp):
                    sp.dma_start(gw[:, :], gate_w).then_inc(gate_in, 16)
                    sp.dma_start(gb[:, :], gate_b.partition_broadcast(P)).then_inc(gate_in, 16)

                @block.gpsimd
                def _(pool):
                    exact = dict(allow_small_or_imprecise_dtypes=True)
                    pool.iota(falling[:, :], pattern=[[-1, E0]], base=E0, channel_multiplier=0, **exact).then_inc(iotas, 1)
                    pool.iota(tile_edge[:, :], pattern=[[P, NB]], base=0, channel_multiplier=0, **exact).then_inc(iotas, 1)
                    pool.iota(tile_no[:, :], pattern=[[1, TILES]], base=0, channel_multiplier=0, **exact).then_inc(iotas, 1)
                    pool.memset(keep[:, :, :], 1.0).then_inc(iotas, 1)
                    pool.memset(ones_e[:, :], 1.0).then_inc(iotas, 1)
                    pool.wait_ge(iotas, 5)
                    pool.memset(keep[:, :, 0:1], 0.0).then_inc(iotas, 1)
                    pool.memset(before[:, :], 1.0).then_inc(iotas, 1)
                    pool.memset(ones16[:, :], 1.0).then_inc(iotas, 1)
                    pool.wait_ge(iotas, 8)
                    pool.affine_select(out=before[:, :], in_=before[:, :], compare_op=ALU.is_gt, fill=0.0,
                                       base=0, pattern=[[1, P]], channel_multiplier=-1).then_inc(iotas, 1)
                    pool.iota(row_ids[:, :, :].rearrange("p k b -> p (k b)"), pattern=[[P, TOP * NB]], base=0,
                              channel_multiplier=1).then_inc(iotas, 1)
                    pool.wait_ge(iotas, 10)

                @block.scalar
                def _(act):
                    act.wait_ge(var_ready, 1)
                    act.activation(tmp[1][:, :], tmp[0][:, :], ACT.Sqrt).then_inc(root_ready, 1)
                    with act.Fori(0, NB // G // 2) as i:
                        for k in range(2):
                            act.wait_ge(xt_ready, i * 2 + (k + 1))
                            act.activation(xnt[:, k, :], ps_t[:, k, :], ACT.Copy).then_inc(xt_copied, 1)
                    act.wait_ge(gap_ready, 1)
                    act.activation(gates[:, 1, :], tmp[0][:, :], ACT.Exp).then_inc(ratio_ready, 1)

                @block.tensor
                def _(pe):
                    pe.wait_ge(gate_in, 32)
                    for g in range(NB // G):
                        k = g % 2
                        pe.wait_ge(xn_ready, g + 1)
                        for c in range(G):
                            t = pe.transpose(ps_t[:, k, c * P:(c + 1) * P], xn[:, g * G + c, :], ident[:, :])
                        t.then_inc(xt_ready, 1)
                        pe.wait_ge(xt_copied, g + 1)
                        for c in range(G):
                            b = g * G + c
                            m = pe.matmul(ps_l[:, b * E0:(b + 1) * E0], xnt[:, k, c * P:(c + 1) * P], gw[:, :],
                                          start=True, stop=True)
                        m.then_inc(logit_ready, 1)
                    pe.wait_ge(iotas, 10)
                    pe.wait_ge(both_ready, 1)
                    rhs = both[:, :, :].rearrange("p e b -> p (e b)")
                    pe.matmul(ps_rank[:, :], before[:, :], rhs, start=True, stop=True)
                    pe.matmul(ps_count[:, :], ones16[:, :], rhs, start=True, stop=True).then_inc(count_ready, 1)

                @block.vector
                def _(dve):
                    v = Steps(dve, v_c)
                    row_norms(dve, v, var_ready, root_ready)
                    with dve.Fori(0, NB // G) as g:
                        for c in range(G):
                            b = g * G + c
                            n = dve.tensor_scalar(xn[:, ds(b, 1), :].rearrange("p a d -> p (a d)"),
                                                  xs[:, ds(b, 1), :].rearrange("p a d -> p (a d)"),
                                                  mean[:, ds(b, 1)], rstd[:, ds(b, 1)], ALU.subtract, ALU.mult)
                        n.then_inc(xn_ready, 1)
                    S3 = [P, NB, E0]
                    dve.wait_ge(iotas, 10)
                    dve.wait_ge(gate_in, 32)
                    dve.wait_ge(logit_ready, NB // G)
                    v.then(dve.tensor_tensor(logit[:, :, :], ps_l[:, :].rearrange("p (b e) -> p b e", e=E0),
                                             over(gb[:, :], S3, 1), ALU.add))
                    v.wait()
                    for k in range(TOP):
                        v.then(dve.tensor_reduce(best[k][:, :], logit[:, :, :], AX.X, ALU.max))
                        v.wait()
                        v.then(dve.tensor_tensor(pick[:, :, :], logit[:, :, :], over(best[k][:, :], S3, 2), ALU.is_ge))
                        v.wait()
                        v.then(dve.tensor_tensor(pick[:, :, :], pick[:, :, :], over(falling[:, :], S3, 1), ALU.mult))
                        v.wait()
                        v.then(dve.tensor_reduce(which[:, :], pick[:, :, :], AX.X, ALU.max))
                        v.wait()
                        v.then(dve.tensor_tensor(hot[k][:, :, :], over(falling[:, :], S3, 1), over(which[:, :], S3, 2), ALU.is_equal))
                        v.wait()
                        if k == 0:
                            v.then(dve.scalar_tensor_tensor(out=logit[:, :, :], in0=hot[0][:, :, :], scalar=TOPK_LOW,
                                                            in1=logit[:, :, :], op0=ALU.mult, op1=ALU.add))
                            v.wait()
                    dve.tensor_tensor(both[:, :, :].rearrange("p e b -> p b e"), hot[0][:, :, :], hot[1][:, :, :], ALU.add)\
                       .then_inc(both_ready, 1)
                    dve.tensor_tensor(tmp[0][:, :], best[1][:, :], best[0][:, :], ALU.subtract).then_inc(gap_ready, 1)
                    dve.wait_ge(ratio_ready, 1)
                    v.then(dve.tensor_scalar(tmp[1][:, :], gates[:, 1, :], 1.0, None, ALU.add))
                    v.wait()
                    v.then(dve.reciprocal(gates[:, 0, :], tmp[1][:, :]))
                    v.wait()
                    v.then(dve.tensor_tensor(gates[:, 1, :], gates[:, 1, :], gates[:, 0, :], ALU.mult))
                    dve.wait_ge(count_ready, 1)
                    v.then(dve.tensor_tensor_scan(upto[:, :, :].rearrange("p e b -> p (e b)"), keep[:, :, :].rearrange("p e b -> p (e b)"),
                                                  ps_count[:, :], 0.0, ALU.mult, ALU.add))
                    v.wait()
                    v.then(dve.tensor_tensor(over_edge[:, :, :], upto[:, :, NB - 1:NB].to_broadcast([P, E0, NB]),
                                             over(tile_edge[:, :], [P, E0, NB], 1), ALU.is_gt))
                    v.wait()
                    v.then(dve.tensor_reduce(ntiles[:, :], over_edge[:, :, :], AX.X, ALU.add))
                    v.then(dve.tensor_tensor(place[:, :, :].rearrange("p e b -> p (e b)"), upto[:, :, :].rearrange("p e b -> p (e b)"),
                                             ps_count[:, :], ALU.subtract))
                    v.wait()
                    v.then(dve.tensor_tensor_scan(cum[:, :], ones_e[:, :], ntiles[:, :], 0.0, ALU.mult, ALU.add))
                    v.wait()
                    v.then(dve.tensor_tensor(first_row[:, :], cum[:, :], ntiles[:, :], ALU.subtract))
                    v.wait()
                    v.then(dve.tensor_scalar(first_row[:, :], first_row[:, :], float(P), None, ALU.mult))
                    v.then(dve.tensor_tensor(place[:, :, :].rearrange("p e b -> p (e b)"), place[:, :, :].rearrange("p e b -> p (e b)"),
                                             ps_rank[:, :], ALU.add))
                    v.wait()
                    v.then(dve.tensor_tensor(place[:, :, :], place[:, :, :], over(first_row[:, :], [P, E0, NB], 2), ALU.add))
                    v.wait()
                    for k in range(TOP):
                        v.then(dve.tensor_tensor(pick[:, :, :], hot[k][:, :, :], place[:, :, :].rearrange("p e b -> p b e"), ALU.mult))
                        v.wait()
                        v.then(dve.tensor_reduce(best[k][:, :], pick[:, :, :], AX.X, ALU.add))
                        v.wait()
                        v.then(dve.tensor_copy(pos[:, k, :], best[k][:, :]))
                    S = [1, TILES, E0]
                    v.then(dve.tensor_tensor(past[:, :, :], over(tile_no[:, :], S, 2), over(cum[0:1, :], S, 1), ALU.is_ge))
                    v.wait()
                    v.then(dve.tensor_reduce(texp[:, :], past[:, :, :], AX.X, ALU.add))
                    v.wait()
                    v.then(dve.tensor_scalar(texp[:, :], texp[:, :], float(E0 - 1), None, ALU.min))
                    v.wait()
                    v.then(dve.tensor_scalar(tile_at[:, :], texp[:, :], float(2 * HC0 * D), None, ALU.mult))
                    v.then(dve.tensor_scalar(rstd[:, :], rstd[:, :], S_X, None, ALU.mult))
                    v.wait()

        expert_ctx = ExitStack()
        w12 = sb("w12", [P, E0, 2, 2 * H0], F16, expert_ctx)
        w3s = sb("w3s", [P, E0, 2, HC0 * D], F16, expert_ctx)
        with ExitStack() as ctx:
            R = 4
            normed = sb("normed", [P, D], F32, ctx)
            row = sb("row", [P, R, TOP, ROW], F32, ctx)
            raw12 = sb("raw12", [P, 2, 2 * H0], F32, ctx)
            raw3 = sb("raw3", [P, 2, HC0 * D], F32, ctx)
            raw_in = [sem(f"raw_in{i}") for i in range(2)]
            high_made, low_made = sem("high_made"), sem("low_made")
            n_ready, pair_ready, rows_ready = sem("n_ready"), sem("pair_ready"), sem("rows_ready")
            scattered = [sem(f"scattered{i}") for i in range(R)]
            with nc.Block() as block:
                @block.sync
                def _(sp):
                    for e in range(E0):
                        if e >= 2:
                            sp.wait_ge(low_made, 2 * (e - 1))
                        sp.dma_start(raw12[:, e % 2, 0:H0], w1[e, :, :]).then_inc(raw_in[e % 2], 16)
                        sp.dma_start(raw12[:, e % 2, H0:2 * H0], w2[e, :, :]).then_inc(raw_in[e % 2], 16)
                        sp.dma_start(raw3[:, e % 2, :].rearrange("p (c o) -> p c o", c=HC0),
                                     w3[e, :, :].rearrange("(c p) o -> p c o", p=P)).then_inc(raw_in[e % 2], 16)

                @block.gpsimd
                def _(pool):
                    for c in range(NB):
                        pool.wait_ge(rows_ready, c + 1)
                        pool.wait_ge(pair_ready, c * 3 + 3)
                        for k in range(TOP):
                            pool.indirect_dma_start(out=sorted_x, out_offset=bass.IndirectOffsetOnAxis(ap=pos[:, k, c:c + 1], axis=0),
                                                    in_=row[:, c % R, k, :], in_offset=None).then_inc(scattered[c % R], 16)
                    for r in range(R):
                        pool.wait_ge(scattered[r], 16 * TOP * NB // R)

                @block.scalar
                def _(act):
                    for c in range(NB):
                        act.wait_ge(pair_ready, c * 3 + 1)
                        act.activation(row[:, c % R, 1, 0:D].bitcast(F16), row[:, c % R, 0, 0:D].bitcast(F16), ACT.Copy).then_inc(rows_ready, 1)
                        if c % 2 == 0:
                            e = c // 2
                            act.wait_ge(raw_in[e % 2], 48 * (e // 2 + 1))
                            act.activation(w12[:, e, 0, :], raw12[:, e % 2, :], ACT.Copy, scale=S_W).then_inc(high_made, 1)
                            act.activation(w3s[:, e, 0, :], raw3[:, e % 2, :], ACT.Copy, scale=S_W).then_inc(high_made, 1)

                @block.vector
                def _(dve):
                    for c in range(NB):
                        if c >= 1:
                            dve.wait_ge(pair_ready, c * 3 - 2)
                        dve.tensor_scalar(normed[:, :], xs[:, c, :], mean[:, c:c + 1], rstd[:, c:c + 1],
                                          ALU.subtract, ALU.mult).then_inc(n_ready, 1)
                        if c >= R:
                            dve.wait_ge(scattered[c % R], 16 * TOP * (c // R))
                        dve.tensor_scalar(row[:, c % R, 0, 0:HALF_ROW].bitcast(F16), xs[:, c, :], mean[:, c:c + 1], rstd[:, c:c + 1],
                                          ALU.subtract, ALU.mult).then_inc(n_ready, 1)
                        dve.wait_ge(n_ready, c * 2 + 2)
                        dve.tensor_tensor(row[:, c % R, 0, HALF_ROW:D].bitcast(F16), normed[:, :], row[:, c % R, 0, 0:HALF_ROW].bitcast(F16), ALU.subtract)\
                           .then_inc(pair_ready, 1)
                        dve.tensor_copy(row[:, c % R, :, D:D + 1].bitcast(U32), row_ids[:, :, c:c + 1]).then_inc(pair_ready, 1)
                        dve.tensor_copy(row[:, c % R, :, D + 1:ROW], gates[:, :, c:c + 1]).then_inc(pair_ready, 1)
                        if c % 2 == 0:
                            e = c // 2
                            dve.wait_ge(high_made, 2 * e + 1)
                            dve.scalar_tensor_tensor(out=w12[:, e, 1, :], in0=raw12[:, e % 2, :], scalar=S_W, in1=w12[:, e, 0, :],
                                                     op0=ALU.mult, op1=ALU.subtract).then_inc(low_made, 1)
                            dve.wait_ge(high_made, 2 * e + 2)
                            dve.scalar_tensor_tensor(out=w3s[:, e, 1, :], in0=raw3[:, e % 2, :], scalar=S_W, in1=w3s[:, e, 0, :],
                                                     op0=ALU.mult, op1=ALU.subtract).then_inc(low_made, 1)

        with ExitStack() as ctx:
            UN = 8
            HP = 4
            xt = sb("xt", [P, UN, ROW], F32, ctx)
            xT = sb("xT", [P, 2, 2, P], F16, ctx)
            hid = sb("hid", [P, 2, HC0 * P], F32, ctx)
            hT = sb("hT", [P, HP, 2, HC0 * P], F16, ctx)
            y = sb("y", [P, 2, D], F32, ctx)
            ps_x = ps("ps_x", [P, 2, 2 * 512], F16, ctx)
            ps_h = ps("ps_h", [P, 2, 512], F32, ctx)
            ps_y = ps("ps_y", [P, 2, 512], F32, ctx)
            row_in = [sem(f"row_in{i}") for i in range(UN)]
            stored = [sem(f"stored{i}") for i in range(2)]
            tx_ready, x_copied, h_ready, gated, hid_ready = sem("tx_ready"), sem("x_copied"), sem("h_ready_e"), sem("gated"), sem("hid_ready")
            high_ready, hp_ready, y_ready, y_scaled = sem("high_ready_e"), sem("hp_ready_e"), sem("y_ready"), sem("y_scaled")
            w12f = w12[:, :, :, :].rearrange("p e t n -> p (e t n)")
            w3f = w3s[:, :, :, :].rearrange("p e t n -> p (e t n)")
            THREE = ((0, 0), (0, 1), (1, 0))
            LAST = TILES + 3
            assert TILES % UN == 0

            def in_steps(eng, step):
                for s in range(UN):
                    step(s, s, s)
                with eng.Fori(1, TILES // UN) as i:
                    for j in range(UN):
                        step(i * UN + j, j, None)
                for s in range(TILES, LAST):
                    step(s, s % UN, s)

            def runs(known, lag):
                return known is None or 0 <= known - lag < TILES

            def has(known, lag, before):
                return known is None or known - lag >= before

            with nc.Block() as block:
                @block.sync
                def _(sp):
                    def load(s, j, known):
                        if not runs(known, 0):
                            return
                        if known is None:
                            sp.wait_ge(stored[j % 2], (s - j) * 8 - 16 * (UN // 2) + 16 * (j // 2 + 1))
                        sp.dma_start(xt[:, j, :], sorted_x.rearrange("(t p) d -> t p d", p=P)[ds(s, 1), :, :]
                                     .rearrange("t p d -> p (t d)")).then_inc(row_in[j], 16)
                    in_steps(sp, load)

                @block.gpsimd
                def _(pool):
                    for t in range(TILES):
                        pool.wait_ge(y_scaled, t + 1)
                        pool.indirect_dma_start(out=expert_rows, out_offset=bass.IndirectOffsetOnAxis(ap=xt[:, t % UN, D:D + 1].bitcast(U32), axis=0),
                                                in_=y[:, t % 2, :], in_offset=None, bounds_check=TOP * N - 1, oob_is_err=False).then_inc(stored[t % 2], 16)
                    pool.wait_ge(stored[0], TILES // 2 * 16)
                    pool.wait_ge(stored[1], TILES // 2 * 16)

                @block.scalar
                def _(act):
                    def step(s, j, known):
                        if runs(known, 0):
                            k = j % 2
                            act.wait_ge(tx_ready, s + 1)
                            if has(known, 0, 2):
                                act.wait_ge(h_ready, s - 1)
                            act.activation(xT[:, k, :, :], ps_x[:, k, 0:2 * P], ACT.Copy).then_inc(x_copied, 1)
                        if runs(known, 1):
                            k = (j - 1) % 2
                            act.wait_ge(h_ready, s)
                            if has(known, 1, 2):
                                act.wait_ge(hp_ready, s - 2)
                            act.activation(hid[:, k, :], ps_h[:, k, 0:H0], ACT.Silu, scale=1.0 / (S_X * S_W)).then_inc(gated, 1)
                        if runs(known, 2):
                            k = (j - 2) % 2
                            act.wait_ge(hid_ready, s - 1)
                            if has(known, 2, HP):
                                act.wait_ge(y_ready, s - (HP + 1))
                            act.activation(hT[:, (j - 2) % HP, 0, :], hid[:, k, :], ACT.Copy).then_inc(high_ready, 1)
                    in_steps(act, step)

                @block.tensor
                def _(pe):
                    BACK = 4
                    at = {}

                    def load_places(first, n, tile0):
                        regs = [pe.alloc_register(f"expert_at_{n}_{m}") for m in range(n)]
                        pe.load(regs, tile_at[0:1, ds(first, n)])
                        at.clear()
                        for m in range(n):
                            at[tile0 + m] = pe.snap(regs[m], donate=True, min_val=0, max_val=(E0 - 1) * 2 * HC0 * D)

                    def row_round(s, j, known):
                        return (known // UN + 1) * 16 if known is not None else (s - j) * (16 // UN) + 16

                    def step(s, j, known):
                        if runs(known, 0):
                            pe.wait_ge(row_in[j], row_round(s, j, known))
                            if has(known, 0, 2):
                                pe.wait_ge(x_copied, s - 1)
                            for a in range(2):
                                t = pe.transpose(ps_x[:, j % 2, a * P:(a + 1) * P], xt[:, j, a * HALF_ROW:(a + 1) * HALF_ROW].bitcast(F16), ident16[:, :])
                            t.then_inc(tx_ready, 1)
                        if runs(known, 1):
                            k = (j - 1) % 2
                            off = at[j - 1] * 2
                            pe.wait_ge(x_copied, s)
                            if has(known, 1, 2):
                                pe.wait_ge(hid_ready, s - 2)
                            for c in range(2 * HC0):
                                for a, b in THREE:
                                    m = pe.matmul(ps_h[:, k, c * P:(c + 1) * P], w12f[:, ds(off + (a * 2 * H0 + c * P), P)], xT[:, k, b, :],
                                                  start=(a + b == 0), stop=(a == 1))
                            m.then_inc(h_ready, 1)
                        if runs(known, 3):
                            k = (j - 3) % 2
                            off = at[j - 3]
                            pe.wait_ge(hp_ready, s - 2)
                            if has(known, 3, 2):
                                pe.wait_ge(y_scaled, s - 4)
                            for c in range(HC0):
                                for a, b in THREE:
                                    m = pe.matmul(ps_y[:, k, 0:D], hT[:, (j - 3) % HP, a, c * P:(c + 1) * P],
                                                  w3f[:, ds(off + (b * HC0 * D + c * D), D)],
                                                  start=(c + a + b == 0), stop=(c + a == HC0))
                            m.then_inc(y_ready, 1)
                    for s in range(UN):
                        if s == 0:
                            load_places(0, UN, 0)
                        step(s, s, s)
                    with pe.Fori(1, TILES // UN) as i:
                        load_places(i * UN - BACK, BACK + UN, -BACK)
                        for j in range(UN):
                            step(i * UN + j, j, None)
                    load_places(TILES - BACK, BACK, -BACK)
                    for s in range(TILES, LAST):
                        step(s, s % UN, s)

                @block.vector
                def _(dve):
                    def step(s, j, known):
                        if runs(known, 1):
                            k = (j - 1) % 2
                            dve.wait_ge(gated, s)
                            dve.scalar_tensor_tensor(out=hid[:, k, :], in0=ps_h[:, k, H0:2 * H0], scalar=S_E / (S_X * S_W),
                                                     in1=hid[:, k, :], op0=ALU.mult, op1=ALU.mult).then_inc(hid_ready, 1)
                        if runs(known, 2):
                            dve.wait_ge(high_ready, s - 1)
                            dve.tensor_tensor(hT[:, (j - 2) % HP, 1, :], hid[:, (j - 2) % 2, :], hT[:, (j - 2) % HP, 0, :], ALU.subtract)\
                               .then_inc(hp_ready, 1)
                        if runs(known, 3):
                            k = (j - 3) % 2
                            dve.wait_ge(y_ready, s - 2)
                            if has(known, 3, 2):
                                dve.wait_ge(stored[k], stored_upto(s, j, known))
                            dve.tensor_scalar(y[:, k, :], ps_y[:, k, 0:D], xt[:, (j - 3) % UN, D + 1:ROW],
                                              1.0 / (S_W * S_E), ALU.mult, ALU.mult).then_inc(y_scaled, 1)

                    def stored_upto(s, j, known):
                        if known is not None:
                            return (known - 3) // 2 * 16
                        return (s - j) * 8 + (j - 3) // 2 * 16
                    in_steps(dve, step)
        expert_ctx.close()

        mean_ctx = ExitStack()
        parts2 = sb("parts2", [P, NB, V2], F16, mean_ctx)
        mask = sb("mask2", [P, 2, NB * P], U8, mean_ctx)
        wide = {"wt": (P, D), "rt": (P, E1), "f1": (P, EH1), "f2": (P, KC1 * D), "b2": (E1, D)}
        source = {"wt": g1_wt, "rt": router_wt, "f1": f_w1, "f2": f_w2, "b2": f_b2}
        scales = {"wt": S_W, "rt": S_W, "f1": S_W, "f2": S_W, "b2": S_W * S_H}
        raw = {n: sb("raw_" + n, [r, c], F32, mean_ctx) for n, (r, c) in wide.items()}
        two = {n: sb("two_" + n, [r, 2, c], F16, mean_ctx) for n, (r, c) in wide.items()}
        rb = sb("rb", [P, E1], F32, mean_ctx)
        fb1 = sb("fb1", [P, KC1], F32, mean_ctx)
        never = sb("never", [E1, KC1, P], BF16, mean_ctx)
        falling1 = sb("falling1", [P, E1], F32, mean_ctx)
        mask_copied = sem("mask_copied")
        with ExitStack() as ctx:
            CK = 4
            NC = NB // CK
            NR = 2
            HALVES = 2
            rows = sb("rows", [P, NR, TOP, CK, D], F32, ctx)
            xn = sb("xn_c", [P, 2, CK, D], F32, ctx)
            wb = sb("wb", [P, D], F32, ctx)
            shift = sb("shift", [P, NB], F32, ctx)
            gathered = [sem(f"gathered{i}") for i in range(NR)]
            v_d, added, var_ready, root_ready = sem("v_d"), sem("added"), sem("var_ready3"), sem("root_ready3")
            norm_ready, xn_ready, high_ready, low_ready = sem("norm_ready3"), sem("xn_ready3"), sem("high_ready3"), sem("low_ready3")
            bias_in, w_in, const_ready = sem("bias_in"), sem("m_w_in"), sem("m_const_ready")
            weight_high, scaled, ones_made = sem("m_weight_high"), sem("m_scaled"), sem("ones_made")
            W = len(wide)
            with nc.Block() as block:
                @block.sync
                def _(sp):
                    def load(q):
                        for k in range(TOP):
                            lo = k * N + q * CK * P
                            sp.dma_start(rows[:, q % NR, k, :, :],
                                         expert_rows[lo:lo + CK * P, :].rearrange("(c p) d -> p c d", p=P)).then_inc(gathered[q % NR], 16)
                    for q in range(NR):
                        load(q)
                    sp.dma_start(wb[:, :], g1_b.partition_broadcast(P)).then_inc(bias_in, 16)
                    for q in range(NR, NC):
                        sp.wait_ge(added, TOP * (q - NR + 1))
                        load(q)
                    for n in wide:
                        sp.dma_start(raw[n][:, :], source[n]).then_inc(w_in, 16)
                    sp.dma_start(rb[:, :], router_b.partition_broadcast(P)).then_inc(w_in, 16)
                    sp.dma_start(fb1[:, :], f_b1).then_inc(w_in, 16)

                @block.gpsimd
                def _(pool):
                    exact = dict(allow_small_or_imprecise_dtypes=True)
                    flat = never[:, :, :].rearrange("e k p -> e (k p)")
                    pool.memset(parts2[:, :, 2 * D:V2], 1.0).then_inc(ones_made, 1)
                    pool.iota(falling1[:, :], pattern=[[-1, E1]], base=E1, channel_multiplier=0, **exact).then_inc(const_ready, 1)
                    pool.wait_ge(const_ready, 1)
                    pool.memset(flat, NEVER).then_inc(const_ready, 1)
                    pool.wait_ge(const_ready, 2)
                    pool.affine_select(out=flat, in_=flat, compare_op=ALU.is_ge, fill=0.0, base=0,
                                       pattern=[[1, EH1]], channel_multiplier=-H1).then_inc(const_ready, 1)
                    pool.wait_ge(const_ready, 3)
                    pool.affine_select(out=flat, in_=flat, compare_op=ALU.is_gt, fill=0.0, base=H1,
                                       pattern=[[-1, EH1]], channel_multiplier=H1).then_inc(const_ready, 1)
                    pool.wait_ge(const_ready, 4)
                    for u in range(2):
                        pool.tensor_copy(mask[:, u, :].bitcast(F32), equal_one[:, u, :].bitcast(F32)).then_inc(mask_copied, 1)
                    pool.wait_ge(bias_in, 16)
                    for q in range(NC):
                        c = slice(q * CK, (q + 1) * CK)
                        pool.wait_ge(xn_ready, q + 1)
                        pool.tensor_tensor(xs[:, c, :], xs[:, c, :], over(wb[:, :], [P, CK, D], 1), ALU.add)

                @block.scalar
                def _(act):
                    for half in range(HALVES):
                        h = slice(half * NB // 2, (half + 1) * NB // 2)
                        act.wait_ge(var_ready, half + 1)
                        act.activation(tmp[1][:, h], tmp[0][:, h], ACT.Sqrt).then_inc(root_ready, 1)
                        act.wait_ge(norm_ready, half + 1)
                        for q in range(half * NC // 2, (half + 1) * NC // 2):
                            if q >= 2:
                                act.wait_ge(low_ready, q - 1)
                            for c in range(CK):
                                b = q * CK + c
                                n = act.activation(xn[:, q % 2, c, :], xs[:, b, :], ACT.Identity, scale=rstd[:, b:b + 1], bias=shift[:, b:b + 1])
                            n.then_inc(xn_ready, 1)
                            act.wait_ge(xn_ready, q + 1)
                            act.activation(parts2[:, q * CK:(q + 1) * CK, 0:D], xn[:, q % 2, :, :], ACT.Copy).then_inc(high_ready, 1)
                    act.wait_ge(w_in, 16 * (W + 2))
                    for n in wide:
                        act.activation(two[n][:, 0, :], raw[n][:, :], ACT.Copy, scale=scales[n]).then_inc(weight_high, 1)
                    act.activation(fb1[:, :], fb1[:, :], ACT.Copy, scale=S_H)

                @block.vector
                def _(dve):
                    v = Steps(dve, v_d)

                    def add_chunk(q):
                        c = slice(q * CK, (q + 1) * CK)
                        dve.wait_ge(gathered[q % NR], 16 * TOP * (q // NR + 1))
                        for k in range(TOP):
                            if k > 0:
                                dve.wait_ge(added, TOP * q + k)
                            dve.tensor_tensor(xs[:, c, :], xs[:, c, :], rows[:, q % NR, k, :, :], ALU.add).then_inc(added, 1)

                    def chunk_stats(q):
                        dve.wait_ge(added, TOP * (q + 1))
                        for c in range(q * CK, (q + 1) * CK):
                            v.then(dve.bn_stats(stats[:, c, :], xs[:, c, :]))

                    def low_part(q):
                        c = slice(q * CK, (q + 1) * CK)
                        dve.wait_ge(high_ready, q + 1)
                        dve.tensor_tensor(parts2[:, c, D:2 * D], xn[:, q % 2, :, :], parts2[:, c, 0:D], ALU.subtract).then_inc(low_ready, 1)

                    def half_norm(half):
                        h = slice(half * NB // 2, (half + 1) * NB // 2)
                        moments(dve, v, h)
                        v.wait()
                        dve.tensor_scalar(tmp[0][:, h], tmp[3][:, h], 1.0 / D, EPS, ALU.mult, ALU.add).then_inc(var_ready, 1)
                        dve.wait_ge(root_ready, half + 1)
                        inverse_root(dve, v, rstd[:, h], tmp[0][:, h], tmp[1][:, h], tmp[2][:, h], 2.0 * S_X)
                        v.wait()
                        dve.scalar_tensor_tensor(out=shift[:, h], in0=mean[:, h], scalar=-1.0, in1=rstd[:, h],
                                                 op0=ALU.mult, op1=ALU.mult).then_inc(norm_ready, 1)

                    add_chunk(0)
                    for q in range(1, NC):
                        add_chunk(q)
                        chunk_stats(q - 1)
                        if q == NC // 2:
                            half_norm(0)
                        if q > NC // 2:
                            low_part(q - NC // 2 - 1)
                    chunk_stats(NC - 1)
                    half_norm(1)
                    for q in range(NC // 2 - 1, NC):
                        low_part(q)
                    for j, n in enumerate(wide):
                        dve.wait_ge(weight_high, j + 1)
                        dve.scalar_tensor_tensor(out=two[n][:, 1, :], in0=raw[n][:, :], scalar=scales[n], in1=two[n][:, 0, :],
                                                 op0=ALU.mult, op1=ALU.subtract)

        with ExitStack() as ctx:
            total = sb("total", [P, D], F32, ctx)
            expert_out = sb("expert_out", [P, D], F32, ctx)
            inv = sb("inv2", [P, 2], F32, ctx)
            agg = sb("agg2", [P, 2, 2, D], F16, ctx)
            aggt = sb("aggt", [P, 2, 2, P], F16, ctx)
            xc = sb("xc", [P, D], F32, ctx)
            squares = sb("squares", [P, D], F32, ctx)
            sq = sb("sq", [P, 6], F32, ctx)
            xn = sb("xn3", [P, 2, 2, D], F16, ctx)
            xnt = sb("xnt3", [P, 2, 2, P], F16, ctx)
            lg = sb("lg", [P, E1], F32, ctx)
            best1 = sb("best_logit", [P, 1], F32, ctx)
            which1 = sb("which1", [P, 1], F32, ctx)
            others = sb("others", [P, E1], F16, ctx)
            others_t = sb("others_t", [E1, P], BF16, ctx)
            hot_t = sb("hot_t", [E1, P], F16, ctx)
            hm = raw["f1"][:, :].rearrange("p (c n) -> p c n", c=KC1)
            hp = sb("hp", [P, 2, KC1, P], F16, ctx)
            fin = sb("fin", [P, 2, D], F32, ctx)
            ps_a = ps("ps_a2", [P, 2, 512], F32, ctx)
            ps_f = ps("ps_f", [P, 2, 512], F32, ctx)
            ps_t = ps("ps_t3", [P, 2, P], F16, ctx)
            ps_w = ps("ps_w", [P, 512], F32, ctx)
            ps_i = ps("ps_i", [P, 4 * P], F16, ctx)
            ps_o = ps("ps_o", [P, 512], F32, ctx)
            names = "agg_ready agg_read norm_ready at_ready at_copied wx_ready var_ready root_ready " \
                    "xn_ready xt_ready xt_copied lg_ready lg_read others_ready ot_ready hot_ready f_ready relu_ready high_ready " \
                    "hp_ready o_half o_read fin_ready".split()
            (agg_ready, agg_read, norm_ready, at_ready, at_copied, wx_ready, var_ready, root_ready,
             xn_ready, xt_ready, xt_copied, lg_ready, lg_read, others_ready, ot_ready, hot_ready, f_ready, relu_ready, high_ready,
             hp_ready, o_half, o_read, fin_ready) = [sem("m_" + n) for n in names]
            own_e = sem("own_e")
            own = {n: sem("own_" + n) for n in "abc"}
            stored = [sem(f"stored_m{i}") for i in range(2)]
            LAST = NB + 3
            CH = KC1 // 2

            def in_steps(eng, step):
                for u in range(4):
                    step(u, u % 2, u)
                with eng.Fori(2, NB // 2) as i:
                    for k in range(2):
                        step(i * 2 + k, k, None)
                for u in range(NB, LAST):
                    step(u, u % 2, u)

            def runs(known, lag):
                return known is None or 0 <= known - lag < NB

            def has(known, lag, before):
                return known is None or known - lag >= before

            with nc.Block() as block:
                @block.sync
                def _(sp):
                    def step(u, k, known):
                        if runs(known, 3):
                            sp.wait_ge(fin_ready, u - 2)
                            sp.dma_start(out.rearrange("(b p) d -> b p d", p=P)[ds(u - 3, 1), :, :].rearrange("b p d -> p (b d)"),
                                         fin[:, 1 - k, :]).then_inc(stored[1 - k], 16)
                    in_steps(sp, step)
                    sp.wait_ge(stored[0], NB // 2 * 16)
                    sp.wait_ge(stored[1], NB // 2 * 16)

                @block.gpsimd
                def _(pool):
                    def step(u, k, known):
                        if runs(known, 0) and known not in (0, 1):
                            pool.wait_ge(agg_ready, u - 1)
                            pool.tensor_copy(mask[:, k, :].bitcast(F32), equal_one[:, ds(u, 1), :].rearrange("p b n -> p (b n)").bitcast(F32))\
                                .then_inc(mask_copied, 1)
                    in_steps(pool, step)

                @block.scalar
                def _(act):
                    def step(u, k, known):
                        o = 1 - k

                        def relus(half, n):
                            act.wait_ge(f_ready, n)
                            for c in range(half * CH, (half + 1) * CH):
                                r = act.activation(hm[:, c, :], ps_f[:, half, (c - half * CH) * P:(c - half * CH + 1) * P],
                                                   ACT.Relu, bias=fb1[:, c:c + 1], scale=S_H / (S_X * S_W))
                            r.then_inc(relu_ready, 1)
                            act.wait_ge(relu_ready, n)
                            act.activation(hp[:, 0, half * CH:(half + 1) * CH, :], hm[:, half * CH:(half + 1) * CH, :], ACT.Copy)\
                               .then_inc(high_ready, 1)
                        if runs(known, 2):
                            act.wait_ge(xt_ready, u - 1)
                            act.activation(xnt[:, k, :, :], ps_i[:, 0:2 * P], ACT.Copy).then_inc(xt_copied, 1)
                        if runs(known, 1):
                            act.wait_ge(at_ready, u)
                            act.activation(aggt[:, o, :, :], ps_t[:, :, :], ACT.Copy).then_inc(at_copied, 1)
                        if runs(known, 3):
                            if has(known, 3, 1):
                                act.wait_ge(hp_ready, u * 2 - 6)
                                act.wait_ge(o_half, u * 2 - 6)
                            relus(1, u * 2 - 4)
                        if runs(known, 2):
                            act.wait_ge(ot_ready, u - 1)
                            act.activation(others_t[:, :], ps_i[0:E1, 2 * P:3 * P], ACT.Copy).then_inc(hot_ready, 1)
                            act.activation(hot_t[:, :], ps_i[0:E1, 2 * P:3 * P], ACT.Copy, bias=1.0).then_inc(hot_ready, 1)
                        if runs(known, 1):
                            act.wait_ge(var_ready, u)
                            act.activation(sq[:, 1:2], sq[:, 0:1], ACT.Sqrt).then_inc(root_ready, 1)
                        if runs(known, 2):
                            if has(known, 2, 1):
                                act.wait_ge(hp_ready, u * 2 - 5)
                                act.wait_ge(o_half, u * 2 - 5)
                            relus(0, u * 2 - 3)
                    in_steps(act, step)

                @block.tensor
                def _(pe):
                    THREE = ((0, 0), (0, 1), (1, 0))

                    def step(u, k, known):
                        o = 1 - k

                        def products(lo, hi):
                            if not runs(known, 0):
                                return
                            if lo == 0:
                                pe.wait_ge(mask_copied, u + 1)
                                if has(known, 0, 2):
                                    pe.wait_ge(agg_read, u * 2 - 2)
                            pe.ldweights(ident16[:, :], tile_position=(0, 0))
                            for c in range(lo, hi):
                                m = pe.matmul(ps_a[:, k, 0:V2], mask[:, k, c * P:(c + 1) * P].bitcast(F8), parts2[:, c, :],
                                              start=(c == 0), stop=(c == NB - 1))
                            if hi == NB:
                                m.then_inc(agg_ready, 1)

                        def second(half):
                            if half == 0:
                                for b in range(2):
                                    pe.matmul(ps_o[:, 0:D], hot_t[:, :], two["b2"][:, b, :], start=(b == 0), stop=False)
                            pe.wait_ge(hp_ready, u * 2 - 5 + half)
                            for c in range(half * CH, (half + 1) * CH):
                                for a, b in THREE:
                                    m = pe.matmul(ps_o[:, 0:D], hp[:, a, c, :], two["f2"][:, b, c * D:(c + 1) * D],
                                                  start=False, stop=(c + a == KC1))
                            m.then_inc(o_half, 1)

                        q = NB // 8
                        products(0, 2 * q)
                        if runs(known, 2):
                            pe.wait_ge(xn_ready, u - 1)
                            for a in range(2):
                                t = pe.transpose(ps_i[:, a * P:(a + 1) * P], xn[:, k, a, :], ident16[:, :])
                            t.then_inc(xt_ready, 1)
                        products(2 * q, 4 * q)
                        if runs(known, 1):
                            pe.wait_ge(norm_ready, u)
                            for a in range(2):
                                t = pe.transpose(ps_t[:, a, :], agg[:, o, a, :], ident16[:, :])
                            t.then_inc(at_ready, 1)
                        if runs(known, 2):
                            pe.wait_ge(xt_copied, u - 1)
                            for a, b in THREE:
                                m = pe.matmul(ps_w[:, D:D + E1], xnt[:, k, a, :], two["rt"][:, b, :], start=(a + b == 0), stop=(a == 1))
                            m.then_inc(lg_ready, 1)
                        if runs(known, 3):
                            if has(known, 3, 1):
                                pe.wait_ge(o_read, u - 3)
                            second(0)
                        if runs(known, 1):
                            pe.wait_ge(at_copied, u)
                            if runs(known, 2):
                                pe.wait_ge(lg_read, u - 1)
                            for a, b in THREE:
                                m = pe.matmul(ps_w[:, 0:D], aggt[:, o, a, :], two["wt"][:, b, :], start=(a + b == 0), stop=(a == 1))
                            m.then_inc(wx_ready, 1)
                        products(4 * q, 5 * q)
                        if runs(known, 2):
                            pe.wait_ge(others_ready, u - 1)
                            pe.transpose(ps_i[0:E1, 2 * P:3 * P], others[:, :], ident16[:, :]).then_inc(ot_ready, 1)
                        products(5 * q, 7 * q)
                        if runs(known, 2):
                            pe.wait_ge(hot_ready, u * 2 - 2)
                            if has(known, 2, 1):
                                pe.wait_ge(relu_ready, u * 2 - 4)
                            for c in range(KC1):
                                to = ps_f[:, c // CH, c % CH * P:(c % CH + 1) * P]
                                for a, b in THREE:
                                    pe.matmul(to, two["f1"][:, a, c * P:(c + 1) * P], xnt[:, k, b, :], start=(a + b == 0), stop=False)
                                m = pe.matmul(to, never[:, c, :], others_t[:, :], start=False, stop=True)
                                if c % CH == CH - 1:
                                    m.then_inc(f_ready, 1)
                        if runs(known, 3):
                            second(1)
                        products(7 * q, 8 * q)
                    in_steps(pe, step)

                @block.vector
                def _(dve):
                    def step(u, k, known):
                        o = 1 - k
                        if runs(known, 1):
                            dve.wait_ge(agg_ready, u)
                            dve.reciprocal(inv[:, o:o + 1], ps_a[:, o, 2 * D:V2]).then_inc(agg_read, 1)
                            dve.tensor_reduce(total[:, :], ps_a[:, o, 0:2 * D].rearrange("p (t f) -> p f t", t=2), AX.X, ALU.add)\
                               .then_inc(agg_read, 1)
                            dve.wait_ge(agg_read, u * 2)
                            dve.tensor_scalar(agg[:, o, 0, :], total[:, :], inv[:, o:o + 1], None, ALU.mult).then_inc(own["a"], 1)
                            dve.wait_ge(own["a"], u)
                            dve.scalar_tensor_tensor(out=agg[:, o, 1, :], in0=total[:, :], scalar=inv[:, o:o + 1], in1=agg[:, o, 0, :],
                                                     op0=ALU.mult, op1=ALU.subtract).then_inc(norm_ready, 1)
                        def low_part(half):
                            c = slice(half * CH, (half + 1) * CH)
                            dve.wait_ge(high_ready, u * 2 - 5 + half)
                            dve.tensor_tensor(hp[:, 1, c, :], hm[:, c, :], hp[:, 0, c, :], ALU.subtract).then_inc(hp_ready, 1)

                        if runs(known, 3):
                            low_part(0)
                        if runs(known, 2):
                            dve.wait_ge(lg_ready, u - 1)
                            dve.scalar_tensor_tensor(out=lg[:, :], in0=ps_w[:, D:D + E1], scalar=1.0 / (S_X * S_W), in1=rb[:, :],
                                                     op0=ALU.mult, op1=ALU.add).then_inc(lg_read, 1)
                            dve.wait_ge(lg_read, u - 1)
                            dve.tensor_reduce(best1[:, :], lg[:, :], AX.X, ALU.max).then_inc(own["b"], 1)
                            dve.wait_ge(own["b"], u * 3 - 5)
                            dve.scalar_tensor_tensor(out=lg[:, :], in0=lg[:, :], scalar=best1[:, :], in1=falling1[:, :],
                                                     op0=ALU.is_ge, op1=ALU.mult).then_inc(own["b"], 1)
                            dve.wait_ge(own["b"], u * 3 - 4)
                            dve.tensor_reduce(which1[:, :], lg[:, :], AX.X, ALU.max).then_inc(own["b"], 1)
                            dve.wait_ge(own["b"], u * 3 - 3)
                            dve.tensor_scalar(others[:, :], falling1[:, :], which1[:, :], 1.0, ALU.is_equal, ALU.subtract)\
                               .then_inc(others_ready, 1)
                        if runs(known, 1):
                            row = xs[:, ds(u - 1, 1), :].rearrange("p a d -> p (a d)")
                            C = 7
                            at = lambda n: u * C - (C - n)
                            dve.wait_ge(wx_ready, u)
                            dve.scalar_tensor_tensor(out=row, in0=ps_w[:, 0:D], scalar=1.0 / (S_X * S_W), in1=row, op0=ALU.mult,
                                                     op1=ALU.add, accum_out=sq[:, 4:5]).then_inc(own["c"], 1)
                            dve.wait_ge(own["c"], at(1))
                            dve.tensor_scalar(sq[:, 5:6], sq[:, 4:5], -1.0 / D, None, ALU.mult).then_inc(own["c"], 1)
                            dve.wait_ge(own["c"], at(2))
                            dve.tensor_scalar(xc[:, :], row, sq[:, 5:6], None, ALU.add).then_inc(own["c"], 1)
                            dve.wait_ge(own["c"], at(3))
                            dve.scalar_tensor_tensor(out=squares[:, :], in0=xc[:, :], scalar=1.0, in1=xc[:, :], op0=ALU.mult,
                                                     op1=ALU.mult, accum_out=sq[:, 4:5]).then_inc(own["c"], 1)
                            dve.wait_ge(own["c"], at(4))
                            dve.tensor_scalar(sq[:, 0:1], sq[:, 4:5], 1.0 / D, EPS, ALU.mult, ALU.add).then_inc(var_ready, 1)
                        if runs(known, 3):
                            low_part(1)
                        if runs(known, 1):
                            dve.wait_ge(root_ready, u)
                            dve.reciprocal(sq[:, 2:3], sq[:, 1:2]).then_inc(own["c"], 1)
                            dve.wait_ge(own["c"], at(5))
                            dve.tensor_scalar(sq[:, 2:3], sq[:, 0:1], sq[:, 2:3], sq[:, 1:2], ALU.mult, ALU.add).then_inc(own["c"], 1)
                            dve.wait_ge(own["c"], at(6))
                            dve.reciprocal(sq[:, 3:4], sq[:, 2:3]).then_inc(own["c"], 1)
                            dve.wait_ge(own["c"], at(7))
                            dve.tensor_scalar(xn[:, o, 0, :], xc[:, :], sq[:, 3:4], 2.0 * S_X, ALU.mult, ALU.mult).then_inc(own_e, 1)
                            dve.tensor_scalar(xc[:, :], xc[:, :], sq[:, 3:4], 2.0 * S_X, ALU.mult, ALU.mult).then_inc(own_e, 1)
                            dve.wait_ge(own_e, u * 2)
                            dve.tensor_tensor(xn[:, o, 1, :], xc[:, :], xn[:, o, 0, :], ALU.subtract).then_inc(xn_ready, 1)
                        if runs(known, 3):
                            dve.wait_ge(o_half, u * 2 - 4)
                            if has(known, 3, 2):
                                dve.wait_ge(stored[o], stored_upto(u, k, known))
                            dve.tensor_scalar(expert_out[:, :], ps_o[:, 0:D], 0.0, 1.0 / (S_W * S_H), ALU.max, ALU.mult).then_inc(o_read, 1)
                            dve.wait_ge(o_read, u - 2)
                            dve.tensor_tensor(fin[:, o, :], expert_out[:, :], xs[:, ds(u - 3, 1), :].rearrange("p a d -> p (a d)"), ALU.add)\
                               .then_inc(fin_ready, 1)

                    def stored_upto(u, k, known):
                        if known is not None:
                            return (known - 3) // 2 * 16
                        return (u - k) * 8 + (k - 3) // 2 * 16
                    in_steps(dve, step)
        mean_ctx.close()


def kernel(**inputs):
    import numpy as np
    import concourse.bacc as bacc
    from concourse.bass_utils import run_bass_kernel_spmd

    a = {k: np.asarray(v) for k, v in inputs.items()}
    n = a["x"].shape[0]
    nb = n // 128
    adj = a["adj"].reshape(nb, 128, 2, nb // 2, 128).transpose(0, 2, 4, 3, 1).reshape(2 * nb, 128, nb // 2 * 128)
    e1, d, h1 = a["L1_ffn_W1"].shape
    arrays = {
        "x": a["x"],
        "adj_t": adj,
        "g0_w": a["L0_gnn_W"], "g0_b": a["L0_gnn_b"], "g0_a": a["L0_gnn_a"],
        "gate_w": a["L0_ffn_gate_w"], "gate_b": a["L0_ffn_gate_b"],
        "w1": a["L0_ffn_w1"], "w2": a["L0_ffn_w2"], "w3": a["L0_ffn_w3"],
        "g1_wt": a["L1_gnn_W"].T, "g1_b": a["L1_gnn_b"],
        "router_wt": a["L1_ffn_router_w"].T, "router_b": a["L1_ffn_router_b"],
        "f_w1": a["L1_ffn_W1"].transpose(1, 0, 2).reshape(d, e1 * h1), "f_b1": a["L1_ffn_b1"].reshape(-1, 128).T, "f_w2": a["L1_ffn_W2"].reshape(-1, 128, d).transpose(1, 0, 2).reshape(128, -1), "f_b2": a["L1_ffn_b2"],
    }
    nc = bacc.Bacc("TRN2", target_bir_lowering=False, num_devices=1)
    sent, args = {}, []
    for name, v in arrays.items():
        v = np.ascontiguousarray(v)
        sent[name] = v
        args.append(nc.dram_tensor(name, v.shape, mybir.dt.from_np(v.dtype), kind="ExternalInput").ap())
    args.append(nc.dram_tensor("out", (n, d), F32, kind="ExternalOutput").ap())
    build(nc, *args)
    r = run_bass_kernel_spmd(nc, [sent], core_ids=[0])
    return r.results[0]["out"]
```

```python
from contextlib import ExitStack

import concourse.bass as bass
from concourse import mybir

ALU = mybir.AluOpType
ACT = mybir.ActivationFunctionType
AX = mybir.AxisListType
F32 = mybir.dt.float32
BF16 = mybir.dt.bfloat16
F16 = mybir.dt.float16
F8 = mybir.dt.float8e4
I32 = mybir.dt.int32
U32 = mybir.dt.uint32
U8 = mybir.dt.uint8
RMAX = bass.bass_isa.ReduceOp.max
ds = bass.ds

P = 128
F8_ONE = 56
EPS = 1e-5
SHIFT = 64.0
S_X = 4096.0
S_W = 256.0
S_H = 64.0
S_E = 16.0
WARM_UP = 64
NEVER = 2.0 ** 100


class Steps:

    def __init__(self, eng, sem, base=0):
        self.eng, self.sem, self.base, self.n = eng, sem, base, 0

    def then(self, ins):
        ins.then_inc(self.sem, 1)
        self.n += 1

    def wait(self):
        self.eng.wait_ge(self.sem, self.base + self.n)


def over(ap, shape, axis):
    return ap.unsqueeze(axis).to_broadcast(shape)


def build(nc, x, adj_t, g0_w, g0_b, g0_a, gate_w, gate_b, w1, w2, w3, g1_wt, g1_b,
          router_wt, router_b, f_w1, f_b1, f_w2, f_b2, out):
    N, D = x.shape
    NB = N // P
    E0, _, H0 = w1.shape
    E1 = router_wt.shape[1]
    H1 = f_w1.shape[1] // E1
    HC0 = H0 // P
    TOP = 2
    HT = 2
    T = HT * P
    TILES = N * TOP // T + E0
    CAP = N + T
    SPARE = E0 * CAP
    EH1 = E1 * H1
    KC1 = EH1 // P
    V3 = 3 * (D + 1)
    V2 = 2 * D + 1
    PART = D + 1

    HALF_ROW = D // 2
    ROW = D + 2
    NOWHERE = TOP * N
    sorted_x = nc.dram_tensor("sorted_x", (SPARE + T, ROW), F32).ap()
    expert_rows = nc.dram_tensor("expert_rows", (TOP * N, D), F32).ap()

    with ExitStack() as whole:
        def sb(name, shape, dt, ctx=whole):
            return ctx.enter_context(nc.sbuf_tensor(name, shape, dt))

        def ps(name, shape, dt, ctx=whole):
            return ctx.enter_context(nc.psum_tensor(name, shape, dt))

        def sem(name):
            return whole.enter_context(nc.semaphore(name))

        equal_one = sb("equal_one", [P, NB, N], U8)
        xs = sb("xs", [P, NB, D], F32)
        ident = sb("ident", [P, P], F32)
        ident16 = sb("ident16", [P, P], F16)
        mean = sb("mean", [P, NB], F32)
        rstd = sb("rstd", [P, NB], F32)
        tmp = [sb(f"tmp{i}", [P, NB], F32) for i in range(4)]
        tile_row = sb("tile_row", [1, TILES], I32)
        end_row = sb("end_row", [1, E0], I32)
        tile_at = sb("tile_at", [1, TILES], I32)

        def inverse_root(dve, v, r, var, root, t, twice):
            v.then(dve.reciprocal(t, root))
            v.wait()
            v.then(dve.tensor_tensor(t, t, var, ALU.mult))
            v.wait()
            v.then(dve.tensor_tensor(t, t, root, ALU.add))
            v.wait()
            v.then(dve.reciprocal(r, t))
            v.wait()
            v.then(dve.tensor_scalar(r, r, twice, None, ALU.mult))

        def moments(dve, v, stats, blocks):
            c = blocks
            v.wait()
            v.then(dve.tensor_tensor(mean[:, c], stats[:, c, 1], stats[:, c, 4], ALU.add))
            v.then(dve.tensor_tensor(tmp[2][:, c], stats[:, c, 1], stats[:, c, 4], ALU.subtract))
            v.then(dve.tensor_tensor(tmp[3][:, c], stats[:, c, 2], stats[:, c, 5], ALU.add))
            v.wait()
            v.then(dve.tensor_scalar(mean[:, c], mean[:, c], 0.5, None, ALU.mult))
            v.then(dve.tensor_tensor(tmp[2][:, c], tmp[2][:, c], tmp[2][:, c], ALU.mult))
            v.wait()
            v.then(dve.scalar_tensor_tensor(out=tmp[3][:, c], in0=tmp[2][:, c], scalar=D / 4.0, in1=tmp[3][:, c],
                                            op0=ALU.mult, op1=ALU.add))

        GB = 4
        PIECE = NB * P // GB
        SLOTS = GB * GB
        assert SLOTS * PIECE * 4 == NB // 2 * N
        ahead = equal_one[:, NB // 2:NB, :].rearrange("p b n -> p (b n)").bitcast(I32)\
            .rearrange("p (j n) -> p j n", j=SLOTS)
        ahead_in = [sem(f"ahead_in{c}") for c in range(GB)]
        ring_ctx, attend_ctx = ExitStack(), ExitStack()
        HB = NB // 2
        ring = sb("ring", [P, HB * V3 // 2], F32, ring_ctx)
        parts = (ring[:, :].bitcast(BF16).rearrange("p (b v) -> p b v", b=HB),
                 sb("parts", [P, HB, V3], BF16, attend_ctx)[:, :, :])
        WR = 4
        EW = 2 * H0 + HC0 * D
        raw = ring[:, 0:WR * EW].rearrange("p (e n) -> p e n", e=WR)
        raw_in = [sem(f"raw_in{i}") for i in range(WR)]

        def load_weights(sp, e):
            sp.dma_start(raw[:, e % WR, 0:H0], w1[e, :, :]).then_inc(raw_in[e % WR], 16)
            sp.dma_start(raw[:, e % WR, H0:2 * H0], w2[e, :, :]).then_inc(raw_in[e % WR], 16)
            sp.dma_start(raw[:, e % WR, 2 * H0:EW].rearrange("p (c o) -> p c o", c=HC0),
                         w3[e, :, :].rearrange("(c p) o -> p c o", p=P)).then_inc(raw_in[e % WR], 16)

        with ExitStack() as ctx:
            G = 4
            NG = NB // G
            HALVES = 2
            CK = NB // 4
            w_sb = sb("w_sb", [P, D], F32, ctx)
            b_bc = sb("b_bc", [P, D], F32, ctx)
            a_bc = sb("a_bc", [P, D], F32, ctx)
            zeros = sb("zeros", [P, ROW], F32, ctx)
            shift = sb("shift_x", [P, NB], F32, ctx)
            stats = sb("stats_x", [P, NB, 6], F32, ctx)
            xn = sb("xn", [P, 2, G, D], F32, ctx)
            xnt = sb("xnt", [P, 2, G * P], F32, ctx)
            h = sb("h", [P, 2, G, D], F32, ctx)
            ha = sb("ha", [P, G, D], F32, ctx)
            values = sb("values", [P, NB, PART], F32, ctx)
            score = sb("score", [P, NB], F32, ctx)
            hsum = sb("hsum", [P, NB], F32, ctx)
            top = sb("top", [P, 2], F32, ctx)
            ps_t = ps("ps_t", [P, 2, G * P], F32, ctx)
            ps_v = ps("ps_v", [P, 2, G * D], F32, ctx)

            x_in = [sem(f"x_in{i}") for i in range(4)]
            w_in, zeroed, cleared = sem("w_in"), sem("zeroed"), sem("cleared")
            ids_ready, ids_zero = sem("ids_ready"), sem("ids_zero")
            v_a, var_ready, root_ready, norm_ready = sem("v_a"), sem("var_ready"), sem("root_ready"), sem("norm_ready")
            xn_ready, xt_ready, xt_copied = sem("xn_ready"), sem("xt_ready"), sem("xt_copied")
            val_ready, val_copied, hb_ready = sem("val_ready"), sem("val_copied"), sem("hb_ready")
            h_ready, scored = sem("h_ready"), sem("scored")
            local_top, all_top, bias_ready, weight_ready = sem("local_top"), sem("all_top"), sem("bias_ready"), sem("weight_ready")
            weighted, high_ready, rest_ready, mid_ready = sem("weighted"), sem("high_ready"), sem("rest_ready"), sem("mid_ready")

            def chunk(q):
                return slice(q * CK, (q + 1) * CK)

            def chunk_parts(q, lo, hi):
                return parts[q // 2][:, q % 2 * CK:(q % 2 + 1) * CK, lo:hi]

            with nc.Block() as block:
                @block.sync
                def _(sp):
                    q = NB // 4
                    for i in range(4):
                        sp.dma_start(xs[:, i * q:(i + 1) * q, :],
                                     x[i * q * P:(i + 1) * q * P, :].rearrange("(c p) d -> p c d", p=P)).then_inc(x_in[i], 16)
                    for j in range(SLOTS):
                        sp.dma_start(ahead[:, j, :], adj_t[j, :, :]).then_inc(ahead_in[j // GB], 16)

                @block.gpsimd
                def _(pool):
                    pool.memset(ident[:, :], 0.0).then_inc(ids_zero, 1)
                    pool.wait_ge(ids_zero, 1)
                    pool.affine_select(out=ident[:, :], in_=ident[:, :], compare_op=ALU.not_equal, fill=1.0,
                                       base=0, pattern=[[-1, P]], channel_multiplier=1).then_inc(ids_ready, 1)
                    pool.wait_ge(ids_ready, 1)
                    pool.tensor_copy(ident16[:, :], ident[:, :]).then_inc(ids_ready, 1)
                    pool.wait_ge(local_top, 1)
                    pool.partition_all_reduce(top[:, 1:2], top[:, 0:1], P, RMAX).then_inc(all_top, 1)

                @block.scalar
                def _(act):
                    act.dma_start(w_sb[:, :], g0_w).then_inc(w_in, 16)
                    act.dma_start(b_bc[:, :], g0_b.partition_broadcast(P)).then_inc(w_in, 16)
                    act.dma_start(a_bc[:, :], g0_a.rearrange("d a -> (a d)").partition_broadcast(P)).then_inc(w_in, 16)
                    act.wait_ge(zeroed, 2)
                    act.dma_start(sorted_x[SPARE:SPARE + T, :].rearrange("(h p) d -> p h d", p=P),
                                  over(zeros[:, :], [P, HT, ROW], 1)).then_inc(cleared, 16)

                    def root(half):
                        c = slice(half * NB // 2, (half + 1) * NB // 2)
                        act.wait_ge(var_ready, half + 1)
                        act.activation(tmp[1][:, c], tmp[0][:, c], ACT.Sqrt).then_inc(root_ready, 1)
                    root(0)
                    for t in range(NG + 3):
                        if t == 2:
                            root(1)
                        if t < NG:
                            act.wait_ge(norm_ready, t // (NG // HALVES) + 1)
                            if t >= 2:
                                act.wait_ge(xt_ready, t - 1)
                            for c in range(G):
                                b = t * G + c
                                n = act.activation(xn[:, t % 2, c, :], xs[:, b, :], ACT.Identity,
                                                   scale=rstd[:, b:b + 1], bias=shift[:, b:b + 1])
                            n.then_inc(xn_ready, 1)
                        g = t - 1
                        if 0 <= g < NG:
                            act.wait_ge(xt_ready, g + 1)
                            if g >= 2:
                                act.wait_ge(val_ready, g - 1)
                            act.activation(xnt[:, g % 2, :], ps_t[:, g % 2, :], ACT.Copy).then_inc(xt_copied, 1)
                        g = t - 2
                        if 0 <= g < NG:
                            act.wait_ge(val_ready, g + 1)
                            act.activation(values[:, g * G:(g + 1) * G, 0:D], ps_v[:, g % 2, :].rearrange("p (c d) -> p c d", c=G), ACT.Copy)\
                                .then_inc(val_copied, 1)
                        g = t - 3
                        if 0 <= g < NG:
                            act.wait_ge(hb_ready, g + 1)
                            act.activation(h[:, g % 2, :, :], h[:, g % 2, :, :], ACT.Tanh).then_inc(h_ready, 1)
                    act.wait_ge(bias_ready, 1)
                    act.activation(values[:, :, D], score[:, :], ACT.Exp, bias=top[:, 0:1]).then_inc(weight_ready, 1)
                    for q in range(5):
                        if q < 4:
                            act.wait_ge(weighted, q + 1)
                            act.activation(chunk_parts(q, 0, PART), values[:, chunk(q), :], ACT.Copy).then_inc(high_ready, 1)
                        if q >= 1:
                            act.wait_ge(rest_ready, q)
                            act.activation(chunk_parts(q - 1, PART, 2 * PART), values[:, chunk(q - 1), :], ACT.Copy).then_inc(mid_ready, 1)
                    act.wait_ge(cleared, 16)

                @block.tensor
                def _(pe):
                    pe.wait_ge(w_in, 48)
                    pe.wait_ge(ids_ready, 2)
                    for t in range(NG + 1):
                        if t < NG:
                            pe.wait_ge(xn_ready, t + 1)
                            if t >= 2:
                                pe.wait_ge(xt_copied, t - 1)
                            for c in range(G):
                                m = pe.transpose(ps_t[:, t % 2, c * P:(c + 1) * P], xn[:, t % 2, c, :], ident[:, :])
                            m.then_inc(xt_ready, 1)
                        g = t - 1
                        if g >= 0:
                            pe.wait_ge(xt_copied, g + 1)
                            if g >= 2:
                                pe.wait_ge(val_copied, g - 1)
                            for c in range(G):
                                m = pe.matmul(ps_v[:, g % 2, c * D:(c + 1) * D], xnt[:, g % 2, c * P:(c + 1) * P], w_sb[:, :],
                                              start=True, stop=True)
                            m.then_inc(val_ready, 1)
                    pe.wait_ge(xt_copied, NG)
                    pe.wait_ge(weighted, 3)
                    for _ in range(WARM_UP):
                        pe.matmul(ps_t[:, 0, 0:P], ident16[:, :], ident16[:, :], start=True, stop=True)

                @block.vector
                def _(dve):
                    v = Steps(dve, v_a)
                    dve.memset(zeros[:, :], 0.0).then_inc(zeroed, 1)
                    dve.wait_ge(zeroed, 1)
                    dve.memset(zeros[:, D:D + 1].bitcast(U32), NOWHERE).then_inc(zeroed, 1)
                    for half in range(HALVES):
                        c = slice(half * NB // 2, (half + 1) * NB // 2)
                        for b in range(half * NB // 2, (half + 1) * NB // 2):
                            if b % (NB // 4) == 0:
                                dve.wait_ge(x_in[b // (NB // 4)], 16)
                            v.then(dve.bn_stats(stats[:, b, :], xs[:, b, :]))
                        moments(dve, v, stats, c)
                        v.wait()
                        dve.tensor_scalar(tmp[0][:, c], tmp[3][:, c], 1.0 / D, EPS, ALU.mult, ALU.add).then_inc(var_ready, 1)
                        dve.wait_ge(root_ready, half + 1)
                        inverse_root(dve, v, rstd[:, c], tmp[0][:, c], tmp[1][:, c], tmp[2][:, c], 2.0)
                        v.wait()
                        dve.scalar_tensor_tensor(out=shift[:, c], in0=mean[:, c], scalar=-1.0, in1=rstd[:, c],
                                                 op0=ALU.mult, op1=ALU.mult).then_inc(norm_ready, 1)
                    dve.wait_ge(w_in, 48)
                    for t in range(NG + 1):
                        if t < NG:
                            dve.wait_ge(val_copied, t + 1)
                            if t >= 2:
                                dve.wait_ge(scored, (t - 1) * (G + 1))
                            dve.tensor_tensor(h[:, t % 2, :, :], values[:, t * G:(t + 1) * G, 0:D],
                                              over(b_bc[:, :], [P, G, D], 1), ALU.add).then_inc(hb_ready, 1)
                        g = t - 1
                        if g >= 0:
                            dve.wait_ge(h_ready, g + 1)
                            dve.tensor_reduce(hsum[:, g * G:(g + 1) * G], h[:, g % 2, :, :], AX.X, ALU.add).then_inc(scored, 1)
                            if g >= 1:
                                dve.wait_ge(scored, g * (G + 1))
                            for c in range(G):
                                b = g * G + c
                                dve.scalar_tensor_tensor(out=ha[:, c, :], in0=h[:, g % 2, c, :], scalar=1.0, in1=a_bc[:, :], op0=ALU.mult,
                                                         op1=ALU.mult, accum_out=score[:, b:b + 1]).then_inc(scored, 1)
                    dve.wait_ge(scored, NG * (G + 1))
                    dve.tensor_reduce(top[:, 0:1], score[:, :], AX.X, ALU.max).then_inc(local_top, 1)
                    v.then(dve.tensor_scalar(hsum[:, :], hsum[:, :], 0.0, None, ALU.not_equal))
                    dve.wait_ge(all_top, 1)
                    dve.tensor_scalar(top[:, 0:1], top[:, 1:2], -1.0, SHIFT, ALU.mult, ALU.add).then_inc(bias_ready, 1)
                    dve.wait_ge(weight_ready, 1)
                    v.wait()
                    v.then(dve.tensor_tensor(values[:, :, D], values[:, :, D], hsum[:, :], ALU.mult))
                    v.wait()
                    for q in range(4 + 3):
                        if q < 4:
                            dve.tensor_tensor(values[:, chunk(q), 0:D], values[:, chunk(q), 0:D],
                                              values[:, chunk(q), D:PART].to_broadcast([P, CK, D]), ALU.mult).then_inc(weighted, 1)
                        if 1 <= q < 5:
                            c = chunk(q - 1)
                            dve.wait_ge(high_ready, q)
                            dve.tensor_tensor(values[:, c, :], values[:, c, :], chunk_parts(q - 1, 0, PART), ALU.subtract)\
                               .then_inc(rest_ready, 1)
                        if q >= 3:
                            c = chunk(q - 3)
                            dve.wait_ge(mid_ready, q - 2)
                            dve.tensor_tensor(chunk_parts(q - 3, 2 * PART, V3), values[:, c, :], chunk_parts(q - 3, PART, 2 * PART), ALU.subtract)

        with ExitStack() as ctx:
            G = GB
            NG = NB // G
            TOPK_LOW = -3e38
            EARLY = NG // 2
            stage = sb("stage", [P, G, PIECE], I32, ctx)
            mask = [sb(f"mask{i}", [P, NB * P], U8, ctx) for i in range(2)]
            inv = sb("inv", [P, 2], F32, ctx)
            row = sb("row", [P, G, TOP, ROW], F32, ctx)
            pair = sb("pair", [P, G, 2, D], F16, ctx)
            xnt = sb("xnt_r", [P, G * 2 * P], F16, ctx)
            before = sb("before", [P, P], BF16, ctx)
            ones16 = sb("ones16", [P, P], BF16, ctx)
            half_off = sb("half_off", [P, 1], F32, ctx)
            gw = sb("gw", [P, E0], F32, ctx)
            gw2 = sb("gw2", [P, 2, E0], F16, ctx)
            gb = sb("gb", [P, E0], F32, ctx)
            falling = sb("falling", [P, E0], F32, ctx)
            start_row = sb("start_row", [P, E0], F32, ctx)
            filled = sb("filled", [P, E0], F32, ctx)
            ids = sb("ids", [P, G, TOP], F32, ctx)
            gstats = sb("gstats", [P, G, 6], F32, ctx)
            rstd_s, shift_s, mean_s, gap_s, var_s, root_s, sq_s = (
                sb(n, [P, G], F32, ctx) for n in ("rstd_s", "shift_s", "mean_s", "gap_s", "var_s", "root_s", "sq_s"))
            lg = sb("lg0", [P, G, E0], F32, ctx)
            pick = sb("pick", [P, G, E0], F32, ctx)
            place = sb("place", [P, G, E0], F32, ctx)
            hot = sb("hot", [P, TOP, G, E0], F32, ctx)
            both = sb("both", [P, G, E0], BF16, ctx)
            best = [sb(f"best{k}", [P, G], F32, ctx) for k in range(TOP)]
            which = sb("which", [P, G], F32, ctx)
            pos_f = sb("pos_f", [P, TOP, G], F32, ctx)
            pos = sb("pos", [P, TOP, G], U32, ctx)
            tile_edge = sb("tile_edge", [1, N // T], F32, ctx)
            ones_e = sb("ones_e", [1, E0], F32, ctx)
            tile_no = sb("tile_no", [1, TILES], F32, ctx)
            expert_no = sb("expert_no", [1, E0], F32, ctx)
            count, ntiles, cum, lead = (sb(n, [1, E0], F32, ctx) for n in ("count", "ntiles", "cum", "lead"))
            spare = stage[0:1, :, :].rearrange("p g n -> p (g n)").bitcast(F32)
            past = spare[:, 0:TILES * E0].rearrange("p (t e) -> p t e", e=E0)
            over_edge = spare[:, TILES * E0:(TILES + N // T) * E0].rearrange("p (e b) -> p e b", e=E0)
            used = (TILES + N // T) * E0
            texp, trow, unused = (spare[:, used + n * TILES:used + (n + 1) * TILES] for n in range(3))
            ps_a = ps("ps_a", [P, 2, 512], F32, ctx)
            ps_t = ps("ps_t2", [P, G * 2 * P], F16, ctx)
            ps_n = ps("ps_n", [P, G, D], F32, ctx)
            ps_l = ps("ps_l", [P, 512], F32, ctx)
            ps_r = ps("ps_r", [P, 512], F32, ctx)

            adj_in = [sem(f"adj_in{i}") for i in range(G)]
            mask_by_act, mask_by_dve = sem("mask_by_act"), sem("mask_by_dve")
            equal_made, agg_ready, agg_free, v_b = sem("equal_made"), sem("agg_ready"), sem("agg_free"), sem("v_b")
            v_c, gate_in, iotas, gw_high, gw_ready = (sem(n) for n in ("v_c", "gate_in", "iotas", "gw_high", "gw_ready"))
            var_ready, root_ready, norm_ready = sem("var_ready2"), sem("root_ready2"), sem("norm_ready2")
            xn_ready, high_ready, pair_ready, tags_ready = sem("xn_ready2"), sem("high_ready2"), sem("pair_ready"), sem("tags_ready")
            xt_ready, xt_copied, logit_ready, gap_ready = sem("xt_ready2"), sem("xt_copied2"), sem("logit_ready"), sem("gap_ready")
            both_ready, rank_ready, pos_ready = sem("both_ready"), sem("rank_ready"), sem("pos_ready")
            rows_ready, scattered, row_free = sem("rows_ready"), sem("scattered"), sem("row_free")
            waits_taken, scatter_begun = sem("waits_taken"), sem("scatter_begun")
            ids_written, pair_free = sem("ids_written"), sem("pair_free")
            flat_equal = equal_one[:, :, :].rearrange("p b n -> p (b n)")
            THREE = ((0, 0), (0, 1), (1, 0))
            DVE_PIECES = (1, 4, 7, 10)
            ACT_PIECES = tuple(j for j in range(SLOTS) if j not in DVE_PIECES)

            def piece(j, early):
                return ahead[:, j, :] if early else stage[:, j % G, :]

            def wait_piece(eng, g, j, early):
                if early:
                    eng.wait_ge(ahead_in[j // G], g * (16 * G) + 16 * G)
                else:
                    eng.wait_ge(adj_in[j % G], g * (16 * G) + 16 * (j // G + 1 - G * EARLY))

            def wait_mask(eng, g, j):
                at = j % SLOTS
                for made, pieces in ((mask_by_dve, DVE_PIECES), (mask_by_act, ACT_PIECES)):
                    if at in pieces:
                        eng.wait_ge(made, g * len(pieces) + (j // SLOTS * len(pieces) + pieces.index(at) + 1))

            SQRT, NEWTON, NORM, LOW, TRANSPOSE, COPY, LOGITS = (4, 5, 6, 8, 7, 10, 9)
            TOP_1, TOP_2, RANK, GATES, POS, FINISH, BN, MOMENTS = (12, 13, 12, 14, 15, 2, 3, 3)

            def in_groups(eng, group):
                group(0, True, True)
                with eng.Fori(1, EARLY) as g:
                    group(g, False, True)
                with eng.Fori(EARLY, NG) as g:
                    group(g, False, False)

            with nc.Block() as block:
                @block.sync
                def _(sp):
                    def load(g, j, to, loaded, before):
                        if before is not None:
                            sp.wait_ge(equal_made, g * SLOTS + (j - before + 1))
                            sp.sem_inc(waits_taken, 1)
                            wait_mask(sp, g, j - before)
                            sp.sem_inc(waits_taken, 1)
                        sp.dma_start(to, adj_t[ds(g * SLOTS + j, 1), :, :].rearrange("a p n -> p (a n)")).then_inc(loaded, 16)
                    with sp.Fori(1, EARLY) as g:
                        for j in range(SLOTS):
                            load(g, j, ahead[:, j, :], ahead_in[j // G], SLOTS)
                    for j in range(G):
                        load(EARLY, j, stage[:, j, :], adj_in[j], None)
                    with sp.Fori(EARLY, NG - 1) as g:
                        for j in range(G, SLOTS + G):
                            load(g, j, stage[:, j % G, :], adj_in[j % G], G)
                    for j in range(G, SLOTS):
                        load(NG - 1, j, stage[:, j % G, :], adj_in[j % G], G)
                    sp.wait_ge(agg_ready, NB)
                    for e in range(WR):
                        load_weights(sp, e)

                @block.gpsimd
                def _(pool):
                    exact = dict(allow_small_or_imprecise_dtypes=True)
                    pool.memset(half_off[:, :], -30.0).then_inc(iotas, 1)
                    pool.iota(falling[:, :], pattern=[[-1, E0]], base=E0, channel_multiplier=0, **exact).then_inc(iotas, 1)
                    pool.iota(start_row[:, :], pattern=[[CAP, E0]], base=0, channel_multiplier=0, **exact).then_inc(iotas, 1)
                    pool.iota(filled[:, :], pattern=[[CAP, E0]], base=0, channel_multiplier=0, **exact).then_inc(iotas, 1)
                    pool.iota(ids[:, :, :].rearrange("p c k -> p (c k)"), pattern=[[P, G], [N, TOP]], base=0, channel_multiplier=1, **exact)\
                        .then_inc(iotas, 1)
                    pool.iota(tile_edge[:, :], pattern=[[T, N // T]], base=0, channel_multiplier=0, **exact).then_inc(iotas, 1)
                    pool.iota(tile_no[:, :], pattern=[[1, TILES]], base=0, channel_multiplier=0, **exact).then_inc(iotas, 1)
                    pool.iota(expert_no[:, :], pattern=[[1, E0]], base=0, channel_multiplier=0, **exact).then_inc(iotas, 1)
                    pool.memset(ones_e[:, :], 1.0).then_inc(iotas, 1)
                    pool.memset(before[:, :], 1.0).then_inc(iotas, 1)
                    pool.memset(ones16[:, :], 1.0).then_inc(iotas, 1)
                    pool.wait_ge(iotas, 11)
                    pool.affine_select(out=before[:, :], in_=before[:, :], compare_op=ALU.is_gt, fill=0.0,
                                       base=0, pattern=[[1, P]], channel_multiplier=-1).then_inc(iotas, 1)

                    def scatter(g):
                        pool.wait_ge(pair_ready, g)
                        pool.sem_inc(scatter_begun, 1)
                        for k in range(TOP):
                            pool.tensor_copy(row[:, :, k, 0:D].bitcast(F16), pair[:, :, :, :].rearrange("p c t d -> p c (t d)"))\
                                .then_inc(rows_ready, 1)
                        pool.wait_ge(rows_ready, g * TOP)
                        pool.sem_inc(pair_free, 1)
                        pool.wait_ge(pos_ready, g)
                        pool.wait_ge(ids_written, g)
                        pool.wait_ge(tags_ready, g)
                        pool.sem_inc(scatter_begun, 1)
                        for c in range(G):
                            for k in range(TOP):
                                pool.indirect_dma_start(out=sorted_x, out_offset=bass.IndirectOffsetOnAxis(ap=pos[:, k, c:c + 1], axis=0),
                                                        in_=row[:, c, k, :], in_offset=None).then_inc(scattered, 16)
                        pool.wait_ge(scattered, g * (16 * TOP * G))
                        pool.sem_inc(row_free, 1)
                    pool.sem_inc(row_free, 1)
                    pool.sem_inc(pair_free, 1)
                    with pool.Fori(1, NG) as g:
                        scatter(g)
                    scatter(NG)

                @block.scalar
                def _(act):
                    act.dma_start(gw[:, :], gate_w).then_inc(gate_in, 16)
                    act.dma_start(gb[:, :], gate_b.partition_broadcast(P)).then_inc(gate_in, 16)
                    act.wait_ge(iotas, 1)

                    def route(g, j):
                        if j == SQRT:
                            act.wait_ge(var_ready, g)
                            act.activation(root_s[:, :], var_s[:, :], ACT.Sqrt).then_inc(root_ready, 1)
                        if j == NORM:
                            act.wait_ge(norm_ready, g)
                            for c in range(G):
                                n = act.activation(ps_n[:, c, :], xs[:, ds(g * G + (c - G), 1), :].rearrange("p a d -> p (a d)"), ACT.Identity,
                                                   scale=rstd_s[:, c:c + 1], bias=shift_s[:, c:c + 1])
                            n.then_inc(xn_ready, 1)
                            act.wait_ge(pair_free, g)
                            act.wait_ge(xn_ready, g)
                            act.activation(pair[:, :, 0, :], ps_n[:, :, :], ACT.Copy).then_inc(high_ready, 1)
                        if j == COPY:
                            act.wait_ge(xt_ready, g)
                            act.activation(xnt[:, :], ps_t[:, :], ACT.Copy).then_inc(xt_copied, 1)
                        if j == GATES:
                            act.wait_ge(gap_ready, g)
                            act.wait_ge(row_free, g)
                            act.activation(row[:, :, 1, D + 1], gap_s[:, :], ACT.Sigmoid)
                            act.activation(row[:, :, 0, D + 1], gap_s[:, :], ACT.Sigmoid, scale=-1.0).then_inc(tags_ready, 1)

                    def group(g, first, early):
                        for j in range(SLOTS):
                            c, part = j // G, j % G
                            if not first:
                                route(g, j - 1)
                            if j not in ACT_PIECES:
                                continue
                            wait_piece(act, g, j, early)
                            if not (first and c < 2):
                                act.wait_ge(agg_ready, g * G + (c - 1))
                            act.sem_inc(waits_taken, 1)
                            act.activation(mask[c % 2][:, part * PIECE:(part + 1) * PIECE].bitcast(F8), piece(j, early), ACT.Sigmoid,
                                           scale=60.0, bias=half_off[:, :], saturate=False).then_inc(mask_by_act, 1)
                        if not first:
                            route(g, SLOTS - 1)
                        else:
                            act.wait_ge(gate_in, 32)
                            act.activation(gw2[:, 0, :], gw[:, :], ACT.Copy, scale=S_W).then_inc(gw_high, 1)
                    in_groups(act, group)
                    for j in range(SLOTS):
                        route(NG, j)

                @block.tensor
                def _(pe):
                    def route(g, j):
                        if j == TRANSPOSE:
                            pe.wait_ge(pair_ready, g)
                            for c in range(G):
                                for a in range(2):
                                    t = pe.transpose(ps_t[:, (c * 2 + a) * P:(c * 2 + a + 1) * P],
                                                     pair[:, c, a, :], ident16[:, :])
                            t.then_inc(xt_ready, 1)
                        if j == LOGITS:
                            pe.wait_ge(xt_copied, g)
                            for c in range(G):
                                for a, b in THREE:
                                    m = pe.matmul(ps_l[:, c * E0:(c + 1) * E0], xnt[:, (c * 2 + a) * P:(c * 2 + a + 1) * P], gw2[:, b, :],
                                                  start=(a + b == 0), stop=(a == 1))
                            m.then_inc(logit_ready, 1)
                        if j == RANK:
                            pe.wait_ge(both_ready, g)
                            for c in range(G):
                                for q in range(c + 1):
                                    pe.matmul(ps_r[:, c * E0:(c + 1) * E0], before[:, :] if q == c else ones16[:, :], both[:, q, :],
                                              start=(q == 0), stop=(q == c))
                            for q in range(G):
                                m = pe.matmul(ps_r[:, G * E0:(G + 1) * E0], ones16[:, :], both[:, q, :], start=(q == 0), stop=(q == G - 1))
                            m.then_inc(rank_ready, 1)

                    def group(g, first, early):
                        for j in range(SLOTS):
                            c, part = j // G, j % G
                            wait_mask(pe, g, j)
                            if part == 0:
                                pe.wait_ge(agg_free, g * G + (c + 1))
                            pe.ldweights(ident16[:, :], tile_position=(0, 0))
                            for q in range(part * NB // G, (part + 1) * NB // G):
                                for a in range(3):
                                    m = pe.matmul(ps_a[:, c % 2, 0:PART], mask[c % 2][:, q * P:(q + 1) * P].bitcast(F8),
                                                  parts[q // HB][:, q % HB, a * PART:(a + 1) * PART],
                                                  start=(q == 0 and a == 0), stop=(q == NB - 1 and a == 2))
                            if part == G - 1:
                                m.then_inc(agg_ready, 1)
                            if not first:
                                route(g, j)
                        if first:
                            pe.wait_ge(gw_ready, 1)
                            pe.wait_ge(iotas, 12)
                    in_groups(pe, group)
                    for j in range(SLOTS):
                        route(NG, j)

                @block.vector
                def _(dve):
                    dve.sem_inc(agg_free, 2)

                    def finish(b, k):
                        dve.wait_ge(agg_ready, b + 1)
                        dve.tensor_scalar(inv[:, k:k + 1], ps_a[:, k, D:PART], 1e-30, None, ALU.max).then_inc(v_b, 1)
                        dve.wait_ge(v_b, b * 2 + 1)
                        dve.reciprocal(inv[:, k:k + 1], inv[:, k:k + 1]).then_inc(v_b, 1)
                        dve.wait_ge(v_b, b * 2 + 2)
                        one = xs[:, ds(b, 1), :].rearrange("p a d -> p (a d)")
                        dve.scalar_tensor_tensor(out=one, in0=ps_a[:, k, 0:D], scalar=inv[:, k:k + 1], in1=one,
                                                 op0=ALU.mult, op1=ALU.add).then_inc(agg_free, 1)

                    S3 = [P, G, E0]
                    OWN = 31

                    def route(g, j, v):
                        if j == BN:
                            for c in range(G):
                                v.then(dve.bn_stats(gstats[:, c, :], xs[:, ds(g * G + (c - G), 1), :].rearrange("p a d -> p (a d)")))
                        if j == MOMENTS:
                            v.wait()
                            v.then(dve.tensor_tensor(mean_s[:, :], gstats[:, :, 1], gstats[:, :, 4], ALU.add))
                            v.then(dve.tensor_tensor(sq_s[:, :], gstats[:, :, 1], gstats[:, :, 4], ALU.subtract))
                            v.then(dve.tensor_tensor(var_s[:, :], gstats[:, :, 2], gstats[:, :, 5], ALU.add))
                            v.wait()
                            v.then(dve.tensor_tensor(sq_s[:, :], sq_s[:, :], sq_s[:, :], ALU.mult))
                            v.wait()
                            v.then(dve.scalar_tensor_tensor(out=var_s[:, :], in0=sq_s[:, :], scalar=D / 4.0, in1=var_s[:, :],
                                                            op0=ALU.mult, op1=ALU.add))
                            v.wait()
                            dve.tensor_scalar(var_s[:, :], var_s[:, :], 1.0 / D, EPS, ALU.mult, ALU.add).then_inc(var_ready, 1)
                        if j == NEWTON:
                            dve.wait_ge(root_ready, g)
                            inverse_root(dve, v, rstd_s[:, :], var_s[:, :], root_s[:, :], sq_s[:, :], 2.0 * S_X)
                            v.wait()
                            dve.scalar_tensor_tensor(out=shift_s[:, :], in0=mean_s[:, :], scalar=-0.5, in1=rstd_s[:, :],
                                                     op0=ALU.mult, op1=ALU.mult).then_inc(norm_ready, 1)
                        if j == LOW:
                            dve.wait_ge(high_ready, g)
                            dve.tensor_tensor(pair[:, :, 1, :], ps_n[:, :, :], pair[:, :, 0, :], ALU.subtract).then_inc(pair_ready, 1)
                        if j == TOP_1 or j == TOP_2:
                            k = 0 if j == TOP_1 else 1
                            if k == 0:
                                dve.wait_ge(logit_ready, g)
                                logits = ps_l[:, 0:G * E0].rearrange("p (c e) -> p c e", e=E0)
                                v.then(dve.scalar_tensor_tensor(out=lg[:, :, :], in0=logits,
                                                                scalar=1.0 / (S_X * S_W), in1=over(gb[:, :], S3, 1), op0=ALU.mult, op1=ALU.add))
                            else:
                                v.then(dve.scalar_tensor_tensor(out=lg[:, :, :], in0=hot[:, 0, :, :], scalar=TOPK_LOW,
                                                                in1=lg[:, :, :], op0=ALU.mult, op1=ALU.add))
                            v.wait()
                            v.then(dve.tensor_reduce(best[k][:, :], lg[:, :, :], AX.X, ALU.max))
                            v.wait()
                            v.then(dve.tensor_tensor(pick[:, :, :], lg[:, :, :], over(best[k][:, :], S3, 2), ALU.is_ge))
                            v.wait()
                            v.then(dve.tensor_tensor(pick[:, :, :], pick[:, :, :], over(falling[:, :], S3, 1), ALU.mult))
                            v.wait()
                            v.then(dve.tensor_reduce(which[:, :], pick[:, :, :], AX.X, ALU.max))
                            v.wait()
                            v.then(dve.tensor_tensor(hot[:, k, :, :], over(falling[:, :], S3, 1), over(which[:, :], S3, 2), ALU.is_equal))
                            v.wait()
                            if k == 1:
                                dve.tensor_tensor(both[:, :, :], hot[:, 0, :, :], hot[:, 1, :, :], ALU.add).then_inc(both_ready, 1)
                                dve.tensor_tensor(gap_s[:, :], best[1][:, :], best[0][:, :], ALU.subtract).then_inc(gap_ready, 1)
                        if j == POS:
                            dve.wait_ge(rank_ready, g)
                            v.then(dve.tensor_tensor(place[:, :, :], ps_r[:, 0:G * E0].rearrange("p (c e) -> p c e", e=E0),
                                                     over(filled[:, :], S3, 1), ALU.add))
                            v.wait()
                            v.then(dve.tensor_tensor(filled[:, :], filled[:, :], ps_r[:, G * E0:(G + 1) * E0], ALU.add))
                            v.then(dve.tensor_tensor(hot[:, :, :, :], hot[:, :, :, :], over(place[:, :, :], [P, TOP, G, E0], 1), ALU.mult))
                            dve.wait_ge(row_free, g)
                            v.wait()
                            v.then(dve.tensor_reduce(pos_f[:, :, :], hot[:, :, :, :], AX.X, ALU.add))
                            v.wait()
                            dve.tensor_copy(pos[:, :, :], pos_f[:, :, :]).then_inc(pos_ready, 1)
                            dve.tensor_copy(row[:, :, :, D].bitcast(U32), ids[:, :, :]).then_inc(ids_written, 1)
                            dve.wait_ge(ids_written, g)
                            v.then(dve.tensor_scalar(ids[:, :, :], ids[:, :, :], float(G * P), None, ALU.add))

                    def group(g, first, early):
                        v = None if first else Steps(dve, v_c, (g - 1) * OWN)
                        for j in range(SLOTS):
                            c, part = j // G, j % G
                            wait_piece(dve, g, j, early)
                            if j == 0 and not early:
                                wait_mask(dve, g, G - 1 - SLOTS)
                            if j == BN and not first:
                                dve.wait_ge(agg_free, g * G + 2)
                            dve.tensor_scalar(flat_equal[:, ds((g * SLOTS + j) * PIECE, PIECE)], piece(j, early), 1, F8_ONE,
                                              ALU.is_equal, ALU.mult).then_inc(equal_made, 1)
                            if j in DVE_PIECES:
                                if not (first and c < 2):
                                    dve.wait_ge(agg_ready, g * G + (c - 1))
                                dve.tensor_scalar(mask[c % 2][:, part * PIECE:(part + 1) * PIECE], piece(j, early), 0, F8_ONE,
                                                  ALU.is_gt, ALU.mult).then_inc(mask_by_dve, 1)
                            if part == FINISH and not (first and c == 0):
                                finish(g * G + (c - 1), (c - 1) % 2)
                            if not first:
                                route(g, j, v)
                        if first:
                            dve.wait_ge(gw_high, 1)
                            dve.scalar_tensor_tensor(out=gw2[:, 1, :], in0=gw[:, :], scalar=S_W, in1=gw2[:, 0, :],
                                                     op0=ALU.mult, op1=ALU.subtract).then_inc(gw_ready, 1)
                            dve.wait_ge(iotas, 12)
                            dve.wait_ge(gate_in, 32)
                        if v:
                            assert v.n == OWN, v.n
                    in_groups(dve, group)
                    finish(NB - 1, (NB - 1) % 2)
                    v = Steps(dve, v_c, (NG - 1) * OWN)
                    dve.wait_ge(agg_free, NB + 2)
                    for j in range(SLOTS):
                        route(NG, j, v)

                    v.wait()
                    v.then(dve.tensor_tensor(count[:, :], filled[0:1, :], start_row[0:1, :], ALU.subtract))
                    v.then(dve.tensor_copy(end_row[:, :], filled[0:1, :]))
                    v.wait()
                    v.then(dve.tensor_tensor(over_edge[:, :, :], over(count[:, :], [1, E0, N // T], 2),
                                             over(tile_edge[:, :], [1, E0, N // T], 1), ALU.is_gt))
                    v.wait()
                    v.then(dve.tensor_reduce(ntiles[:, :], over_edge[:, :, :], AX.X, ALU.add))
                    v.wait()
                    v.then(dve.tensor_tensor_scan(cum[:, :], ones_e[:, :], ntiles[:, :], 0.0, ALU.mult, ALU.add))
                    v.wait()
                    v.then(dve.tensor_tensor(lead[:, :], cum[:, :], ntiles[:, :], ALU.subtract))
                    v.wait()
                    v.then(dve.scalar_tensor_tensor(out=lead[:, :], in0=lead[:, :], scalar=-float(T), in1=start_row[0:1, :],
                                                    op0=ALU.mult, op1=ALU.add))
                    S = [1, TILES, E0]
                    v.then(dve.tensor_tensor(past[:, :, :], over(tile_no[:, :], S, 2), over(cum[:, :], S, 1), ALU.is_ge))
                    v.wait()
                    v.then(dve.tensor_reduce(texp[:, :], past[:, :, :], AX.X, ALU.add))
                    v.wait()
                    v.then(dve.tensor_tensor(past[:, :, :], over(texp[:, :], S, 2), over(expert_no[:, :], S, 1), ALU.is_equal))
                    v.wait()
                    v.then(dve.tensor_tensor(past[:, :, :], past[:, :, :], over(lead[:, :], S, 1), ALU.mult))
                    v.wait()
                    v.then(dve.tensor_reduce(trow[:, :], past[:, :, :], AX.X, ALU.add))
                    v.then(dve.tensor_scalar(unused[:, :], texp[:, :], float(E0), None, ALU.is_ge))
                    v.wait()
                    v.then(dve.scalar_tensor_tensor(out=trow[:, :], in0=tile_no[:, :], scalar=float(T), in1=trow[:, :],
                                                    op0=ALU.mult, op1=ALU.add))
                    v.wait()
                    v.then(dve.scalar_tensor_tensor(out=trow[:, :], in0=unused[:, :], scalar=float(SPARE), in1=trow[:, :],
                                                    op0=ALU.mult, op1=ALU.max))
                    v.then(dve.tensor_scalar(texp[:, :], texp[:, :], float(E0 - 1), float(2 * HC0 * D), ALU.min, ALU.mult))
                    v.wait()
                    v.then(dve.tensor_copy(tile_row[:, :], trow[:, :]))
                    v.then(dve.tensor_copy(tile_at[:, :], texp[:, :]))
        attend_ctx.close()

        expert_ctx = ExitStack()
        w12 = sb("w12", [P, E0, 2, 2 * H0], F16, expert_ctx)
        w3s = sb("w3s", [P, E0, 2, HC0 * D], F16, expert_ctx)
        with ExitStack() as ctx:
            zeros = sb("zero_rows", [P, ROW], F32, ctx)
            high_made, low_made, zeroed, padded = sem("high_made"), sem("low_made"), sem("zeroed2"), sem("padded")
            with nc.Block() as block:
                @block.sync
                def _(sp):
                    for e in range(WR, E0):
                        sp.wait_ge(low_made, 2 * (e - WR + 1))
                        load_weights(sp, e)

                @block.gpsimd
                def _(pool):
                    pool.memset(zeros[:, :], 0.0).then_inc(zeroed, 1)
                    pool.wait_ge(zeroed, 1)
                    pool.memset(zeros[:, D:D + 1].bitcast(U32), NOWHERE).then_inc(zeroed, 1)
                    pool.wait_ge(zeroed, 2)
                    ends = [pool.alloc_register(f"end_row{e}") for e in range(E0)]
                    pool.load(ends, end_row[:, :])
                    for e in range(E0):
                        first = pool.snap(ends[e], donate=True, min_val=e * CAP, max_val=e * CAP + N)
                        pool.dma_start(sorted_x[ds(first, T), :].rearrange("(h p) d -> p h d", p=P), over(zeros[:, :], [P, HT, ROW], 1))\
                            .then_inc(padded, 16)
                    pool.wait_ge(padded, 16 * E0)

                @block.scalar
                def _(act):
                    for e in range(E0):
                        act.wait_ge(raw_in[e % WR], 48 * (e // WR + 1))
                        act.activation(w12[:, e, 0, :], raw[:, e % WR, 0:2 * H0], ACT.Copy, scale=S_W).then_inc(high_made, 1)
                        act.activation(w3s[:, e, 0, :], raw[:, e % WR, 2 * H0:EW], ACT.Copy, scale=S_W).then_inc(high_made, 1)

                @block.vector
                def _(dve):
                    for e in range(E0):
                        dve.wait_ge(high_made, 2 * e + 1)
                        dve.scalar_tensor_tensor(out=w12[:, e, 1, :], in0=raw[:, e % WR, 0:2 * H0], scalar=S_W, in1=w12[:, e, 0, :],
                                                 op0=ALU.mult, op1=ALU.subtract).then_inc(low_made, 1)
                        dve.wait_ge(high_made, 2 * e + 2)
                        dve.scalar_tensor_tensor(out=w3s[:, e, 1, :], in0=raw[:, e % WR, 2 * H0:EW], scalar=S_W, in1=w3s[:, e, 0, :],
                                                 op0=ALU.mult, op1=ALU.subtract).then_inc(low_made, 1)

        with ExitStack() as ctx:
            UN = 8
            XR = 4
            hT_at = XR * HT * ROW
            y_at = hT_at + 2 * HC0 * T
            act_at = y_at + 2 * HT * D
            assert act_at + HC0 * T <= HB * V3 // 2
            xt = ring[:, 0:hT_at].rearrange("p (x h d) -> p x h d", x=XR, h=HT)
            places = sb("places", [P, UN, HT], U32, ctx)
            gates = sb("gates", [P, UN, HT], F32, ctx)
            xT = sb("xT", [P, 2, T], F16, ctx)
            gate_act = ring[:, act_at:act_at + HC0 * T]
            hT = ring[:, hT_at:y_at].bitcast(F16).rearrange("p (k a n) -> p k a n", k=2, a=2)
            y = ring[:, y_at:y_at + 2 * HT * D].rearrange("p (k h d) -> p k h d", k=2, h=HT)
            ps_x = ps("ps_x", [P, 2, 2 * 512], F16, ctx)
            ps_h = ps("ps_h", [P, 2, 2, HC0 * T], F32, ctx)
            ps_y = ps("ps_y", [P, 2, 512], F32, ctx)
            row_in = [sem(f"row_in{i}") for i in range(XR)]
            stored = [sem(f"stored{i}") for i in range(2)]
            tx_ready, tags_read, x_copied, h_ready, gated, hid_ready = (
                sem(n) for n in ("tx_ready", "tags_read", "x_copied", "h_ready_e", "gated", "hid_ready"))
            high_ready, hp_ready, y_ready, y_scaled = sem("high_ready_e"), sem("hp_ready_e"), sem("y_ready"), sem("y_scaled")
            w12f = w12[:, :, :, :].rearrange("p e t n -> p (e t n)")
            w3f = w3s[:, :, :, :].rearrange("p e t n -> p (e t n)")
            THREE = ((0, 0), (0, 1), (1, 0))
            LAST = TILES + 3
            assert TILES % UN == 0

            def in_steps(eng, step, before_round=None):
                if before_round:
                    before_round(0)
                for s in range(UN):
                    step(s, s, s)
                with eng.Fori(1, TILES // UN) as i:
                    if before_round:
                        before_round(i)
                    for j in range(UN):
                        step(i * UN + j, j, None)
                if before_round:
                    before_round(None)
                for s in range(TILES, LAST):
                    step(s, s % UN, s)

            def runs(known, lag):
                return known is None or 0 <= known - lag < TILES

            def has(known, lag, before):
                return known is None or known - lag >= before

            def row_round(s, j, known):
                return (known // XR + 1) * 16 if known is not None else (s - j) * (16 // XR) + 16 * (j // XR + 1)

            with nc.Block() as block:
                @block.sync
                def _(sp):
                    first = []

                    def load_rows(i):
                        if i is None:
                            return
                        regs = [sp.alloc_register(f"tile_row_{'first' if isinstance(i, int) else 'loop'}_{n}") for n in range(UN)]
                        sp.load(regs, tile_row[0:1, ds(i * UN, UN)])
                        first[:] = [sp.snap(r, donate=True, min_val=0, max_val=SPARE) for r in regs]

                    def load(s, j, known):
                        if not runs(known, 0):
                            return
                        if has(known, 0, XR):
                            sp.wait_ge(tx_ready, s - (XR - 1))
                            sp.sem_inc(waits_taken, 1)
                            sp.wait_ge(tags_read, s * 2 - (2 * XR - 2))
                            sp.sem_inc(waits_taken, 1)
                        sp.dma_start(xt[:, j % XR, :, :], sorted_x[ds(first[j], T), :].rearrange("(h p) d -> p h d", p=P))\
                          .then_inc(row_in[j % XR], 16)
                    in_steps(sp, load, load_rows)

                @block.gpsimd
                def _(pool):
                    for t in range(TILES):
                        for h in range(HT):
                            pool.wait_ge(y_scaled, t * HT + h + 1)
                            pool.indirect_dma_start(out=expert_rows,
                                                    out_offset=bass.IndirectOffsetOnAxis(ap=places[:, t % UN, h:h + 1], axis=0),
                                                    in_=y[:, t % 2, h, :], in_offset=None, bounds_check=TOP * N - 1, oob_is_err=False)\
                                .then_inc(stored[t % 2], 16)
                    pool.wait_ge(stored[0], TILES // 2 * 16 * HT)
                    pool.wait_ge(stored[1], TILES // 2 * 16 * HT)

                @block.scalar
                def _(act):
                    def step(s, j, known):
                        if runs(known, 0):
                            act.wait_ge(tx_ready, s + 1)
                            if has(known, 0, 1):
                                act.wait_ge(h_ready, s)
                            act.activation(xT[:, :, :], ps_x[:, j % 2, 0:2 * T].rearrange("p (a r) -> p a r", a=2), ACT.Copy)\
                               .then_inc(x_copied, 1)
                        if runs(known, 1):
                            act.wait_ge(h_ready, s)
                            if has(known, 1, 1):
                                act.wait_ge(hid_ready, s - 1)
                            act.activation(gate_act[:, :], ps_h[:, (j - 1) % 2, 0, :], ACT.Silu, scale=1.0 / (S_X * S_W))\
                               .then_inc(gated, 1)
                            act.wait_ge(hid_ready, s)
                            if has(known, 1, 2):
                                act.wait_ge(y_ready, s - 2)
                            act.activation(hT[:, (j - 1) % 2, 0, :], ps_h[:, (j - 1) % 2, 0, :], ACT.Copy).then_inc(high_ready, 1)
                    in_steps(act, step)

                @block.tensor
                def _(pe):
                    BACK = 4
                    at = {}

                    def load_places(i):
                        if isinstance(i, int):
                            tile0, start, n, name = 0, 0, UN, "first"
                        elif i is None:
                            tile0, start, n, name = -BACK, TILES - BACK, BACK, "last"
                        else:
                            tile0, start, n, name = -BACK, i * UN - BACK, BACK + UN, "loop"
                        regs = [pe.alloc_register(f"expert_at_{name}_{m}") for m in range(n)]
                        pe.load(regs, tile_at[0:1, ds(start, n)])
                        at.clear()
                        for m in range(n):
                            at[tile0 + m] = pe.snap(regs[m], donate=True, min_val=0, max_val=(E0 - 1) * 2 * HC0 * D)

                    def step(s, j, known):
                        if runs(known, 0):
                            pe.wait_ge(row_in[j % XR], row_round(s, j, known))
                            if has(known, 0, 2):
                                pe.wait_ge(x_copied, s - 1)
                            for a in range(2):
                                for h in range(HT):
                                    t = pe.transpose(ps_x[:, j % 2, a * T + h * P:a * T + (h + 1) * P],
                                                     xt[:, j % XR, h, a * HALF_ROW:(a + 1) * HALF_ROW].bitcast(F16), ident16[:, :])
                            t.then_inc(tx_ready, 1)
                        if runs(known, 1):
                            k = (j - 1) % 2
                            off = at[j - 1] * 2
                            pe.wait_ge(x_copied, s)
                            if has(known, 1, 2):
                                pe.wait_ge(hp_ready, s - 2)
                            for c in range(2 * HC0):
                                for a, b in THREE:
                                    m = pe.matmul(ps_h[:, k, c // HC0, c % HC0 * T:(c % HC0 + 1) * T],
                                                  w12f[:, ds(off + (a * 2 * H0 + c * P), P)], xT[:, b, :],
                                                  start=(a + b == 0), stop=(a == 1))
                            m.then_inc(h_ready, 1)
                        if runs(known, 3):
                            k = (j - 3) % 2
                            off = at[j - 3]
                            pe.wait_ge(hp_ready, s - 2)
                            if has(known, 3, 2):
                                pe.wait_ge(y_scaled, s * HT - 4 * HT)
                            for h in range(HT):
                                for c in range(HC0):
                                    for a, b in THREE:
                                        m = pe.matmul(ps_y[:, k, h * D:(h + 1) * D], hT[:, k, a, c * T + h * P:c * T + (h + 1) * P],
                                                      w3f[:, ds(off + (b * HC0 * D + c * D), D)],
                                                      start=(c + a + b == 0), stop=(c + a == HC0))
                            m.then_inc(y_ready, 1)
                    in_steps(pe, step, load_places)

                @block.vector
                def _(dve):
                    def step(s, j, known):
                        if runs(known, 1):
                            k = (j - 1) % 2
                            dve.wait_ge(gated, s)
                            dve.scalar_tensor_tensor(out=ps_h[:, k, 0, :], in0=ps_h[:, k, 1, :], scalar=S_E / (S_X * S_W),
                                                     in1=gate_act[:, :], op0=ALU.mult, op1=ALU.mult).then_inc(hid_ready, 1)
                        if runs(known, 3):
                            k = (j - 3) % 2
                            dve.wait_ge(y_ready, s - 2)
                            dve.wait_ge(tags_read, s * 2 - 4)
                            if has(known, 3, 2):
                                dve.wait_ge(stored[k], stored_upto(s, j, known))
                            for h in range(HT):
                                dve.tensor_scalar(y[:, k, h, :], ps_y[:, k, h * D:(h + 1) * D], gates[:, (j - 3) % UN, h:h + 1],
                                                  1.0 / (S_W * S_E), ALU.mult, ALU.mult).then_inc(y_scaled, 1)
                        if runs(known, 0):
                            dve.wait_ge(row_in[j % XR], row_round(s, j, known))
                            if has(known, 0, UN):
                                dve.wait_ge(stored[j % 2], s * (8 * HT) - (8 * HT) * (j % 2) - 16 * HT * (UN // 2 - 1))
                            dve.tensor_copy(places[:, j, :], xt[:, j % XR, :, D].bitcast(U32)).then_inc(tags_read, 1)
                            dve.tensor_copy(gates[:, j, :], xt[:, j % XR, :, D + 1]).then_inc(tags_read, 1)
                        if runs(known, 1):
                            dve.wait_ge(high_ready, s)
                            dve.tensor_tensor(hT[:, (j - 1) % 2, 1, :], ps_h[:, (j - 1) % 2, 0, :], hT[:, (j - 1) % 2, 0, :], ALU.subtract)\
                               .then_inc(hp_ready, 1)

                    def stored_upto(s, j, known):
                        if known is not None:
                            return (known - 3) // 2 * 16 * HT
                        return (s - j) * (8 * HT) + (j - 3) // 2 * 16 * HT
                    in_steps(dve, step)
        expert_ctx.close()
        ring_ctx.close()

        mean_ctx = ExitStack()
        parts2 = sb("parts2", [P, NB, V2], F16, mean_ctx)
        mask = sb("mask2", [P, 2, NB * P], U8, mean_ctx)
        wide = {"wt": (P, D), "rt": (P, E1), "f1": (P, EH1), "f2": (P, KC1 * D), "b2": (E1, D)}
        source = {"wt": g1_wt, "rt": router_wt, "f1": f_w1, "f2": f_w2, "b2": f_b2}
        scales = {"wt": S_W, "rt": S_W, "f1": S_W, "f2": S_W, "b2": S_W * S_H}
        raw = {n: sb("raw_" + n, [r, c], F32, mean_ctx) for n, (r, c) in wide.items()}
        two = {n: sb("two_" + n, [r, 2, c], F16, mean_ctx) for n, (r, c) in wide.items()}
        rb = sb("rb", [P, E1], F32, mean_ctx)
        fb1 = sb("fb1", [P, KC1], F32, mean_ctx)
        never = sb("never", [E1, KC1, P], BF16, mean_ctx)
        falling1 = sb("falling1", [P, E1], F32, mean_ctx)
        mask_copied = sem("mask_copied")
        with ExitStack() as ctx:
            CK = 4
            NC = NB // CK
            NR = 3
            HALVES = 2
            warm_bank = ps("warm_bank", [P, 512], F32, ctx)
            rows = sb("rows", [P, NR, TOP, CK, D], F32, ctx)
            xn = sb("xn_c", [P, 2, CK, D], F32, ctx)
            wb = sb("wb", [P, D], F32, ctx)
            shift = tmp[0]
            stats = sb("stats", [P, NB, 6], F32, ctx)
            gathered = [sem(f"gathered{i}") for i in range(NR)]
            v_d, added, var_ready, root_ready = sem("v_d"), sem("added"), sem("var_ready3"), sem("root_ready3")
            norm_ready, xn_ready, high_ready, low_ready = sem("norm_ready3"), sem("xn_ready3"), sem("high_ready3"), sem("low_ready3")
            bias_in, w_in, const_ready = sem("bias_in"), sem("m_w_in"), sem("m_const_ready")
            weight_high, ones_made = sem("m_weight_high"), sem("ones_made")
            W = len(wide)
            last_ready = sem("last_ready")
            last_xn = rows[:, (NC - 2) % NR, 0, :, :]
            with nc.Block() as block:
                @block.sync
                def _(sp):
                    def load(q):
                        for k in range(TOP):
                            lo = k * N + q * CK * P
                            sp.dma_start(rows[:, q % NR, k, :, :],
                                         expert_rows[lo:lo + CK * P, :].rearrange("(c p) d -> p c d", p=P)).then_inc(gathered[q % NR], 16)
                    for q in range(NR):
                        load(q)
                    sp.dma_start(wb[:, :], g1_b.partition_broadcast(P)).then_inc(bias_in, 16)
                    for n in ("wt", "rt", "b2"):
                        sp.dma_start(raw[n][:, :], source[n]).then_inc(w_in, 16)
                    sp.dma_start(rb[:, :], router_b.partition_broadcast(P)).then_inc(w_in, 16)
                    sp.dma_start(fb1[:, :], f_b1).then_inc(w_in, 16)
                    for q in range(NR, NC):
                        sp.wait_ge(added, TOP * (q - NR + 1))
                        load(q)
                        if q == NR:
                            for n in ("f1", "f2"):
                                sp.dma_start(raw[n][:, :], source[n]).then_inc(w_in, 16)

                @block.gpsimd
                def _(pool):
                    exact = dict(allow_small_or_imprecise_dtypes=True)
                    flat = never[:, :, :].rearrange("e k p -> e (k p)")
                    pool.memset(parts2[:, :, 2 * D:V2], 1.0).then_inc(ones_made, 1)
                    pool.iota(falling1[:, :], pattern=[[-1, E1]], base=E1, channel_multiplier=0, **exact).then_inc(const_ready, 1)
                    pool.wait_ge(const_ready, 1)
                    pool.memset(flat, NEVER).then_inc(const_ready, 1)
                    pool.wait_ge(const_ready, 2)
                    pool.affine_select(out=flat, in_=flat, compare_op=ALU.is_ge, fill=0.0, base=0,
                                       pattern=[[1, EH1]], channel_multiplier=-H1).then_inc(const_ready, 1)
                    pool.wait_ge(const_ready, 3)
                    pool.affine_select(out=flat, in_=flat, compare_op=ALU.is_gt, fill=0.0, base=H1,
                                       pattern=[[-1, EH1]], channel_multiplier=H1).then_inc(const_ready, 1)
                    pool.wait_ge(const_ready, 4)
                    for u in range(2):
                        pool.tensor_copy(mask[:, u, :].bitcast(F32), equal_one[:, u, :].bitcast(F32)).then_inc(mask_copied, 1)
                    pool.wait_ge(bias_in, 16)
                    for q in range(NC):
                        c = slice(q * CK, (q + 1) * CK)
                        if q < NC - 1:
                            pool.wait_ge(xn_ready, q + 1)
                        else:
                            pool.wait_ge(last_ready, 1)
                        pool.tensor_tensor(xs[:, c, :], xs[:, c, :], over(wb[:, :], [P, CK, D], 1), ALU.add)

                @block.scalar
                def _(act):
                    act.wait_ge(w_in, 16 * (W + 2))
                    for n in wide:
                        act.activation(two[n][:, 0, :], raw[n][:, :], ACT.Copy, scale=scales[n]).then_inc(weight_high, 1)
                    act.activation(fb1[:, :], fb1[:, :], ACT.Copy, scale=S_H)
                    for half in range(HALVES):
                        h = slice(half * NB // 2, (half + 1) * NB // 2)
                        act.wait_ge(var_ready, half + 1)
                        act.activation(tmp[1][:, h], tmp[0][:, h], ACT.Sqrt).then_inc(root_ready, 1)
                        act.wait_ge(norm_ready, half + 1)
                        for q in range(half * NC // 2, min((half + 1) * NC // 2, NC - 1)):
                            if q >= 2:
                                act.wait_ge(low_ready, q - 1)
                            for c in range(CK):
                                b = q * CK + c
                                n = act.activation(xn[:, q % 2, c, :], xs[:, b, :], ACT.Identity,
                                                   scale=rstd[:, b:b + 1], bias=shift[:, b:b + 1])
                            n.then_inc(xn_ready, 1)
                            act.wait_ge(xn_ready, q + 1)
                            act.activation(parts2[:, q * CK:(q + 1) * CK, 0:D], xn[:, q % 2, :, :], ACT.Copy).then_inc(high_ready, 1)

                @block.tensor
                def _(pe):
                    pe.wait_ge(last_ready, 1)
                    for _ in range(WARM_UP):
                        pe.matmul(warm_bank[:, 0:P], ident16[:, :], ident16[:, :], start=True, stop=True)

                @block.vector
                def _(dve):
                    v = Steps(dve, v_d)

                    def add_chunk(q):
                        c = slice(q * CK, (q + 1) * CK)
                        dve.wait_ge(gathered[q % NR], 16 * TOP * (q // NR + 1))
                        for k in range(TOP):
                            if k > 0:
                                dve.wait_ge(added, TOP * q + k)
                            dve.tensor_tensor(xs[:, c, :], xs[:, c, :], rows[:, q % NR, k, :, :], ALU.add).then_inc(added, 1)

                    def chunk_stats(q):
                        dve.wait_ge(added, TOP * (q + 1))
                        for c in range(q * CK, (q + 1) * CK):
                            v.then(dve.bn_stats(stats[:, c, :], xs[:, c, :]))

                    def low_part(q):
                        c = slice(q * CK, (q + 1) * CK)
                        dve.wait_ge(high_ready, q + 1)
                        dve.tensor_tensor(parts2[:, c, D:2 * D], xn[:, q % 2, :, :], parts2[:, c, 0:D], ALU.subtract).then_inc(low_ready, 1)

                    def half_norm(half):
                        h = slice(half * NB // 2, (half + 1) * NB // 2)
                        moments(dve, v, stats, h)
                        v.wait()
                        dve.tensor_scalar(tmp[0][:, h], tmp[3][:, h], 1.0 / D, EPS, ALU.mult, ALU.add).then_inc(var_ready, 1)
                        dve.wait_ge(root_ready, half + 1)
                        inverse_root(dve, v, rstd[:, h], tmp[0][:, h], tmp[1][:, h], tmp[2][:, h], 2.0 * S_X)
                        v.wait()
                        dve.scalar_tensor_tensor(out=shift[:, h], in0=mean[:, h], scalar=-1.0, in1=rstd[:, h],
                                                 op0=ALU.mult, op1=ALU.mult).then_inc(norm_ready, 1)

                    add_chunk(0)
                    for q in range(1, NC):
                        add_chunk(q)
                        chunk_stats(q - 1)
                        if q == NC // 2:
                            half_norm(0)
                        if q > NC // 2:
                            low_part(q - NC // 2 - 1)
                    chunk_stats(NC - 1)
                    half_norm(1)
                    low_part(NC // 2 - 1)
                    c = slice((NC - 1) * CK, NC * CK)
                    v.wait()
                    dve.wait_ge(norm_ready, HALVES)
                    for b in range((NC - 1) * CK, NC * CK):
                        n = dve.tensor_scalar(last_xn[:, b % CK, :], xs[:, b, :], rstd[:, b:b + 1], shift[:, b:b + 1], ALU.mult, ALU.add)
                    n.then_inc(last_ready, 1)
                    dve.wait_ge(last_ready, 1)
                    v.then(dve.tensor_copy(parts2[:, c, 0:D], last_xn))
                    v.wait()
                    dve.tensor_tensor(parts2[:, c, D:2 * D], last_xn, parts2[:, c, 0:D], ALU.subtract)
                    for q, names in zip(range(NC // 2, NC), (("wt", "rt", "b2", "f1"), ("f2",), (), ())):
                        if q < NC - 1:
                            low_part(q)
                        for n in names:
                            dve.wait_ge(weight_high, list(wide).index(n) + 1)
                            dve.scalar_tensor_tensor(out=two[n][:, 1, :], in0=raw[n][:, :], scalar=scales[n], in1=two[n][:, 0, :],
                                                     op0=ALU.mult, op1=ALU.subtract)

        with ExitStack() as ctx:
            total = sb("total", [P, D], F32, ctx)
            expert_out = sb("expert_out", [P, D], F32, ctx)
            inv = sb("inv2", [P, 2], F32, ctx)
            agg = sb("agg2", [P, 2, 2, D], F16, ctx)
            aggt = sb("aggt", [P, 2, 2, P], F16, ctx)
            xc = sb("xc", [P, D], F32, ctx)
            squares = sb("squares", [P, D], F32, ctx)
            sq = sb("sq", [P, 6], F32, ctx)
            xn = sb("xn3", [P, 2, 2, D], F16, ctx)
            xnt = sb("xnt3", [P, 2, 2, P], F16, ctx)
            lg = sb("lg", [P, E1], F32, ctx)
            best1 = sb("best_logit", [P, 1], F32, ctx)
            which1 = sb("which1", [P, 1], F32, ctx)
            others = sb("others", [P, E1], F16, ctx)
            others_t = sb("others_t", [E1, P], BF16, ctx)
            hot_t = sb("hot_t", [E1, P], F16, ctx)
            hm = raw["f1"][:, :].rearrange("p (c n) -> p c n", c=KC1)
            hp = sb("hp", [P, 2, KC1, P], F16, ctx)
            fin = sb("fin", [P, 2, D], F32, ctx)
            ps_a = ps("ps_a2", [P, 2, 512], F32, ctx)
            ps_f = ps("ps_f", [P, 2, 512], F32, ctx)
            ps_t = ps("ps_t3", [P, 2, P], F16, ctx)
            ps_w = ps("ps_w", [P, 512], F32, ctx)
            ps_i = ps("ps_i", [P, 4 * P], F16, ctx)
            ps_o = ps("ps_o", [P, 512], F32, ctx)
            names = "agg_ready agg_read norm_ready at_ready at_copied wx_ready var_ready root_ready " \
                    "xn_ready xt_ready xt_copied lg_ready lg_read others_ready ot_ready hot_ready f_ready relu_ready high_ready " \
                    "hp_ready o_half o_read fin_ready".split()
            (agg_ready, agg_read, norm_ready, at_ready, at_copied, wx_ready, var_ready, root_ready,
             xn_ready, xt_ready, xt_copied, lg_ready, lg_read, others_ready, ot_ready, hot_ready, f_ready, relu_ready, high_ready,
             hp_ready, o_half, o_read, fin_ready) = [sem("m_" + n) for n in names]
            own_e = sem("own_e")
            own = {n: sem("own_" + n) for n in "abc"}
            stored = [sem(f"stored_m{i}") for i in range(2)]
            LAST = NB + 3
            CH = KC1 // 2

            def in_steps(eng, step):
                for u in range(4):
                    step(u, u % 2, u)
                with eng.Fori(2, NB // 2) as i:
                    for k in range(2):
                        step(i * 2 + k, k, None)
                for u in range(NB, LAST):
                    step(u, u % 2, u)

            def runs(known, lag):
                return known is None or 0 <= known - lag < NB

            def has(known, lag, before):
                return known is None or known - lag >= before

            with nc.Block() as block:
                @block.sync
                def _(sp):
                    def step(u, k, known):
                        if runs(known, 3):
                            sp.wait_ge(fin_ready, u - 2)
                            sp.dma_start(out.rearrange("(b p) d -> b p d", p=P)[ds(u - 3, 1), :, :].rearrange("b p d -> p (b d)"),
                                         fin[:, 1 - k, :]).then_inc(stored[1 - k], 16)
                    in_steps(sp, step)
                    sp.wait_ge(stored[0], NB // 2 * 16)
                    sp.wait_ge(stored[1], NB // 2 * 16)

                @block.gpsimd
                def _(pool):
                    def step(u, k, known):
                        if runs(known, 0) and known not in (0, 1):
                            pool.wait_ge(agg_ready, u - 1)
                            one = equal_one[:, ds(u, 1), :].rearrange("p b n -> p (b n)")
                            pool.tensor_copy(mask[:, k, :].bitcast(F32), one.bitcast(F32)).then_inc(mask_copied, 1)
                    in_steps(pool, step)

                @block.scalar
                def _(act):
                    def step(u, k, known):
                        o = 1 - k

                        def relus(half, n):
                            act.wait_ge(f_ready, n)
                            for c in range(half * CH, (half + 1) * CH):
                                r = act.activation(hm[:, c, :], ps_f[:, half, (c - half * CH) * P:(c - half * CH + 1) * P],
                                                   ACT.Relu, bias=fb1[:, c:c + 1], scale=S_H / (S_X * S_W))
                            r.then_inc(relu_ready, 1)
                            act.wait_ge(relu_ready, n)
                            act.activation(hp[:, 0, half * CH:(half + 1) * CH, :], hm[:, half * CH:(half + 1) * CH, :], ACT.Copy)\
                               .then_inc(high_ready, 1)
                        if runs(known, 2):
                            act.wait_ge(xt_ready, u - 1)
                            act.activation(xnt[:, k, :, :], ps_i[:, 0:2 * P], ACT.Copy).then_inc(xt_copied, 1)
                        if runs(known, 1):
                            act.wait_ge(at_ready, u)
                            act.activation(aggt[:, o, :, :], ps_t[:, :, :], ACT.Copy).then_inc(at_copied, 1)
                        if runs(known, 3):
                            if has(known, 3, 1):
                                act.wait_ge(hp_ready, u * 2 - 6)
                                act.wait_ge(o_half, u * 2 - 6)
                            relus(1, u * 2 - 4)
                        if runs(known, 2):
                            act.wait_ge(ot_ready, u - 1)
                            act.activation(others_t[:, :], ps_i[0:E1, 2 * P:3 * P], ACT.Copy).then_inc(hot_ready, 1)
                            act.activation(hot_t[:, :], ps_i[0:E1, 2 * P:3 * P], ACT.Copy, bias=1.0).then_inc(hot_ready, 1)
                        if runs(known, 1):
                            act.wait_ge(var_ready, u)
                            act.activation(sq[:, 1:2], sq[:, 0:1], ACT.Sqrt).then_inc(root_ready, 1)
                        if runs(known, 2):
                            if has(known, 2, 1):
                                act.wait_ge(hp_ready, u * 2 - 5)
                                act.wait_ge(o_half, u * 2 - 5)
                            relus(0, u * 2 - 3)
                    in_steps(act, step)

                @block.tensor
                def _(pe):
                    THREE = ((0, 0), (0, 1), (1, 0))

                    def step(u, k, known):
                        o = 1 - k

                        def products(lo, hi):
                            if not runs(known, 0):
                                if lo == 0:
                                    pe.wait_ge(agg_read, NB * 2 - 2)
                                for _ in range(lo, hi if hi < NB or known < LAST - 1 else lo):
                                    pe.matmul(ps_a[:, 0, 0:P], ident16[:, :], ident16[:, :], start=True, stop=True)
                                return
                            if lo == 0:
                                pe.wait_ge(mask_copied, u + 1)
                                if has(known, 0, 2):
                                    pe.wait_ge(agg_read, u * 2 - 2)
                            pe.ldweights(ident16[:, :], tile_position=(0, 0))
                            for c in range(lo, hi):
                                m = pe.matmul(ps_a[:, k, 0:V2], mask[:, k, c * P:(c + 1) * P].bitcast(F8), parts2[:, c, :],
                                              start=(c == 0), stop=(c == NB - 1))
                            if hi == NB:
                                m.then_inc(agg_ready, 1)

                        def second(half):
                            if half == 0:
                                for b in range(2):
                                    pe.matmul(ps_o[:, 0:D], hot_t[:, :], two["b2"][:, b, :], start=(b == 0), stop=False)
                            pe.wait_ge(hp_ready, u * 2 - 5 + half)
                            for c in range(half * CH, (half + 1) * CH):
                                for a, b in THREE:
                                    m = pe.matmul(ps_o[:, 0:D], hp[:, a, c, :], two["f2"][:, b, c * D:(c + 1) * D],
                                                  start=False, stop=(c + a == KC1))
                            m.then_inc(o_half, 1)

                        q = NB // 8
                        products(0, 2 * q)
                        if runs(known, 2):
                            pe.wait_ge(xn_ready, u - 1)
                            for a in range(2):
                                t = pe.transpose(ps_i[:, a * P:(a + 1) * P], xn[:, k, a, :], ident16[:, :])
                            t.then_inc(xt_ready, 1)
                        products(2 * q, 4 * q)
                        if runs(known, 1):
                            pe.wait_ge(norm_ready, u)
                            for a in range(2):
                                t = pe.transpose(ps_t[:, a, :], agg[:, o, a, :], ident16[:, :])
                            t.then_inc(at_ready, 1)
                        if runs(known, 2):
                            pe.wait_ge(xt_copied, u - 1)
                            for a, b in THREE:
                                m = pe.matmul(ps_w[:, D:D + E1], xnt[:, k, a, :], two["rt"][:, b, :], start=(a + b == 0), stop=(a == 1))
                            m.then_inc(lg_ready, 1)
                        if runs(known, 3):
                            if has(known, 3, 1):
                                pe.wait_ge(o_read, u - 3)
                            second(0)
                        if runs(known, 1):
                            pe.wait_ge(at_copied, u)
                            if runs(known, 2):
                                pe.wait_ge(lg_read, u - 1)
                            for a, b in THREE:
                                m = pe.matmul(ps_w[:, 0:D], aggt[:, o, a, :], two["wt"][:, b, :], start=(a + b == 0), stop=(a == 1))
                            m.then_inc(wx_ready, 1)
                        products(4 * q, 5 * q)
                        if runs(known, 2):
                            pe.wait_ge(others_ready, u - 1)
                            pe.transpose(ps_i[0:E1, 2 * P:3 * P], others[:, :], ident16[:, :]).then_inc(ot_ready, 1)
                        products(5 * q, 7 * q)
                        if runs(known, 2):
                            pe.wait_ge(hot_ready, u * 2 - 2)
                            if has(known, 2, 1):
                                pe.wait_ge(relu_ready, u * 2 - 4)
                            for c in range(KC1):
                                to = ps_f[:, c // CH, c % CH * P:(c % CH + 1) * P]
                                for a, b in THREE:
                                    pe.matmul(to, two["f1"][:, a, c * P:(c + 1) * P], xnt[:, k, b, :], start=(a + b == 0), stop=False)
                                m = pe.matmul(to, never[:, c, :], others_t[:, :], start=False, stop=True)
                                if c % CH == CH - 1:
                                    m.then_inc(f_ready, 1)
                        if runs(known, 3):
                            second(1)
                        products(7 * q, 8 * q)
                    in_steps(pe, step)

                @block.vector
                def _(dve):
                    def step(u, k, known):
                        o = 1 - k
                        if runs(known, 1):
                            dve.wait_ge(agg_ready, u)
                            dve.reciprocal(inv[:, o:o + 1], ps_a[:, o, 2 * D:V2]).then_inc(agg_read, 1)
                            dve.tensor_reduce(total[:, :], ps_a[:, o, 0:2 * D].rearrange("p (t f) -> p f t", t=2), AX.X, ALU.add)\
                               .then_inc(agg_read, 1)
                            dve.wait_ge(agg_read, u * 2)
                            dve.tensor_scalar(agg[:, o, 0, :], total[:, :], inv[:, o:o + 1], None, ALU.mult).then_inc(own["a"], 1)
                            dve.wait_ge(own["a"], u)
                            dve.scalar_tensor_tensor(out=agg[:, o, 1, :], in0=total[:, :], scalar=inv[:, o:o + 1], in1=agg[:, o, 0, :],
                                                     op0=ALU.mult, op1=ALU.subtract).then_inc(norm_ready, 1)

                        def low_part(half):
                            c = slice(half * CH, (half + 1) * CH)
                            dve.wait_ge(high_ready, u * 2 - 5 + half)
                            dve.tensor_tensor(hp[:, 1, c, :], hm[:, c, :], hp[:, 0, c, :], ALU.subtract).then_inc(hp_ready, 1)

                        if runs(known, 3):
                            low_part(0)
                        if runs(known, 2):
                            dve.wait_ge(lg_ready, u - 1)
                            dve.scalar_tensor_tensor(out=lg[:, :], in0=ps_w[:, D:D + E1], scalar=1.0 / (S_X * S_W), in1=rb[:, :],
                                                     op0=ALU.mult, op1=ALU.add).then_inc(lg_read, 1)
                            dve.wait_ge(lg_read, u - 1)
                            dve.tensor_reduce(best1[:, :], lg[:, :], AX.X, ALU.max).then_inc(own["b"], 1)
                            dve.wait_ge(own["b"], u * 3 - 5)
                            dve.scalar_tensor_tensor(out=lg[:, :], in0=lg[:, :], scalar=best1[:, :], in1=falling1[:, :],
                                                     op0=ALU.is_ge, op1=ALU.mult).then_inc(own["b"], 1)
                            dve.wait_ge(own["b"], u * 3 - 4)
                            dve.tensor_reduce(which1[:, :], lg[:, :], AX.X, ALU.max).then_inc(own["b"], 1)
                            dve.wait_ge(own["b"], u * 3 - 3)
                            dve.tensor_scalar(others[:, :], falling1[:, :], which1[:, :], 1.0, ALU.is_equal, ALU.subtract)\
                               .then_inc(others_ready, 1)
                        if runs(known, 1):
                            row = xs[:, ds(u - 1, 1), :].rearrange("p a d -> p (a d)")
                            C = 7

                            def at(n):
                                return u * C - (C - n)
                            dve.wait_ge(wx_ready, u)
                            dve.scalar_tensor_tensor(out=row, in0=ps_w[:, 0:D], scalar=1.0 / (S_X * S_W), in1=row, op0=ALU.mult,
                                                     op1=ALU.add, accum_out=sq[:, 4:5]).then_inc(own["c"], 1)
                            dve.wait_ge(own["c"], at(1))
                            dve.tensor_scalar(sq[:, 5:6], sq[:, 4:5], -1.0 / D, None, ALU.mult).then_inc(own["c"], 1)
                            dve.wait_ge(own["c"], at(2))
                            dve.tensor_scalar(xc[:, :], row, sq[:, 5:6], None, ALU.add).then_inc(own["c"], 1)
                            dve.wait_ge(own["c"], at(3))
                            dve.scalar_tensor_tensor(out=squares[:, :], in0=xc[:, :], scalar=1.0, in1=xc[:, :], op0=ALU.mult,
                                                     op1=ALU.mult, accum_out=sq[:, 4:5]).then_inc(own["c"], 1)
                            dve.wait_ge(own["c"], at(4))
                            dve.tensor_scalar(sq[:, 0:1], sq[:, 4:5], 1.0 / D, EPS, ALU.mult, ALU.add).then_inc(var_ready, 1)
                        if runs(known, 3):
                            low_part(1)
                        if runs(known, 1):
                            dve.wait_ge(root_ready, u)
                            dve.reciprocal(sq[:, 2:3], sq[:, 1:2]).then_inc(own["c"], 1)
                            dve.wait_ge(own["c"], at(5))
                            dve.tensor_scalar(sq[:, 2:3], sq[:, 0:1], sq[:, 2:3], sq[:, 1:2], ALU.mult, ALU.add).then_inc(own["c"], 1)
                            dve.wait_ge(own["c"], at(6))
                            dve.reciprocal(sq[:, 3:4], sq[:, 2:3]).then_inc(own["c"], 1)
                            dve.wait_ge(own["c"], at(7))
                            dve.tensor_scalar(xn[:, o, 0, :], xc[:, :], sq[:, 3:4], 2.0 * S_X, ALU.mult, ALU.mult).then_inc(own_e, 1)
                            dve.tensor_scalar(xc[:, :], xc[:, :], sq[:, 3:4], 2.0 * S_X, ALU.mult, ALU.mult).then_inc(own_e, 1)
                            dve.wait_ge(own_e, u * 2)
                            dve.tensor_tensor(xn[:, o, 1, :], xc[:, :], xn[:, o, 0, :], ALU.subtract).then_inc(xn_ready, 1)
                        if runs(known, 3):
                            dve.wait_ge(o_half, u * 2 - 4)
                            if has(known, 3, 2):
                                dve.wait_ge(stored[o], stored_upto(u, k, known))
                            dve.tensor_scalar(expert_out[:, :], ps_o[:, 0:D], 0.0, 1.0 / (S_W * S_H), ALU.max, ALU.mult).then_inc(o_read, 1)
                            dve.wait_ge(o_read, u - 2)
                            dve.tensor_tensor(fin[:, o, :], expert_out[:, :], xs[:, ds(u - 3, 1), :].rearrange("p a d -> p (a d)"),
                                              ALU.add).then_inc(fin_ready, 1)

                    def stored_upto(u, k, known):
                        if known is not None:
                            return (known - 3) // 2 * 16
                        return (u - k) * 8 + (k - 3) // 2 * 16
                    in_steps(dve, step)
        mean_ctx.close()


def kernel(**inputs):
    import numpy as np
    import concourse.bacc as bacc
    from concourse.bass_utils import run_bass_kernel_spmd

    a = {k: np.asarray(v) for k, v in inputs.items()}
    n = a["x"].shape[0]
    nb = n // 128
    adj = a["adj"].reshape(nb, 128, 4, nb // 4, 128).transpose(0, 2, 4, 3, 1).reshape(4 * nb, 128, nb // 4 * 128)
    e1, d, h1 = a["L1_ffn_W1"].shape
    arrays = {
        "x": a["x"],
        "adj_t": adj,
        "g0_w": a["L0_gnn_W"], "g0_b": a["L0_gnn_b"], "g0_a": a["L0_gnn_a"],
        "gate_w": a["L0_ffn_gate_w"], "gate_b": a["L0_ffn_gate_b"],
        "w1": a["L0_ffn_w1"], "w2": a["L0_ffn_w2"], "w3": a["L0_ffn_w3"],
        "g1_wt": a["L1_gnn_W"].T, "g1_b": a["L1_gnn_b"],
        "router_wt": a["L1_ffn_router_w"].T, "router_b": a["L1_ffn_router_b"],
        "f_w1": a["L1_ffn_W1"].transpose(1, 0, 2).reshape(d, e1 * h1),
        "f_b1": a["L1_ffn_b1"].reshape(-1, 128).T,
        "f_w2": a["L1_ffn_W2"].reshape(-1, 128, d).transpose(1, 0, 2).reshape(128, -1), "f_b2": a["L1_ffn_b2"],
    }
    nc = bacc.Bacc("TRN2", target_bir_lowering=False, num_devices=1)
    sent, args = {}, []
    for name, v in arrays.items():
        v = np.ascontiguousarray(v)
        sent[name] = v
        args.append(nc.dram_tensor(name, v.shape, mybir.dt.from_np(v.dtype), kind="ExternalInput").ap())
    args.append(nc.dram_tensor("out", (n, d), F32, kind="ExternalOutput").ap())
    build(nc, *args)
    r = run_bass_kernel_spmd(nc, [sent], core_ids=[0])
    return r.results[0]["out"]
```
